# Optimizing a Trainium2 kernel written in Bass

```python
import numpy as np
import jax
import jax.numpy as jnp

def _softmax(x, axis=-1):
    return jax.nn.softmax(x, axis=axis)

def _gelu(x):
    return jax.nn.gelu(x, approximate=True)

def _silu(x):
    return jax.nn.silu(x)

def _sigmoid(x):
    return jax.nn.sigmoid(x)

def _layernorm(x, axis=-1, eps=1e-05):
    m = jnp.mean(x, axis=axis, keepdims=True)
    v = jnp.var(x, axis=axis, keepdims=True)
    return (x - m) / jnp.sqrt(v + eps)

def _scatter_add(tgt, idx, src, axis=0):
    return tgt.at[idx].add(src)

def _segment_sum(src, seg, n):
    return jax.ops.segment_sum(src, seg, n)
kernel_name = 'mk_adaln_ffn_d2_seqx_r8_968af3'

def setup_inputs(seed: int=0):
    np.random.seed(seed)
    _w = jnp.asarray

    def _rec_inputs():
        import jax
        import jax.numpy as jnp
        _rk = jax.random.key(seed)
        x = -7.109e-05 + 0.9999 * jax.random.normal(jax.random.fold_in(_rk, 1), (32, 128, 128), jnp.float32)
        _lenS = 128 - jax.random.randint(jax.random.fold_in(_rk, 7), (32,), 0, max(1, 128 // 4) + 1, jnp.int32)
        _lenS2 = 128 - jax.random.randint(jax.random.fold_in(_rk, 8), (32,), 0, max(1, 128 // 4) + 1, jnp.int32)
        cond_512 = 0.0061147 + 1.02565 * jax.random.normal(jax.random.fold_in(_rk, 11), (32, 64), jnp.float32)
        return (x, cond_512)
    x, cond_512 = _rec_inputs()

    def _L0_cond_setup():
        import jax, jax.numpy as jnp
        import numpy as np
        W_DIM = 64
        CLAMP = 256.0
        key = jax.random.key(seed)
        ks = jax.random.split(key, 6)
        B, L, C = (8, 1024, 128)
        return {'x': jax.random.normal(ks[0], (B, L, C), dtype=jnp.float32), 'w': jax.random.normal(ks[1], (B, W_DIM), dtype=jnp.float32), 'weight': jax.random.normal(ks[2], (C, C), dtype=jnp.float32), 'bias': jax.random.normal(ks[3], (C,), dtype=jnp.float32), 'affine_w': jax.random.normal(ks[4], (C, W_DIM), dtype=jnp.float32), 'affine_b': jnp.ones((C,), dtype=jnp.float32)}
    _L0_cond_all = _L0_cond_setup()
    _L0_cond_in = {k: v for k, v in _L0_cond_all.items() if k in ('weight', 'bias', 'affine_w', 'affine_b')}
    del _L0_cond_all

    def _L0_ffn_setup():
        import jax, jax.numpy as jnp
        import numpy as np
        B, T, C = (4, 256, 128)
        E = 8
        K = 2
        H = 176
        HS = 176 * 2
        key = jax.random.key(seed)
        k = jax.random.split(key, 8)
        s = 0.02
        return {'x': jax.random.normal(k[0], (B, T, C), jnp.float32), 'Wg': jax.random.normal(k[1], (C, E), jnp.float32) * s, 'W1': jax.random.normal(k[2], (E, C, H), jnp.float32) * s, 'W2': jax.random.normal(k[3], (E, C, H), jnp.float32) * s, 'W3': jax.random.normal(k[4], (E, H, C), jnp.float32) * s, 'Ws1': jax.random.normal(k[5], (C, HS), jnp.float32) * s, 'Ws2': jax.random.normal(k[6], (C, HS), jnp.float32) * s, 'Ws3': jax.random.normal(k[7], (HS, C), jnp.float32) * s}
    _L0_ffn_all = _L0_ffn_setup()
    _L0_ffn_in = {k: v for k, v in _L0_ffn_all.items() if k in ('Wg', 'W1', 'W2', 'W3', 'Ws1', 'Ws2', 'Ws3')}
    del _L0_ffn_all

    def _L1_cond_setup():
        import jax, jax.numpy as jnp
        import numpy as np
        B, S, D, H, C = (8, 512, 128, 32, 64)
        INIT_RANGE = 0.01
        key = jax.random.key(seed)
        ks = jax.random.split(key, 6)
        return {'hidden_states': jax.random.normal(ks[0], (B, S, D), dtype=jnp.float32), 'conditions': jax.random.normal(ks[1], (B, C), dtype=jnp.float32), 'down_project': jax.random.normal(ks[2], (D, H), dtype=jnp.float32) * INIT_RANGE, 'down_gamma': jax.random.normal(ks[3], (C, H), dtype=jnp.float32), 'down_beta': jnp.zeros((C, H), dtype=jnp.float32), 'up_project': jax.random.normal(ks[4], (H, D), dtype=jnp.float32) * INIT_RANGE, 'up_gamma': jax.random.normal(ks[5], (C, D), dtype=jnp.float32), 'up_beta': jnp.zeros((C, D), dtype=jnp.float32)}
    _L1_cond_all = _L1_cond_setup()
    _L1_cond_in = {k: v for k, v in _L1_cond_all.items() if k in ('down_project', 'down_gamma', 'down_beta', 'up_project', 'up_gamma', 'up_beta')}
    del _L1_cond_all

    def _L1_ffn_setup():
        import jax, jax.numpy as jnp
        import numpy as np
        D = 128
        H = 16
        DK = D // H
        E = 8
        DFF = 4 * D
        TOPK = 2
        EPS = 1e-05

        def _layernorm(x, g, b):
            m = jnp.mean(x, axis=-1, keepdims=True)
            v = jnp.mean(jnp.square(x - m), axis=-1, keepdims=True)
            return (x - m) * jax.lax.rsqrt(v + EPS) * g + b
        key = jax.random.key(seed)
        ks = jax.random.split(key, 16)
        s_in = 1.0 / np.sqrt(D)
        s_ff = 1.0 / np.sqrt(DFF)
        return {'x': jax.random.normal(ks[0], (2, 256, D), dtype=jnp.float32), 'ln1_g': jnp.ones((D,), jnp.float32), 'ln1_b': jnp.zeros((D,), jnp.float32), 'w_qkv': jax.random.normal(ks[1], (D, 3 * D), jnp.float32) * s_in, 'b_qkv': jnp.zeros((3 * D,), jnp.float32), 'w_o': jax.random.normal(ks[2], (D, D), jnp.float32) * s_in, 'b_o': jnp.zeros((D,), jnp.float32), 'ln2_g': jnp.ones((D,), jnp.float32), 'ln2_b': jnp.zeros((D,), jnp.float32), 'gate_w': jax.random.normal(ks[3], (D, E), jnp.float32) * s_in, 'gate_b': jnp.zeros((E,), jnp.float32), 'W1': jax.random.normal(ks[4], (E, D, DFF), jnp.float32) * s_in, 'b1': jnp.zeros((E, DFF), jnp.float32), 'W2': jax.random.normal(ks[5], (E, DFF, D), jnp.float32) * s_ff, 'b2': jnp.zeros((E, D), jnp.float32)}
    _L1_ffn_all = _L1_ffn_setup()
    _L1_ffn_in = {k: v for k, v in _L1_ffn_all.items() if k in ('ln1_g', 'ln1_b', 'w_qkv', 'b_qkv', 'w_o', 'b_o', 'ln2_g', 'ln2_b', 'gate_w', 'gate_b', 'W1', 'b1', 'W2', 'b2')}
    del _L1_ffn_all
    return {'x': x, 'cond_512': cond_512, 'L0_cond_weight': _L0_cond_in['weight'], 'L0_cond_bias': _L0_cond_in['bias'], 'L0_cond_affine_w': _L0_cond_in['affine_w'], 'L0_cond_affine_b': _L0_cond_in['affine_b'], 'L0_ffn_Wg': _L0_ffn_in['Wg'], 'L0_ffn_W1': _L0_ffn_in['W1'], 'L0_ffn_W2': _L0_ffn_in['W2'], 'L0_ffn_W3': _L0_ffn_in['W3'], 'L0_ffn_Ws1': _L0_ffn_in['Ws1'], 'L0_ffn_Ws2': _L0_ffn_in['Ws2'], 'L0_ffn_Ws3': _L0_ffn_in['Ws3'], 'L1_cond_down_project': _L1_cond_in['down_project'], 'L1_cond_down_gamma': _L1_cond_in['down_gamma'], 'L1_cond_down_beta': _L1_cond_in['down_beta'], 'L1_cond_up_project': _L1_cond_in['up_project'], 'L1_cond_up_gamma': _L1_cond_in['up_gamma'], 'L1_cond_up_beta': _L1_cond_in['up_beta'], 'L1_ffn_ln1_g': _L1_ffn_in['ln1_g'], 'L1_ffn_ln1_b': _L1_ffn_in['ln1_b'], 'L1_ffn_w_qkv': _L1_ffn_in['w_qkv'], 'L1_ffn_b_qkv': _L1_ffn_in['b_qkv'], 'L1_ffn_w_o': _L1_ffn_in['w_o'], 'L1_ffn_b_o': _L1_ffn_in['b_o'], 'L1_ffn_ln2_g': _L1_ffn_in['ln2_g'], 'L1_ffn_ln2_b': _L1_ffn_in['ln2_b'], 'L1_ffn_gate_w': _L1_ffn_in['gate_w'], 'L1_ffn_gate_b': _L1_ffn_in['gate_b'], 'L1_ffn_W1': _L1_ffn_in['W1'], 'L1_ffn_b1': _L1_ffn_in['b1'], 'L1_ffn_W2': _L1_ffn_in['W2'], 'L1_ffn_b2': _L1_ffn_in['b2']}

def reference(x, cond_512, L0_cond_weight, L0_cond_bias, L0_cond_affine_w, L0_cond_affine_b, L0_ffn_Wg, L0_ffn_W1, L0_ffn_W2, L0_ffn_W3, L0_ffn_Ws1, L0_ffn_Ws2, L0_ffn_Ws3, L1_cond_down_project, L1_cond_down_gamma, L1_cond_down_beta, L1_cond_up_project, L1_cond_up_gamma, L1_cond_up_beta, L1_ffn_ln1_g, L1_ffn_ln1_b, L1_ffn_w_qkv, L1_ffn_b_qkv, L1_ffn_w_o, L1_ffn_b_o, L1_ffn_ln2_g, L1_ffn_ln2_b, L1_ffn_gate_w, L1_ffn_gate_b, L1_ffn_W1, L1_ffn_b1, L1_ffn_W2, L1_ffn_b2):
    import jax
    import jax.numpy as jnp

    def _L0_cond_ref(x, w, weight, bias, affine_w, affine_b):
        import jax, jax.numpy as jnp
        import numpy as np
        W_DIM = 64
        CLAMP = 256.0
        B, L, C = x.shape
        gain = 1.0 / np.sqrt(W_DIM).astype(np.float32)
        styles = w @ (affine_w * gain).T + affine_b
        ws = weight[None, :, :] * styles[:, None, :]
        dcoefs = jax.lax.rsqrt(jnp.sum(ws * ws, axis=2) + 1e-08)
        xm = x * styles[:, None, :]
        y = jnp.einsum('blc,oc->blo', xm, weight)
        y = y * dcoefs[:, None, :]
        y = jnp.clip(y + bias, -CLAMP, CLAMP)
        return y

    def _L0_ffn_ref(x, Wg, W1, W2, W3, Ws1, Ws2, Ws3):
        import jax, jax.numpy as jnp
        import numpy as np
        B, T, C = (4, 256, 128)
        E = 8
        K = 2
        H = 176
        HS = 176 * 2
        b, t, c = x.shape
        xf = x.reshape(-1, c)
        n = xf.shape[0]
        router = xf @ Wg
        top_logits, idx = jax.lax.top_k(router, K)
        probs = jax.nn.softmax(top_logits.astype(jnp.float32), axis=-1).astype(x.dtype)
        w = jnp.zeros((n, E), x.dtype).at[jnp.arange(n)[:, None], idx].add(probs)
        h = jax.nn.silu(jnp.einsum('tc,ech->eth', xf, W1)) * jnp.einsum('tc,ech->eth', xf, W2)
        y = jnp.einsum('eth,ehc,te->tc', h, W3, w)
        y = y.reshape(b, t, c)
        hs = jax.nn.silu(xf @ Ws1) * (xf @ Ws2)
        y = y + (hs @ Ws3).reshape(b, t, c)
        return y

    def _L1_cond_ref(hidden_states, conditions, down_project, down_gamma, down_beta, up_project, up_gamma, up_beta):
        import jax, jax.numpy as jnp
        import numpy as np
        B, S, D, H, C = (8, 512, 128, 32, 64)
        INIT_RANGE = 0.01
        dg = conditions @ down_gamma
        db = conditions @ down_beta
        ug = conditions @ up_gamma
        ub = conditions @ up_beta
        w_down = down_project[None, :, :] * dg[:, None, :] + db[:, None, :]
        down = jnp.einsum('bsd,bdh->bsh', hidden_states, w_down)
        act = jax.nn.relu(down)
        w_up = up_project[None, :, :] * ug[:, None, :] + ub[:, None, :]
        up = jnp.einsum('bsh,bhd->bsd', act, w_up)
        return up + hidden_states

    def _L1_ffn_ref(x, ln1_g, ln1_b, w_qkv, b_qkv, w_o, b_o, ln2_g, ln2_b, gate_w, gate_b, W1, b1, W2, b2):
        import jax, jax.numpy as jnp
        import numpy as np
        D = 128
        H = 16
        DK = D // H
        E = 8
        DFF = 4 * D
        TOPK = 2
        EPS = 1e-05

        def _layernorm(x, g, b):
            m = jnp.mean(x, axis=-1, keepdims=True)
            v = jnp.mean(jnp.square(x - m), axis=-1, keepdims=True)
            return (x - m) * jax.lax.rsqrt(v + EPS) * g + b
        B, S, _ = x.shape
        h = _layernorm(x, ln1_g, ln1_b)
        qkv = h @ w_qkv + b_qkv
        q, k, v = jnp.split(qkv, 3, axis=-1)
        q = q.reshape(B, S, H, DK)
        k = k.reshape(B, S, H, DK)
        v = v.reshape(B, S, H, DK)
        scores = jnp.einsum('bqhd,bkhd->bhqk', q, k) / np.sqrt(DK)
        attn = jax.nn.softmax(scores, axis=-1)
        o = jnp.einsum('bhqk,bkhd->bqhd', attn, v).reshape(B, S, D)
        x = x + o @ w_o + b_o
        h = _layernorm(x, ln2_g, ln2_b).reshape(B * S, D)
        logits = h @ gate_w + gate_b
        topv, topi = jax.lax.top_k(logits, TOPK)
        gw = jax.nn.softmax(topv, axis=-1)
        ew = jnp.sum(jax.nn.one_hot(topi, E, dtype=h.dtype) * gw[..., None], axis=1)
        hid = jax.nn.relu(jnp.einsum('td,edf->etf', h, W1) + b1[:, None, :])
        out_e = jnp.einsum('etf,efd->etd', hid, W2) + b2[:, None, :]
        moe = jnp.einsum('etd,te->td', out_e, ew)
        return x + moe.reshape(B, S, D)
    x = x + _L0_ffn_ref(_L0_cond_ref(x, cond_512, L0_cond_weight, L0_cond_bias, L0_cond_affine_w, L0_cond_affine_b), L0_ffn_Wg, L0_ffn_W1, L0_ffn_W2, L0_ffn_W3, L0_ffn_Ws1, L0_ffn_Ws2, L0_ffn_Ws3)
    x = x + _L1_ffn_ref(_L1_cond_ref(x, cond_512, L1_cond_down_project, L1_cond_down_gamma, L1_cond_down_beta, L1_cond_up_project, L1_cond_up_gamma, L1_cond_up_beta), L1_ffn_ln1_g, L1_ffn_ln1_b, L1_ffn_w_qkv, L1_ffn_b_qkv, L1_ffn_w_o, L1_ffn_b_o, L1_ffn_ln2_g, L1_ffn_ln2_b, L1_ffn_gate_w, L1_ffn_gate_b, L1_ffn_W1, L1_ffn_b1, L1_ffn_W2, L1_ffn_b2)
    return x

_drawn_inputs = setup_inputs


def setup_inputs(seed=0):
    import zlib

    import numpy as np

    out = dict(_drawn_inputs(seed))
    spreads = {'L0_cond_affine_b': (1.0, 0.6),
     'L1_cond_down_beta': (0.0, 0.1),
     'L1_cond_up_beta': (0.0, 0.1),
     'L1_ffn_ln1_g': (1.0, 0.6),
     'L1_ffn_ln1_b': (0.0, 2.0),
     'L1_ffn_b_qkv': (0.0, 2.0),
     'L1_ffn_b_o': (0.0, 2.0),
     'L1_ffn_ln2_g': (1.0, 0.6),
     'L1_ffn_ln2_b': (0.0, 0.8),
     'L1_ffn_gate_b': (0.0, 2.0),
     'L1_ffn_b1': (0.0, 2.0),
     'L1_ffn_b2': (0.0, 2.0)}
    factors = {'L0_cond_weight': 3.046,
     'L0_cond_bias': 2.856,
     'L0_cond_affine_w': 3.955,
     'L0_ffn_Wg': 6.91,
     'L0_ffn_W1': 6.622,
     'L0_ffn_W2': 6.101,
     'L0_ffn_W3': 5.968,
     'L0_ffn_Ws2': 3.863,
     'L0_ffn_Ws3': 3.015,
     'L1_ffn_w_qkv': 5.408,
     'L1_ffn_w_o': 5.444,
     'L1_ffn_gate_w': 8.0,
     'L1_ffn_W1': 8.0,
     'L1_ffn_W2': 8.0}
    for name, (base, spread) in spreads.items():
        noise = np.random.default_rng([zlib.crc32(name.encode()), seed]).standard_normal(out[name].shape)
        drawn = base * np.exp(spread * noise) if base else spread * noise
        out[name] = jnp.asarray(drawn.astype(out[name].dtype))
    for name, factor in factors.items():
        out[name] = (out[name] * factor).astype(out[name].dtype)
    return out
```

```python
from contextlib import ExitStack

import numpy as np

import concourse.bass as bass
from concourse import mybir

F32 = mybir.dt.float32
F32R = mybir.dt.float32r
BF16 = mybir.dt.bfloat16
U32 = mybir.dt.uint32
I32 = mybir.dt.int32
ALU = mybir.AluOpType
ACT = mybir.ActivationFunctionType
AX_X = mybir.AxisListType.X

P = 128
SEQS = 32
TOK = SEQS * P
GT = 4
GROUPS = SEQS // GT
GW = GT * P
E = 8
TOPK = 2
COND = 64
SLOTS = 256
REGION = TOK + SLOTS
ETILES = TOK * TOPK // SLOTS + E
MAXT = TOK // SLOTS
HALF = 88
HS = 352
DOWN = 32
HEADS = 16
HG = 4
KT1 = 4
CLAMP = 256.0
EPS = 1e-5
ATT_SCALE = float(1.0 / np.sqrt(8.0))

C_ID = 0
C_TRI = C_ID + P
C_ONESB = C_TRI + P
C_SEL = C_ONESB + P
C_MASK = C_SEL + 4
C_EXP = C_MASK + 4
C_REG = C_EXP + E
C_TILE = C_REG + E
C_STEP = C_TILE + ETILES
C_END = C_STEP + MAXT

V_BIAS, V_AFFB, V_LN1G, V_LN1B, V_LN2G, V_LN2B, V_BQ, V_BK = range(8)
R_BV, R_BO, R_GB = 0, P, 2 * P
R_END = 2 * P + E


def constants():
    c = np.zeros((P, C_END), np.float32)
    p = np.arange(P)
    c[:, C_ID:C_ID + P] = np.eye(P)
    c[:, C_TRI:C_TRI + P] = p[:, None] < p[None, :]
    col = np.arange(32)
    for j in range(4):
        c[:, C_ONESB + 32 * j:C_ONESB + 32 * j + 32] = (col // 8 == j)[None, :]
        c[:, C_SEL + j] = (p // 32 == j) & (p % 32 < 8)
        c[:, C_MASK + j] = (p % 32) // 8 == j
    c[:, C_EXP:C_EXP + E] = np.arange(E)
    c[:, C_REG:C_REG + E] = np.arange(E) * REGION
    c[:, C_TILE:C_TILE + ETILES] = np.arange(ETILES)
    c[:, C_STEP:C_STEP + MAXT] = np.arange(MAXT) * SLOTS
    return c


def rounds(engine, total, unroll, head=0, tail=0):
    for n in range(head):
        yield n, n % unroll, n // unroll
    with engine.Fori(0, (total - head - tail) // unroll) as i:
        for u in range(unroll):
            yield i * unroll + (head + u), u, i + head // unroll
    for n in range(total - tail, total):
        yield n, n % unroll, n // unroll


def first(n):
    return isinstance(n, int) and n == 0


def is_last(n, total):
    return isinstance(n, int) and n == total - 1


def wait(engine, sem, value):
    if not (isinstance(value, int) and value <= 0):
        engine.wait_ge(sem, value)


def hold(m, engine, sem, value):
    wait(engine, sem, value)
    if not isinstance(value, int):
        engine.sem_inc(m.passed, 1)


class Chain:

    def __init__(self, m, engine, sem, per=0):
        self.m = m
        self.engine, self.sem, self.per, self.base, self.count = engine, sem, per, 0, 0

    def begin(self, n):
        self.base, self.count = n * self.per, 0

    def __call__(self, instruction):
        self.count += 1
        instruction.then_inc(self.sem, 1)
        hold(self.m, self.engine, self.sem, self.base + self.count)


def bc(ap, *shape):
    return ap.to_broadcast(list(shape))


class Machine:

    def __init__(self, nc, ctx):
        self.nc, self.ctx = nc, ctx

    def sb(self, name, shape, dt=F32, ctx=None):
        return (ctx or self.ctx).enter_context(self.nc.sbuf_tensor(name, shape, dt))

    def ps(self, name, shape, ctx, dt=F32):
        return ctx.enter_context(self.nc.psum_tensor(name, shape, dt))

    def sem(self, name):
        return self.ctx.enter_context(self.nc.semaphore(name))

    def sems(self, *names):
        return [self.sem(n) for n in names]


def allocate(m, d):
    nc = m.nc
    m.passed = m.sem("passed")
    m.X = m.sb("X", [P, SEQS, P])
    m.X3 = m.sb("X3", [P, SEQS, P])
    m.V = m.sb("V", [P, SEQS, P])
    m.const = m.sb("const", [P, C_END])
    m.vec = m.sb("vec", [P, 8])
    m.rows = m.sb("rows", [P, R_END])
    m.tri = m.sb("tri", [P, P], BF16)
    m.ones = m.sb("ones", [P, P], BF16)
    m.ident = m.const[:, C_ID:C_ID + P]
    m.pos = m.sb("pos", [P, SEQS, TOPK])
    m.hot = m.sb("hot", [P, SEQS, TOPK, E])
    m.diff = m.sb("diff", [P, SEQS])
    m.pw = m.sb("pw", [P, SEQS, TOPK])
    m.gidx = m.sb("gidx", [P, SEQS * TOPK], U32)
    m.base = m.sb("base", [P, E])
    m.table = m.sb("table", [P, 2 * ETILES + E], I32)
    m.zero = m.sb("zero", [P, 2, P])
    m.styles = m.sb("styles", [P, SEQS])
    m.dcoef = m.sb("dcoef", [P, SEQS])
    m.gbD = m.sb("gbD", [P, SEQS, 2 * DOWN])
    m.xbuf = nc.dram_tensor("dispatch_rows", ((E + 1) * REGION, P), F32, kind="Internal").ap()
    m.ybuf = nc.dram_tensor("expert_rows", (ETILES * SLOTS, P), F32, kind="Internal").ap()
    m.gb_dram = nc.dram_tensor("cond_rows", (SEQS, 2 * DOWN + 2 * P), F32, kind="Internal").ap()
    m.qk_dram = nc.dram_tensor("qk_parts", (4, P, TOK), F32, kind="Internal").ap()



def setup(m, d):
    nc = m.nc
    with ExitStack() as ctx:
        condT = m.sb("condT", [COND, SEQS], ctx=ctx)
        affT = m.sb("affT", [COND, P], ctx=ctx)
        WT = m.sb("WT_sq_in", [P, P], ctx=ctx)
        gb = m.sb("gb", [COND, 2 * DOWN + 2 * P], ctx=ctx)
        sq = m.sb("sq", [P, P], ctx=ctx)
        ssq = m.sb("ssq", [P, SEQS], ctx=ctx)
        dsum = m.sb("dsum", [P, SEQS], ctx=ctx)
        half = m.sb("half", [P, SEQS], ctx=ctx)
        gbrow = m.sb("gbrow", [SEQS, 2 * DOWN + 2 * P], ctx=ctx)
        ps = m.ps("ps_setup", [P, 3, 512], ctx)
        (loaded, consts, styled, squared, pe_st, pe_dc, pe_gb, gb_copied, summed, dc_done, made,
         gb_out, gb_in) = m.sems("loaded", "consts", "styled", "squared", "pe_st", "pe_dc", "pe_gb",
                                 "gb_copied", "summed", "dc_done", "made", "gb_out", "gb_in")
        with nc.Block() as block:
            @block.sync
            def _(sp):
                small = [(condT[:], d["condT"]), (affT[:], d["affT"]), (WT[:], d["WT"]), (gb[:], d["gb"]),
                         (m.vec[:], d["vec"]), (m.const[:], d["const"]),
                         (m.rows[:], d["rows"].to_broadcast([P, R_END]))]
                for dst, src in small:
                    sp.dma_start(dst, src).then_inc(loaded, 16)
                sp.wait_ge(gb_copied, 1)
                sp.dma_start(m.gb_dram, gbrow[:]).then_inc(gb_out, 16)
                sp.wait_ge(gb_out, 16)
                sp.dma_start(m.gbD[:], m.gb_dram[:, 0:2 * DOWN].unsqueeze(0).to_broadcast(
                    [P, SEQS, 2 * DOWN])).then_inc(gb_in, 16)
                sp.wait_ge(gb_in, 16)

            @block.gpsimd
            def _(pool):
                nc.gpsimd.memset(half[:], -0.5).then_inc(made, 1)
                nc.gpsimd.memset(m.zero[:], 0.0)
                nc.gpsimd.memset(m.ones[:], 1.0)
                pool.wait_ge(summed, 1)
                pool.wait_ge(made, 1)
                nc.gpsimd.tensor_tensor(m.dcoef[:], dsum[:], half[:], ALU.pow).then_inc(dc_done, 1)
                pool.wait_ge(dc_done, 1)

            @block.tensor
            def _(pe):
                pe.wait_ge(loaded, 16 * 7)
                nc.tensor.matmul(ps[:, 0, 0:SEQS], affT[:], condT[:], start=True, stop=True).then_inc(pe_st, 1)
                nc.tensor.matmul(ps[0:SEQS, 1, 0:2 * DOWN + 2 * P], condT[:], gb[:], start=True,
                                 stop=True).then_inc(pe_gb, 1)
                pe.wait_ge(squared, 2)
                nc.tensor.matmul(ps[:, 2, 0:SEQS], sq[:], ssq[:], start=True, stop=True).then_inc(pe_dc, 1)

            @block.vector
            def _(dve):
                dve.wait_ge(loaded, 16 * 7)
                nc.vector.tensor_tensor(sq[:], WT[:], WT[:], ALU.mult).then_inc(squared, 1)
                nc.vector.tensor_copy(m.tri[:], m.const[:, C_TRI:C_TRI + P])
                nc.vector.tensor_copy(m.base[:], m.const[:, C_REG:C_REG + E])
                dve.wait_ge(pe_st, 1)
                nc.vector.tensor_scalar(m.styles[:], ps[:, 0, 0:SEQS], float(1 / np.sqrt(COND)),
                                        m.vec[:, V_AFFB:V_AFFB + 1], ALU.mult, ALU.add).then_inc(styled, 1)
                dve.wait_ge(styled, 1)
                nc.vector.tensor_tensor(ssq[:], m.styles[:], m.styles[:], ALU.mult).then_inc(squared, 1)
                dve.wait_ge(pe_gb, 1)
                nc.vector.tensor_copy(gbrow[:], ps[0:SEQS, 1, 0:2 * DOWN + 2 * P]).then_inc(gb_copied, 1)
                dve.wait_ge(pe_dc, 1)
                nc.vector.tensor_scalar(dsum[:], ps[:, 2, 0:SEQS], 1e-8, None, ALU.add).then_inc(summed, 1)



ROUTE_LINKS = 6


class Router:

    def __init__(self, m, ctx, tag, bias):
        self.m, self.bias = m, bias
        self.logits = [m.sb(f"logits{tag}{b}", [P, GT, E], ctx=ctx) for b in range(2)]
        self.best = [m.sb(f"best{tag}{b}", [P, GT, 8], ctx=ctx) for b in range(2)]
        self.choice = [m.sb(f"choice{tag}{b}", [P, GT, 8], U32, ctx=ctx) for b in range(2)]
        self.mask = [m.sb(f"mask{tag}{b}", [P, GT, E], BF16, ctx=ctx) for b in range(2)]
        self.slot = [m.sb(f"slot{tag}{b}", [P, GT, E], ctx=ctx) for b in range(2)]
        self.prod = [m.sb(f"prod{tag}{b}", [P, GT, TOPK, E], ctx=ctx) for b in range(2)]
        self.index = [m.sb(f"index{tag}{b}", [P, GT * TOPK], U32, ctx=ctx) for b in range(2)]
        self.row = [m.sb(f"row{tag}{b}", [P, GT, P], ctx=ctx) for b in range(2)]
        (self.link, self.got, self.masked, self.ranked,
         self.indexed) = m.sems(*(f"{s}{tag}" for s in ("rt_link", "rt_got", "rt_masked", "rt_ranked", "rt_indexed")))
        self.scattered = m.sems(f"rt_scattered{tag}_0", f"rt_scattered{tag}_1")
        self.sends = 16 * GT * TOPK


def route_choose(r, dve, chain, n, b, nat, nat_ready):
    m, nc = r.m, r.m.nc
    tiles = bass.ds(n * GT, GT)
    chain.begin(n)
    dve.wait_ge(nat_ready, n + 1)
    lg = r.logits[b][:].rearrange("p (a c) e -> p a c e", a=2)
    src = nat[:, :, 0:2 * (P + E)].rearrange("p a (c w) -> p a c w", c=2)[:, :, :, P:P + E]
    if r.bias is None:
        ins = nc.vector.tensor_copy(lg, src)
    else:
        ins = nc.vector.tensor_tensor(lg, src, bc(r.bias.unsqueeze(1).unsqueeze(1), P, 2, 2, E), ALU.add)
    ins.then_inc(r.got, 1)
    hold(m, dve, r.got, n + 1)
    for t in range(GT):
        ins = nc.vector.max(r.best[b][:, t, :], r.logits[b][:, t, :])
    chain(ins)
    for t in range(GT):
        ins = nc.vector.max_index(r.choice[b][:, t, :], r.best[b][:, t, :], r.logits[b][:, t, :])
    chain(ins)
    nc.vector.tensor_tensor(m.diff[:, tiles], r.best[b][:, :, 1], r.best[b][:, :, 0], ALU.subtract)
    hot = m.hot[:, tiles, :, :]
    chain(nc.vector.tensor_tensor(
        hot, bc(r.choice[b][:, :, 0:TOPK].unsqueeze(3), P, GT, TOPK, E),
        bc(m.const[:, C_EXP:C_EXP + E].unsqueeze(1).unsqueeze(1), P, GT, TOPK, E), ALU.is_equal))
    nc.vector.tensor_tensor(r.mask[b][:], m.hot[:, tiles, 0, :], m.hot[:, tiles, 1, :], ALU.add
                            ).then_inc(r.masked, 1)


def route_rank(r, pe, n, b, rank):
    m, nc = r.m, r.m.nc
    pe.wait_ge(r.masked, n + 1)
    wait(pe, r.indexed, n)
    for t in range(GT + 1):
        out = rank[:, t * E:(t + 1) * E]
        for u in range(min(t + 1, GT)):
            ins = nc.tensor.matmul(out, m.tri[:] if u == t else m.ones[:], r.mask[b][:, u, :],
                                   start=(u == 0), stop=(u == min(t, GT - 1)), skip_group_check=True)
    ins.then_inc(r.ranked, 1)


def route_index(r, dve, chain, n, b, i, rank):
    m, nc = r.m, r.m.nc
    tiles = bass.ds(n * GT, GT)
    dve.wait_ge(r.ranked, n + 1)
    chain(nc.vector.tensor_tensor(r.slot[b][:], rank[:, 0:GT * E].rearrange("p (t e) -> p t e", t=GT),
                                  bc(m.base[:].unsqueeze(1), P, GT, E), ALU.add))
    nc.vector.tensor_tensor(m.base[:], m.base[:], rank[:, GT * E:(GT + 1) * E], ALU.add)
    chain(nc.vector.tensor_tensor(r.prod[b][:], m.hot[:, tiles, :, :],
                                  bc(r.slot[b][:].unsqueeze(2), P, GT, TOPK, E), ALU.mult))
    chain(nc.vector.tensor_reduce(m.pos[:, tiles, :], r.prod[b][:], AX_X, ALU.add))
    hold(m, dve, r.scattered[b], r.sends * i)
    nc.vector.tensor_copy(r.index[b][:].rearrange("p (t k) -> p t k", t=GT), m.pos[:, tiles, :]
                          ).then_inc(r.indexed, 1)


def route_scatter(r, pool, n, b, rows_ready):
    m = r.m
    pool.wait_ge(r.indexed, n + 1)
    hold(m, pool, rows_ready, n + 1)
    for t in range(GT):
        for k in range(TOPK):
            c = t * TOPK + k
            pool.indirect_dma_start(
                out=m.xbuf, out_offset=bass.IndirectOffsetOnAxis(ap=r.index[b][:, c:c + 1], axis=0),
                in_=r.row[b][:, t, :], in_offset=None).then_inc(r.scattered[b], 16)


def tile_table(m, tag):
    nc = m.nc
    with ExitStack() as ctx:
        sb = lambda name, shape: m.sb(name + tag, shape, ctx=ctx)
        cnt = sb("cnt", [P, E])
        over = sb("over", [P, E, MAXT])
        need = sb("need", [P, E])
        one = sb("one", [P, E])
        incl = sb("incl", [P, E])
        excl = sb("excl", [P, E])
        delta = sb("delta", [P, E])
        cmp = sb("cmp", [P, ETILES, E])
        expert = sb("expert", [P, ETILES])
        is_e = sb("is_e", [P, ETILES, E])
        val = sb("val", [P, ETILES, E])
        row = sb("row_of", [P, ETILES])
        spare = sb("spare", [P, ETILES])
        prod = sb("prod_g", [P, SEQS * TOPK, E])
        shift = sb("shift", [P, SEQS * TOPK])
        total = sb("total", [P, SEQS])
        ex = sb("ex", [P, SEQS])
        link, tabled, exped, tails = m.sems(*(s + tag for s in ("tt_link", "tabled", "exped", "tails")))
        exps = m.const[:, C_EXP:C_EXP + E]
        regs = m.const[:, C_REG:C_REG + E]
        tl = m.const[:, C_TILE:C_TILE + ETILES]
        steps = m.const[:, C_STEP:C_STEP + MAXT]
        with nc.Block() as block:
            @block.scalar
            def _(act):
                nc.scalar.activation(ex[:], m.diff[:], ACT.Exp).then_inc(exped, 1)

            @block.sync
            def _(sp):
                sp.wait_ge(tabled, 1)
                for e in range(E):
                    at = sp.value_load(m.table[0:1, 2 * ETILES + e:2 * ETILES + e + 1],
                                       min_val=e * REGION, max_val=e * REGION + TOK)
                    sp.dma_start(m.xbuf[bass.ds(at, SLOTS), :].rearrange("(a p) c -> p a c", p=P),
                                 m.zero[:]).then_inc(tails, 16)
                sp.dma_start(m.xbuf[E * REGION:E * REGION + SLOTS, :].rearrange("(a p) c -> p a c", p=P),
                             m.zero[:]).then_inc(tails, 16)
                sp.wait_ge(tails, 16 * (E + 1))

            @block.vector
            def _(dve):
                v = nc.vector
                c = Chain(m, dve, link)
                v.memset(one[:], 1.0)
                c(v.tensor_tensor(cnt[:], m.base[:], regs, ALU.subtract))
                c(v.tensor_tensor(over[:], bc(cnt[:].unsqueeze(2), P, E, MAXT),
                                  bc(steps.unsqueeze(1), P, E, MAXT), ALU.is_gt))
                c(v.tensor_reduce(need[:], over[:], AX_X, ALU.add))
                c(v.tensor_tensor_scan(incl[:], one[:], need[:], 0.0, ALU.mult, ALU.add))
                c(v.tensor_tensor(excl[:], incl[:], need[:], ALU.subtract))
                c(v.scalar_tensor_tensor(out=delta[:], in0=excl[:], scalar=float(SLOTS), in1=regs,
                                         op0=ALU.mult, op1=ALU.subtract))
                c(v.tensor_tensor(cmp[:], bc(incl[:].unsqueeze(1), P, ETILES, E),
                                  bc(tl.unsqueeze(2), P, ETILES, E), ALU.is_le))
                c(v.tensor_reduce(expert[:], cmp[:], AX_X, ALU.add))
                c(v.tensor_tensor(is_e[:], bc(expert[:].unsqueeze(2), P, ETILES, E),
                                  bc(exps.unsqueeze(1), P, ETILES, E), ALU.is_equal))
                c(v.scalar_tensor_tensor(out=val[:], in0=bc(tl.unsqueeze(2), P, ETILES, E), scalar=float(SLOTS),
                                         in1=bc(delta[:].unsqueeze(1), P, ETILES, E),
                                         op0=ALU.mult, op1=ALU.subtract))
                c(v.tensor_tensor(val[:], val[:], is_e[:], ALU.mult))
                c(v.tensor_reduce(row[:], val[:], AX_X, ALU.add))
                c(v.tensor_scalar(spare[:], expert[:], float(E) - 0.5, float(E * REGION), ALU.is_gt, ALU.mult))
                v.tensor_scalar(m.table[:, 0:ETILES], expert[:], float(E - 1), None, ALU.min)
                v.tensor_tensor(m.table[:, ETILES:2 * ETILES], row[:], spare[:], ALU.add)
                v.tensor_copy(m.table[:, 2 * ETILES:], m.base[:]).then_inc(tabled, 1)
                c(v.tensor_tensor(prod[:], m.hot[:].rearrange("p s k e -> p (s k) e"),
                                  bc(delta[:].unsqueeze(1), P, SEQS * TOPK, E), ALU.mult))
                c(v.tensor_reduce(shift[:], prod[:], AX_X, ALU.add))
                v.tensor_tensor(m.gidx[:], shift[:], m.pos[:].rearrange("p s k -> p (s k)"), ALU.add)
                dve.wait_ge(exped, 1)
                c(v.tensor_scalar(total[:], ex[:], 1.0, None, ALU.add))
                c(v.reciprocal(m.pw[:, :, 0], total[:]))
                v.tensor_tensor(m.pw[:, :, 1], m.pw[:, :, 0], ex[:], ALU.mult)
                dve.wait_ge(tabled, 1)
                c(v.tensor_copy(m.base[:], regs))



def layer0(m, d):
    nc = m.nc
    MS = [P, P, HS - 2 * P]
    with ExitStack() as ctx:
        sb = lambda n, s, dt=F32: m.sb(n, s, dt, ctx)
        xT = sb("xT", [P, TOK])
        WT = sb("WT", [P, P])
        IG = sb("IG0", [P, P + E])
        Ws1, Ws2 = sb("Ws1", [P, HS]), sb("Ws2", [P, HS])
        Ws3 = sb("Ws3", [P, 3, P])
        xm = [sb(f"xm{b}", [P, GT, P]) for b in range(2)]
        y = [sb(f"y{b}", [P, GW]) for b in range(2)]
        xf = [sb(f"xf{b}", [P, GW]) for b in range(2)]
        s = [sb(f"s{q}", [P, GW]) for q in range(2)]
        h = [[sb(f"h{b}{k}", [P, GW]) for k in range(3)] for b in range(2)]
        psY = m.ps("psY", [P, 512], ctx)
        psN = m.ps("psN", [P, 2, 512], ctx)
        psO = m.ps("psO", [P, 512], ctx)
        psA = m.ps("psA", [P, 2, 512], ctx)
        psB = m.ps("psB", [P, 2, 512], ctx)
        rank = psO[:, 0:(GT + 1) * E]
        r = Router(m, ctx, "0", None)
        (ld, scaled, projected, biased, clipped, nat, nat_copied, up_a, up_b, silu, gated, down,
         added) = m.sems("ld0", "scaled", "projected", "biased", "clipped", "nat0", "nat_copied0",
                         "up_a", "up_b", "silu", "gated", "down", "added")
        with nc.Block() as block:
            @block.sync
            def _(sp):
                for dst, src in [(WT[:], d["WT"]), (xT[:], d["xT"]), (IG[:, 0:P], d["const"][:, C_ID:C_ID + P]),
                                 (IG[:, P:], d["Wg"]), (Ws1[:], d["Ws1"]), (Ws2[:], d["Ws2"]),
                                 (Ws3[:, 0:2, :], d["Ws3"][0:2 * P, :].rearrange("(k p) c -> p k c", p=P)),
                                 (Ws3[0:MS[2], 2, :], d["Ws3"][2 * P:HS, :]),
                                 (m.X[:], d["x"].rearrange("(s p) c -> p s c", p=P))]:
                    sp.dma_start(dst, src).then_inc(ld, 16)
                sp.wait_ge(ld, 16 * 9)

            @block.gpsimd
            def _(pool):
                for n, b, _ in rounds(pool, GROUPS, 2):
                    route_scatter(r, pool, n, b, nat_copied)
                for b in range(2):
                    pool.wait_ge(r.scattered[b], r.sends * GROUPS // 2)

            @block.vector
            def _(dve):
                chain = Chain(m, dve, r.link, ROUTE_LINKS)

                def scale(n, b):
                    wait(dve, projected, n - 1)
                    nc.vector.tensor_tensor(
                        xm[b][:], xT[:, bass.ds(n * GW, GW)].rearrange("p (s t) -> p s t", s=GT),
                        bc(m.styles[:, bass.ds(n * GT, GT)].unsqueeze(2), P, GT, P), ALU.mult).then_inc(scaled, 1)

                def clip(n, b):
                    dve.wait_ge(biased, n + 1)
                    wait(dve, down, n - 1)
                    nc.vector.tensor_scalar(xf[b][:], y[b][:], CLAMP, -CLAMP, ALU.min, ALU.max).then_inc(clipped, 1)

                def gate(n, b, k):
                    c, q = 3 * n + k, (3 * b + k) % 2
                    dve.wait_ge(up_b, c + 1)
                    dve.wait_ge(silu, c + 1)
                    wait(dve, down, n - 1)
                    nc.vector.tensor_tensor(h[b][k][0:MS[k], :], psB[0:MS[k], q, :], s[q][0:MS[k], :],
                                            ALU.mult).then_inc(gated, 1)

                dve.wait_ge(ld, 16 * 9)
                scale(0, 0)
                clip(0, 0)
                for n, b, i in rounds(dve, GROUPS, 2, head=2, tail=2):
                    route_choose(r, dve, chain, n, b, psN, nat)
                    if not is_last(n, GROUPS):
                        scale(n + 1, 1 - b)
                    gate(n, b, 0)
                    gate(n, b, 1)
                    route_index(r, dve, chain, n, b, i, rank)
                    if not is_last(n, GROUPS):
                        clip(n + 1, 1 - b)
                    gate(n, b, 2)
                    dve.wait_ge(down, n + 1)
                    nc.vector.tensor_tensor(m.X[:, bass.ds(n * GT, GT), :], m.X[:, bass.ds(n * GT, GT), :],
                                            psO[:].rearrange("p (s c) -> p s c", s=GT), ALU.add).then_inc(added, 1)

            @block.scalar
            def _(act):
                def bias(n, b):
                    act.wait_ge(projected, n + 1)
                    wait(act, clipped, n - 1)
                    for t in range(GT):
                        ins = nc.scalar.activation(y[b][:, t * P:(t + 1) * P], psY[:, t * P:(t + 1) * P], ACT.Identity,
                                                   bias=m.vec[:, V_BIAS:V_BIAS + 1],
                                                   scale=m.dcoef[:, bass.ds(n * GT + t, 1)])
                    ins.then_inc(biased, 1)

                act.wait_ge(ld, 16 * 9)
                bias(0, 0)
                for n, b, i in rounds(act, GROUPS, 2, head=2, tail=2):
                    act.wait_ge(r.got, n + 1)
                    wait(act, r.scattered[b], r.sends * i)
                    nc.scalar.activation(r.row[b][:].rearrange("p (a c) w -> p a c w", a=2),
                                         psN[:, :, 0:2 * (P + E)].rearrange("p a (c w) -> p a c w", c=2)[:, :, :, 0:P],
                                         ACT.Copy).then_inc(nat_copied, 1)
                    for k in range(3):
                        c, q = 3 * n + k, (3 * b + k) % 2
                        act.wait_ge(up_a, c + 1)
                        wait(act, gated, c - 1)
                        nc.scalar.activation(s[q][0:MS[k], :], psA[0:MS[k], q, :], ACT.Silu).then_inc(silu, 1)
                        if k == 1 and not is_last(n, GROUPS):
                            bias(n + 1, 1 - b)

            @block.tensor
            def _(pe):
                def project(n, b):
                    pe.wait_ge(scaled, n + 1)
                    wait(pe, biased, n)
                    nc.tensor.matmul(psY[:], WT[:], xm[b][:].rearrange("p s t -> p (s t)"),
                                     start=True, stop=True).then_inc(projected, 1)

                def up(n, b, k):
                    c, q = 3 * n + k, (3 * b + k) % 2
                    wait(pe, silu, c - 1)
                    nc.tensor.matmul(psA[0:MS[k], q, :], Ws1[:, k * P:k * P + MS[k]], xf[b][:],
                                     start=True, stop=True).then_inc(up_a, 1)
                    wait(pe, gated, c - 1)
                    nc.tensor.matmul(psB[0:MS[k], q, :], Ws2[:, k * P:k * P + MS[k]], xf[b][:],
                                     start=True, stop=True).then_inc(up_b, 1)

                pe.wait_ge(ld, 16 * 9)
                project(0, 0)
                for n, b, _ in rounds(pe, GROUPS, 2, head=2, tail=2):
                    pe.wait_ge(clipped, n + 1)
                    wait(pe, nat_copied, n)
                    for t in range(GT):
                        w = (t % 2) * (P + E)
                        ins = nc.tensor.matmul(psN[:, t // 2, w:w + P + E], xf[b][:, t * P:(t + 1) * P], IG[:],
                                               start=True, stop=True, skip_group_check=True)
                    ins.then_inc(nat, 1)
                    up(n, b, 0)
                    if not is_last(n, GROUPS):
                        project(n + 1, 1 - b)
                    up(n, b, 1)
                    wait(pe, added, n)
                    route_rank(r, pe, n, b, rank)
                    up(n, b, 2)
                    pe.wait_ge(r.indexed, n + 1)
                    pe.wait_ge(gated, 3 * n + 3)
                    for t in range(GT):
                        for k in range(3):
                            ins = nc.tensor.matmul(psO[:, t * P:(t + 1) * P], h[b][k][0:MS[k], t * P:(t + 1) * P],
                                                   Ws3[0:MS[k], k, :], start=(k == 0), stop=(k == 2),
                                                   skip_group_check=True)
                    ins.then_inc(down, 1)



EB = 4


def experts0(m, d):
    nc = m.nc
    with ExitStack() as ctx:
        sb = lambda n, s, dt=F32: m.sb(n, s, dt, ctx)
        w12 = [sb(f"w12_{b}", [P, 4, HALF]) for b in range(EB)]
        w3 = [sb(f"w3_{b}", [HALF, 2, P]) for b in range(EB)]
        xs = [sb(f"xs{b}", [P, 2, P]) for b in range(EB)]
        out = [sb(f"eo{b}", [P, 2, P]) for b in range(EB)]
        xsT = [sb(f"xsT{q}", [P, SLOTS]) for q in range(2)]
        s = [sb(f"es{q}", [HALF, 2, SLOTS]) for q in range(2)]
        h = [sb(f"eh{q}", [HALF, 2, SLOTS]) for q in range(2)]
        psT = m.ps("psT", [P, 2, 512], ctx)
        psA = m.ps("psA0", [P, 2, 512], ctx)
        psB = m.ps("psB0", [P, 2, 512], ctx)
        psO = m.ps("psO0", [P, 2, 512], ctx)
        ld = [m.sem(f"e0_ld{b}") for b in range(EB)]
        st = [m.sem(f"e0_st{b}") for b in range(EB)]
        (turned, copied, up_a, up_b, silu, gated, down, evac) = m.sems(
            "e0_turned", "e0_copied", "e0_up_a", "e0_up_b", "e0_silu", "e0_gated", "e0_down", "e0_evac")
        with nc.Block() as block:
            @block.sync
            def _(sp):
                for n, b, i in rounds(sp, ETILES, EB, head=EB):
                    e = sp.value_load(m.table[0:1, bass.ds(n, 1)], min_val=0, max_val=E - 1)
                    row = sp.value_load(m.table[0:1, bass.ds(n + ETILES, 1)], min_val=0, max_val=E * REGION)
                    hold(m, sp, down, n - EB + 1)
                    sp.dma_start(xs[b][:], m.xbuf[bass.ds(row, SLOTS), :].rearrange("(a p) c -> p a c", p=P)
                                 ).then_inc(ld[b], 16)
                    sp.dma_start(w12[b][:], d["W12"][bass.ds(e, 1)].rearrange("e p (a h) -> (e p) a h", a=4)
                                 ).then_inc(ld[b], 16)
                    sp.dma_start(w3[b][:], d["W3"][bass.ds(e, 1)].rearrange("e p (a h) -> (e p) a h", a=2)
                                 ).then_inc(ld[b], 16)

            @block.tensor
            def _(pe):
                def up(n, b, i):
                    q = b % 2
                    pe.wait_ge(ld[b], 48 * (i + 1))
                    wait(pe, copied, n - 1)
                    for a in range(2):
                        ins = nc.tensor.transpose(psT[:, q, a * P:(a + 1) * P], xs[b][:, a, :],
                                                  m.ident)
                    ins.then_inc(turned, 1)
                    pe.wait_ge(copied, n + 1)
                    wait(pe, silu, n - 1)
                    for a in range(2):
                        ins = nc.tensor.matmul(psA[0:HALF, q, a * SLOTS:(a + 1) * SLOTS], w12[b][:, a, :], xsT[q][:],
                                               start=True, stop=True, skip_group_check=True)
                    ins.then_inc(up_a, 1)
                    wait(pe, gated, n - 1)
                    for a in range(2):
                        ins = nc.tensor.matmul(psB[0:HALF, q, a * SLOTS:(a + 1) * SLOTS], w12[b][:, 2 + a, :], xsT[q][:],
                                               start=True, stop=True, skip_group_check=True)
                    ins.then_inc(up_b, 1)

                up(0, 0, 0)
                for n, b, i in rounds(pe, ETILES, EB, head=EB, tail=EB):
                    if not is_last(n, ETILES):
                        up(n + 1, (b + 1) % EB, i + (b + 1) // EB)
                    q = b % 2
                    pe.wait_ge(gated, n + 1)
                    wait(pe, evac, n - 1)
                    for a in range(2):
                        for k in range(2):
                            ins = nc.tensor.matmul(psO[:, q, a * P:(a + 1) * P], h[q][:, k, a * P:(a + 1) * P],
                                                   w3[b][:, k, :], start=(k == 0), stop=(k == 1), skip_group_check=True)
                    ins.then_inc(down, 1)

            @block.vector
            def _(dve):
                def copy(n, b):
                    q = b % 2
                    dve.wait_ge(turned, n + 1)
                    wait(dve, up_b, n - 1)
                    nc.vector.tensor_copy(xsT[q][:], psT[:, q, 0:SLOTS]).then_inc(copied, 1)

                copy(0, 0)
                for n, b, _ in rounds(dve, ETILES, EB, head=EB, tail=EB):
                    q = b % 2
                    if not is_last(n, ETILES):
                        copy(n + 1, (b + 1) % EB)
                    dve.wait_ge(up_b, n + 1)
                    dve.wait_ge(silu, n + 1)
                    wait(dve, down, n - 1)
                    nc.vector.tensor_tensor(h[q][:], psB[0:HALF, q, :].rearrange("p (a t) -> p a t", a=2), s[q][:],
                                            ALU.mult).then_inc(gated, 1)

            @block.scalar
            def _(act):
                def store(n, b, i):
                    act.wait_ge(down, n + 1)
                    wait(act, st[b], 16 * i)
                    nc.scalar.activation(out[b][:], psO[:, b % 2, 0:SLOTS].rearrange("p (a c) -> p a c", a=2), ACT.Copy
                                         ).then_inc(evac, 1)
                    act.wait_ge(evac, n + 1)
                    act.dma_start(m.ybuf[bass.ds(n * SLOTS, SLOTS), :].rearrange("(a p) c -> p a c", p=P), out[b][:]
                                  ).then_inc(st[b], 16)

                for n, b, i in rounds(act, ETILES, EB, head=2 * EB):
                    act.wait_ge(up_a, n + 1)
                    wait(act, gated, n - 1)
                    nc.scalar.activation(s[b % 2][:], psA[0:HALF, b % 2, :].rearrange("p (a t) -> p a t", a=2),
                                         ACT.Silu).then_inc(silu, 1)
                    if not first(n):
                        store(n - 1, (b - 1) % EB, i if b else i - 1)
                store(ETILES - 1, EB - 1, ETILES // EB - 1)
                for b in range(EB):
                    act.wait_ge(st[b], 16 * (ETILES // EB))



def gather(m, pool, n, b, index, rows, indexed, gathered, free, free_at):
    nc = m.nc
    wait(pool, free, free_at)
    nc.gpsimd.tensor_copy(index[b][:], m.gidx[:, bass.ds(n * GT * TOPK, GT * TOPK)]).then_inc(indexed, 1)
    hold(m, pool, indexed, n + 1)
    for c in range(GT * TOPK):
        pool.indirect_dma_start(
            out=rows[b][:, c, :], out_offset=None, in_=m.ybuf,
            in_offset=bass.IndirectOffsetOnAxis(ap=index[b][:, c:c + 1], axis=0)).then_inc(gathered[b], 16)


def finish(m, d, out):
    nc = m.nc
    with ExitStack() as ctx:
        index = [m.sb(f"fi{b}", [P, GT * TOPK], U32, ctx) for b in range(2)]
        rows = [m.sb(f"fr{b}", [P, GT * TOPK, P], F32, ctx) for b in range(2)]
        part = [m.sb(f"fp{b}", [P, GT, P], F32, ctx) for b in range(2)]
        res = [m.sb(f"fo{b}", [P, GT, P], F32, ctx) for b in range(2)]
        indexed, halfway, summed = m.sems("f_indexed", "f_halfway", "f_summed")
        gathered = m.sems("f_gathered0", "f_gathered1")
        stored = m.sems("f_stored0", "f_stored1")
        with nc.Block() as block:
            @block.gpsimd
            def _(pool):
                for n, b, i in rounds(pool, GROUPS, 2, head=2):
                    gather(m, pool, n, b, index, rows, indexed, gathered, summed, n - 1)

            @block.vector
            def _(dve):
                for n, b, i in rounds(dve, GROUPS, 2, head=2):
                    dve.wait_ge(gathered[b], 16 * GT * TOPK * (i + 1))
                    for t in range(GT):
                        ins = nc.vector.scalar_tensor_tensor(
                            out=part[b][:, t, :], in0=rows[b][:, 2 * t, :],
                            scalar=m.pw[:, bass.ds(n * GT + t, 1), 0:1].rearrange("p a k -> p (a k)"),
                            in1=m.X[:, bass.ds(n * GT + t, 1), :].rearrange("p a c -> p (a c)"), op0=ALU.mult, op1=ALU.add)
                    ins.then_inc(halfway, 1)
                    dve.wait_ge(halfway, n + 1)
                    wait(dve, stored[b], 16 * i)
                    for t in range(GT):
                        ins = nc.vector.scalar_tensor_tensor(
                            out=res[b][:, t, :], in0=rows[b][:, 2 * t + 1, :],
                            scalar=m.pw[:, bass.ds(n * GT + t, 1), 1:2].rearrange("p a k -> p (a k)"),
                            in1=part[b][:, t, :], op0=ALU.mult, op1=ALU.add)
                    ins.then_inc(summed, 1)

            @block.sync
            def _(sp):
                for n, b, i in rounds(sp, GROUPS, 2, head=2):
                    hold(m, sp, summed, n + 1)
                    sp.dma_start(out[bass.ds(n * GT, GT)].rearrange("s p c -> p s c"), res[b][:]).then_inc(stored[b], 16)
                for b in range(2):
                    sp.wait_ge(stored[b], 16 * (GROUPS // 2))


PRE_LINKS = 3


def pre_attention(m, d):
    nc = m.nc
    with ExitStack() as ctx:
        sb = lambda n, s, dt=F32: m.sb(n, s, dt, ctx)
        two = lambda n, s, dt=F32: [m.sb(f"{n}{b}", s, dt, ctx) for b in range(2)]
        wqkv = sb("wqkv", [P, 3 * P])
        dproj = sb("dproj", [P, DOWN])
        uproj = sb("uproj", [DOWN, P])
        index = two("gi", [P, GT * TOPK], U32)
        rows = two("gr", [P, GT * TOPK, P])
        part = two("part", [P, GT, P])
        x1, x2 = two("x1_", [P, GT, P]), two("x2_", [P, GT, P])
        gbu = two("gbu", [DOWN, GT, 2 * P])
        wd, wdt = two("wd", [P, GT, DOWN]), two("wdt", [P, GT, DOWN])
        wu, wut = two("wu", [P, GT, P]), two("wut", [DOWN, GT, P])
        x1T = two("x1T", [P, GW])
        aT = two("aT", [P, GW])
        stats = two("stats", [P, GT, 6])
        mv = two("mv", [P, GT, 2])
        var, std, rstd = two("var", [P, GT]), two("std", [P, GT]), two("rstd", [P, GT])
        norm = two("norm", [P, GT, P])
        hT = two("hT", [P, GW])
        qk = two("qk", [P, 4, GW], F32R)
        psX, psD, psU = m.ps("psX", [P, 512], ctx), m.ps("psD", [P, 512], ctx), m.ps("psU", [P, 512], ctx)
        psH, psV = m.ps("psH", [P, 512], ctx), m.ps("psV", [P, 512], ctx)
        psQK = m.ps("psQK", [P, 2, 512], ctx)
        (ld, indexed, cleared, blend1, blended, mod1, modded, turned, x1T_done, downed, relu, upped, x2_done,
         biased, link, sqrted, var_done, normed, turned2, hT_done, q_done, k_done, v_done, high, low, v_kept) = m.sems(
            "p_ld", "p_indexed", "p_cleared", "p_blend1", "p_blended", "p_mod1", "p_modded", "p_turned", "p_x1T",
            "p_downed", "p_relu", "p_upped", "p_x2", "p_biased", "p_link", "p_sqrted", "p_var", "p_normed", "p_turned2",
            "p_hT", "p_q", "p_k", "p_v", "p_high", "p_low", "p_v_kept")
        gathered = m.sems("p_gathered0", "p_gathered1")
        gbu_in = m.sems("p_gbu0", "p_gbu1")
        qk_out = m.sems("p_qk_out0", "p_qk_out1")
        qk_view = m.qk_dram.rearrange("a p t -> p a t")
        gb_up = m.gb_dram[:, 2 * DOWN:]
        with nc.Block() as block:
            @block.sync
            def _(sp):
                sp.dma_start(wqkv[:], d["wqkv"]).then_inc(ld, 16)
                sp.dma_start(dproj[:], d["dproj"]).then_inc(ld, 16)
                sp.dma_start(uproj[:], d["uproj"]).then_inc(ld, 16)

                def modulation(n, b):
                    hold(m, sp, modded, n - 1)
                    sp.dma_start(gbu[b][:], gb_up[bass.ds(n * GT, GT), :].unsqueeze(0).to_broadcast(
                        [DOWN, GT, 2 * P])).then_inc(gbu_in[b], 16)

                modulation(0, 0)
                for n, b, i in rounds(sp, GROUPS, 2, head=2, tail=2):
                    if not is_last(n, GROUPS):
                        modulation(n + 1, 1 - b)
                    sp.wait_ge(high, 2 * (n + 1))
                    hold(m, sp, low, 2 * (n + 1))
                    sp.dma_start(qk_view[:, :, bass.ds(n * GW, GW)], qk[b][:].bitcast(F32)).then_inc(qk_out[b], 16)
                for b in range(2):
                    sp.wait_ge(qk_out[b], 16 * GROUPS // 2)

            @block.gpsimd
            def _(pool):
                def keep(n, b):
                    mine = bass.ds(n * GT, GT)
                    pool.wait_ge(x2_done, n + 1)
                    nc.gpsimd.tensor_copy(m.X[:, mine, :], x1[b][:])
                    nc.gpsimd.tensor_tensor(m.X3[:, mine, :], x2[b][:], bc(m.rows[:, R_BO:R_BO + P].unsqueeze(1), P, GT, P),
                                            ALU.add).then_inc(biased, 1)

                for b in range(2):
                    nc.gpsimd.memset(aT[b][:], 0.0)
                    nc.gpsimd.memset(wu[b][:], 0.0).then_inc(cleared, 1)
                for n, b, i in rounds(pool, GROUPS, 2, head=2, tail=2):
                    gather(m, pool, n, b, index, rows, indexed, gathered, blended, n - 1)
                    if not first(n):
                        keep(n - 1, 1 - b)
                keep(GROUPS - 1, 1)

            @block.vector
            def _(dve):
                chain = Chain(m, dve, link, PRE_LINKS)

                def blend(n, b, i):
                    dve.wait_ge(gathered[b], 16 * GT * TOPK * (i + 1))
                    wait(dve, biased, n - 1)
                    weighted(m, n, part[b], rows[b], 0, m.X[:, bass.ds(n * GT, GT), :]).then_inc(blend1, 1)
                    dve.wait_ge(blend1, n + 1)
                    wait(dve, turned, n - 1)
                    weighted(m, n, x1[b], rows[b], 1, part[b][:]).then_inc(blended, 1)

                def modulate(n, b, i):
                    gd = m.gbD[:, bass.ds(n * GT, GT), :]
                    dve.wait_ge(gbu_in[b], 16 * (i + 1))
                    wait(dve, upped, n - 1)
                    nc.vector.tensor_tensor(wdt[b][:], bc(dproj[:].unsqueeze(1), P, GT, DOWN), gd[:, :, 0:DOWN], ALU.mult)
                    nc.vector.tensor_tensor(wut[b][:], bc(uproj[:].unsqueeze(1), DOWN, GT, P), gbu[b][:, :, 0:P],
                                            ALU.mult).then_inc(mod1, 1)
                    dve.wait_ge(mod1, n + 1)
                    nc.vector.tensor_tensor(wd[b][:], wdt[b][:], gd[:, :, DOWN:], ALU.add)
                    nc.vector.tensor_tensor(wu[b][0:DOWN], wut[b][:], gbu[b][:, :, P:], ALU.add).then_inc(modded, 1)

                dve.wait_ge(ld, 48)
                dve.wait_ge(cleared, 2)
                modulate(0, 0, 0)
                blend(0, 0, 0)
                for n, b, i in rounds(dve, GROUPS, 2, head=2, tail=2):
                    chain.begin(n)
                    mine = bass.ds(n * GT, GT)
                    dve.wait_ge(upped, n + 1)
                    wait(dve, biased, n - 1)
                    nc.vector.tensor_tensor(x2[b][:], psU[:].rearrange("p (t c) -> p t c", t=GT), x1[b][:],
                                            ALU.add).then_inc(x2_done, 1)
                    dve.wait_ge(x2_done, n + 1)
                    layernorm(m, dve, chain, n, lambda t: x2[b][:, t, :], stats[b], mv[b], var[b], var_done, std[b], sqrted, rstd[b], norm[b],
                              turned2, normed)
                    if not is_last(n, GROUPS):
                        modulate(n + 1, 1 - b, i + b)
                        blend(n + 1, 1 - b, i + b)
                    for w, ready in ((0, q_done), (1, k_done)):
                        dve.wait_ge(high, 2 * n + w + 1)
                        nc.vector.scalar_tensor_tensor(
                            out=qk[b][:, 2 * w + 1, :], in0=psQK[:, w, :], scalar=m.vec[:, V_BQ + w:V_BQ + w + 1],
                            in1=qk[b][:, 2 * w, :].bitcast(F32), op0=ALU.add, op1=ALU.subtract).then_inc(low, 1)
                    dve.wait_ge(v_done, n + 1)
                    nc.vector.tensor_tensor(m.V[:, mine, :], psV[:].rearrange("p (t c) -> p t c", t=GT),
                                            bc(m.rows[:, R_BV:R_BV + P].unsqueeze(1), P, GT, P), ALU.add
                                            ).then_inc(v_kept, 1)

            @block.scalar
            def _(act):
                act.wait_ge(cleared, 2)
                for n, b, i in rounds(act, GROUPS, 2, head=2):
                    act.wait_ge(turned, n + 1)
                    wait(act, downed, n - 1)
                    nc.scalar.activation(x1T[b][:], psX[:], ACT.Copy).then_inc(x1T_done, 1)
                    act.wait_ge(downed, n + 1)
                    wait(act, upped, n - 1)
                    nc.scalar.activation(aT[b][0:DOWN, :], psD[0:DOWN, :], ACT.Relu).then_inc(relu, 1)
                    act.wait_ge(var_done, n + 1)
                    nc.scalar.activation(std[b][:], var[b][:], ACT.Sqrt).then_inc(sqrted, 1)
                    act.wait_ge(turned2, n + 1)
                    wait(act, v_done, n - 1)
                    nc.scalar.activation(hT[b][:], psH[:], ACT.Identity, bias=m.vec[:, V_LN1B:V_LN1B + 1],
                                         scale=m.vec[:, V_LN1G:V_LN1G + 1]).then_inc(hT_done, 1)
                    wait(act, qk_out[b], 16 * i)
                    for w, ready in ((0, q_done), (1, k_done)):
                        act.wait_ge(ready, n + 1)
                        nc.scalar.activation(qk[b][:, 2 * w, :], psQK[:, w, :], ACT.Identity,
                                             bias=m.vec[:, V_BQ + w:V_BQ + w + 1]).then_inc(high, 1)

            @block.tensor
            def _(pe):
                pe.wait_ge(ld, 48)
                for n, b, i in rounds(pe, GROUPS, 2, head=2):
                    pe.wait_ge(blended, n + 1)
                    wait(pe, x1T_done, n)
                    for t in range(GT):
                        ins = nc.tensor.transpose(psX[:, t * P:(t + 1) * P], x1[b][:, t, :], m.ident)
                    ins.then_inc(turned, 1)
                    pe.wait_ge(x1T_done, n + 1)
                    pe.wait_ge(modded, n + 1)
                    wait(pe, relu, n)
                    for t in range(GT):
                        ins = nc.tensor.matmul(psD[0:DOWN, t * P:(t + 1) * P], wd[b][:, t, :], x1T[b][:, t * P:(t + 1) * P],
                                               start=True, stop=True, skip_group_check=True)
                    ins.then_inc(downed, 1)
                    pe.wait_ge(relu, n + 1)
                    wait(pe, x2_done, n)
                    for t in range(GT):
                        ins = nc.tensor.matmul(psU[:, t * P:(t + 1) * P], aT[b][:, t * P:(t + 1) * P], wu[b][:, t, :],
                                               start=True, stop=True, skip_group_check=True)
                    ins.then_inc(upped, 1)
                    pe.wait_ge(normed, n + 1)
                    wait(pe, hT_done, n)
                    for t in range(GT):
                        ins = nc.tensor.transpose(psH[:, t * P:(t + 1) * P], norm[b][:, t, :], m.ident)
                    ins.then_inc(turned2, 1)
                    pe.wait_ge(hT_done, n + 1)
                    for w, ready in ((0, q_done), (1, k_done)):
                        wait(pe, low, 2 * n - 1 + w)
                        nc.tensor.matmul(psQK[:, w, :], wqkv[:, w * P:(w + 1) * P], hT[b][:], start=True, stop=True
                                         ).then_inc(ready, 1)
                    wait(pe, v_kept, n)
                    for t in range(GT):
                        ins = nc.tensor.matmul(psV[:, t * P:(t + 1) * P], hT[b][:, t * P:(t + 1) * P], wqkv[:, 2 * P:],
                                               start=True, stop=True, skip_group_check=True)
                    ins.then_inc(v_done, 1)


def weighted(m, n, out, rows, k, plus):
    for t in range(GT):
        ins = m.nc.vector.scalar_tensor_tensor(
            out=out[:, t, :], in0=rows[:, TOPK * t + k, :],
            scalar=m.pw[:, bass.ds(n * GT + t, 1), k:k + 1].rearrange("p a k -> p (a k)"),
            in1=plus[:, t, :], op0=ALU.mult, op1=ALU.add)
    return ins


def layernorm(m, dve, chain, n, at, stats, mv, var, var_done, std, sqrted, rstd, norm, used, normed):
    nc = m.nc
    for t in range(GT):
        ins = nc.vector.bn_stats(stats[:, t, :], at(t))
    chain(ins)
    for t in range(GT):
        ins = nc.vector.bn_aggr(mv[:, t, :], stats[:, t, :])
    chain(ins)
    nc.vector.tensor_scalar(var[:], mv[:, :, 1], EPS, None, ALU.add).then_inc(var_done, 1)
    dve.wait_ge(sqrted, n + 1)
    chain(nc.vector.reciprocal(rstd[:], std[:]))
    wait(dve, used, n - 1)
    for t in range(GT):
        ins = nc.vector.tensor_scalar(norm[:, t, :], at(t), mv[:, t, 0:1], rstd[:, t:t + 1], ALU.subtract, ALU.mult)
    ins.then_inc(normed, 1)



PAIR = 2 * P
ATT_LINKS = 3


def attention(m, d):
    nc = m.nc
    with ExitStack() as ctx:
        sb = lambda n, s, dt=F32: m.sb(n, s, dt, ctx)
        two = lambda n, s, dt=F32: [m.sb(f"{n}{b}", s, dt, ctx) for b in range(2)]
        wo = sb("wo", [P, P])
        selr = sb("selr", [P, HG, P], F32R)
        qp = two("qp", [96, HG, PAIR], F32R)
        kp = two("kp", [96, HG, PAIR], F32R)
        qm = two("qm", [96, HG, 4, P], F32R)
        km = two("km", [96, HG, 4, P], F32R)
        vb = two("vb", [P, HEADS, 32])
        mneg = two("mneg", [P, HG, 4])
        xm = two("xmx", [P, 4, P])
        mxT = two("mxT", [P, 4 * P], F32R)
        prob = two("prob", [P, HG, 4 * P])
        rec = two("rec", [P, P])
        oT = two("oT", [P, P])
        ps1, ps2 = m.ps("ps1", [P, 2, 512], ctx), m.ps("ps2", [P, 2, 512], ctx)
        psM, psW = m.ps("psM", [P, 512], ctx), m.ps("psW", [P, 512], ctx)
        psO = m.ps("psAO", [P, 2, 512], ctx)
        (ld, cleared, made, qm_done, km_done, vb_done, scored, maxed, link, parted, turned, mxT_done, shifted,
         exped, mixed, divided, projected, kept) = m.sems(
            "a_ld", "a_cleared", "a_made", "a_qm", "a_km", "a_vb", "a_scored", "a_maxed", "a_link", "a_parted",
            "a_turned", "a_mxT", "a_shifted", "a_exped", "a_mixed", "a_divided", "a_projected", "a_kept")
        pair_in = m.sems("a_pair0", "a_pair1")
        mask = lambda j: m.const[0:96, C_MASK + j:C_MASK + j + 1]
        tok = lambda s4: slice((s4 % 2) * P, (s4 % 2 + 1) * P)
        PAIRS = SEQS // 2

        with nc.Block() as block:
            @block.sync
            def _(sp):
                sp.dma_start(wo[:], d["wo"]).then_inc(ld, 16)
                for n, b, i in rounds(sp, PAIRS, 2, head=2):
                    hold(m, sp, shifted, 8 * (n - 1))
                    hold(m, sp, qm_done, 2 * (n - 1))
                    hold(m, sp, km_done, 2 * (n - 1))
                    for side, parts in ((qp[b], (0, 1, 0)), (kp[b], (2, 2, 3))):
                        for r, a in enumerate(parts):
                            sp.dma_start(side[32 * r:32 * r + 32].bitcast(F32),
                                         m.qk_dram[a, :, bass.ds(n * PAIR, PAIR)].rearrange("(g r) t -> r g t", g=HG)
                                         ).then_inc(pair_in[b], 16)

            @block.gpsimd
            def _(pool):
                for b in range(2):
                    nc.gpsimd.memset(vb[b][:], 0.0)
                    nc.gpsimd.memset(xm[b][:], 0.0).then_inc(cleared, 1)
                pool.wait_ge(cleared, 2)
                for s, u, i in rounds(pool, SEQS, 4, head=4):
                    p, b = u % 2, u // 2
                    if p == 0:
                        pool.wait_ge(pair_in[b], 96 * (i + 1))
                    hold(m, pool, scored, 4 * (s - 1))
                    for j in range(4):
                        ins = nc.gpsimd.tensor_scalar(km[p][:, :, j, :], kp[b][:, :, tok(u)].bitcast(F32), mask(j), None,
                                                      ALU.mult)
                    ins.then_inc(km_done, 1)
                    wait(pool, mixed, s - 1)
                    for g in range(HG):
                        v = vb[p][:, 4 * g:4 * g + 4, :]
                        diag = bass.AP(v.tensor, v.offset, [list(v.ap[0]), [40, 4], [1, 8]])
                        ins = nc.gpsimd.tensor_copy(diag, m.V[:, bass.ds(s, 1), 32 * g:32 * g + 32].rearrange(
                            "p a (j e) -> p (a j) e", j=4))
                    ins.then_inc(vb_done, 1)

            @block.vector
            def _(dve):
                def maxima(s, u, i):
                    p = u % 2
                    for g in range(HG):
                        dve.wait_ge(scored, 4 * s + g + 1)
                        ins = nc.vector.tensor_reduce(mneg[p][:, g, :], ps1[:, g % 2, :].rearrange("p (j k) -> p j k", j=4),
                                                      AX_X, ALU.max, negate=True)
                        ins.then_inc(maxed, 1)
                    dve.wait_ge(maxed, 4 * s + 4)
                    wait(dve, turned, s - 1)
                    x = xm[p][:]
                    hi, lo = (bass.AP(x.tensor, x.offset + w, [list(x.ap[0]), [32, 4], [130, 4]]) for w in range(2))
                    nc.vector.tensor_copy(hi.bitcast(F32R), mneg[p][:]).then_inc(link, 1)
                    dve.wait_ge(link, s + 1)
                    nc.vector.tensor_tensor(lo, mneg[p][:], hi, ALU.subtract).then_inc(parted, 1)

                def mask_q(s, u, i):
                    p, b = u % 2, u // 2
                    if p == 0:
                        dve.wait_ge(pair_in[b], 96 * (i + 1))
                    wait(dve, shifted, 4 * (s - 1))
                    for j in range(4):
                        ins = nc.vector.tensor_scalar(qm[p][:, :, j, :], qp[b][:, :, tok(u)].bitcast(F32), mask(j), None,
                                                      ALU.mult)
                    ins.then_inc(qm_done, 1)

                def divide(s, u):
                    p = u % 2
                    dve.wait_ge(mixed, s + 1)
                    nc.vector.reciprocal(rec[p][:], psO[:, p, P:2 * P]).then_inc(made, 1)
                    dve.wait_ge(made, s + 1)
                    wait(dve, projected, s - 1)
                    nc.vector.tensor_tensor(oT[p][:], psO[:, p, 0:P], rec[p][:], ALU.mult).then_inc(divided, 1)

                def keep(s, u):
                    dve.wait_ge(projected, s + 1)
                    x3 = m.X3[:, bass.ds(s, 1), :].rearrange("p a c -> p (a c)")
                    nc.vector.tensor_tensor(x3, psW[:, 0:P], x3, ALU.add).then_inc(kept, 1)

                dve.wait_ge(cleared, 2)
                for g in range(HG):
                    ins = nc.vector.tensor_copy(selr[:, g, :], bc(m.const[:, C_SEL + g:C_SEL + g + 1], P, P))
                mask_q(0, 0, 0)
                maxima(0, 0, 0)
                for s, u, i in rounds(dve, SEQS, 4, head=4, tail=4):
                    nxt = (s + 1, (u + 1) % 4, i + (u + 1) // 4)
                    if not first(s):
                        divide(s - 1, u - 1)
                    if not is_last(s, SEQS):
                        maxima(*nxt)
                        mask_q(*nxt)
                    if not first(s):
                        keep(s - 1, u - 1)
                divide(SEQS - 1, 1)
                keep(SEQS - 1, 1)

            @block.scalar
            def _(act):
                def copy_max(s, u):
                    act.wait_ge(turned, s + 1)
                    wait(act, shifted, 4 * (s - 1))
                    nc.scalar.activation(mxT[u % 2][:], psM[:], ACT.Copy).then_inc(mxT_done, 1)

                copy_max(0, 0)
                for s, u, i in rounds(act, SEQS, 4, head=4, tail=4):
                    p = u % 2
                    wait(act, mixed, s - 1)
                    for g in range(HG):
                        act.wait_ge(shifted, 4 * s + g + 1)
                        nc.scalar.activation(prob[p][:, g, :], ps2[:, g % 2, :], ACT.Exp, scale=ATT_SCALE
                                             ).then_inc(exped, 1)
                    if not is_last(s, SEQS):
                        copy_max(s + 1, u + 1)

            @block.tensor
            def _(pe):
                def score(s, u, i, g):
                    p, b = u % 2, u // 2
                    wait(pe, maxed, 4 * s + g - 1)
                    nc.tensor.matmul(ps1[:, g % 2, :], qp[b][:, g, tok(u)], km[p][:, g].rearrange("p j k -> p (j k)"),
                                     start=True, stop=True).then_inc(scored, 1)

                def shift(s, u, g):
                    p, b = u % 2, u // 2
                    wait(pe, exped, 4 * s + g - 1)
                    nc.tensor.matmul(ps2[:, g % 2, :], kp[b][:, g, tok(u)], qm[p][:, g].rearrange("p j k -> p (j k)"),
                                     start=True, stop=False)
                    nc.tensor.matmul(ps2[:, g % 2, :], selr[:, g, :], mxT[p][:], start=False, stop=True
                                     ).then_inc(shifted, 1)

                def turn_max(s, u):
                    pe.wait_ge(parted, s + 1)
                    wait(pe, mxT_done, s)
                    for j in range(4):
                        ins = nc.tensor.transpose(psM[:, j * P:(j + 1) * P], xm[u % 2][:, j, :], m.ident)
                    ins.then_inc(turned, 1)

                def mix(s, u):
                    p = u % 2
                    pe.wait_ge(exped, 4 * s + 4)
                    pe.wait_ge(vb_done, s + 1)
                    wait(pe, divided, s - 1)
                    for j in range(4):
                        for g in range(HG):
                            nc.tensor.matmul(psO[32 * g:32 * g + 32, p, 0:P], vb[p][:, 4 * g + j, :],
                                             prob[p][:, g, j * P:(j + 1) * P], start=(j == 0), stop=(j == 3),
                                             skip_group_check=True)
                    for j in range(4):
                        for g in range(HG):
                            ins = nc.tensor.matmul(psO[32 * g:32 * g + 32, p, P:2 * P],
                                                   m.const[:, C_ONESB + 32 * j:C_ONESB + 32 * j + 32],
                                                   prob[p][:, g, j * P:(j + 1) * P], start=(j == 0), stop=(j == 3),
                                                   skip_group_check=True)
                    ins.then_inc(mixed, 1)

                def project(s, u):
                    pe.wait_ge(divided, s + 1)
                    wait(pe, kept, s)
                    nc.tensor.matmul(psW[:, 0:P], oT[u % 2][:], wo[:], start=True, stop=True).then_inc(projected, 1)

                def ready(s, u, i):
                    if u % 2 == 0:
                        pe.wait_ge(pair_in[u // 2], 96 * (i + 1))
                    pe.wait_ge(km_done, s + 1)

                pe.wait_ge(ld, 16)
                ready(0, 0, 0)
                for g in range(HG):
                    score(0, 0, 0, g)
                turn_max(0, 0)
                for s, u, i in rounds(pe, SEQS, 4, head=4, tail=4):
                    nxt = (s + 1, (u + 1) % 4, i + (u + 1) // 4)
                    more = not is_last(s, SEQS)
                    if more:
                        ready(*nxt)
                        score(*nxt, 0)
                        score(*nxt, 1)
                    pe.wait_ge(qm_done, s + 1)
                    pe.wait_ge(mxT_done, s + 1)
                    for g in range(HG):
                        shift(s, u, g)
                        if more and g < 2:
                            score(*nxt, g + 2)
                    if not first(s):
                        project(s - 1, u - 1)
                    if more:
                        turn_max(s + 1, u + 1)
                    mix(s, u)
                project(SEQS - 1, 1)



def post_attention(m, d):
    nc = m.nc
    with ExitStack() as ctx:
        two = lambda n, s, dt=F32: [m.sb(f"{n}{b}", s, dt, ctx) for b in range(2)]
        IG = m.sb("IG1", [P, P + E], ctx=ctx)
        stats = two("stats2", [P, GT, 6])
        mv = two("mv2", [P, GT, 2])
        var, std, rstd = two("var2", [P, GT]), two("std2", [P, GT]), two("rstd2", [P, GT])
        norm = two("norm2", [P, GT, P])
        hT = two("h2T", [P, GW])
        psH = m.ps("psH2", [P, 512], ctx)
        psN = m.ps("psN2", [P, 2, 512], ctx)
        psR = m.ps("psR2", [P, 512], ctx)
        rank = psR[:, 0:(GT + 1) * E]
        r = Router(m, ctx, "1", m.rows[:, R_GB:R_GB + E])
        ld, link, var_done, sqrted, normed, turned, hT_done, nat, nat_copied, summed = m.sems(
            "q_ld", "q_link", "q_var", "q_sqrted", "q_normed", "q_turned", "q_hT", "q_nat", "q_nat_copied", "q_summed")
        with nc.Block() as block:
            @block.sync
            def _(sp):
                sp.dma_start(IG[:, 0:P], d["const"][:, C_ID:C_ID + P]).then_inc(ld, 16)
                sp.dma_start(IG[:, P:], d["gate"]).then_inc(ld, 16)
                sp.wait_ge(ld, 32)

            @block.gpsimd
            def _(pool):
                for n, b, i in rounds(pool, GROUPS, 2):
                    route_scatter(r, pool, n, b, nat_copied)
                for b in range(2):
                    pool.wait_ge(r.scattered[b], r.sends * GROUPS // 2)

            @block.vector
            def _(dve):
                chain = Chain(m, dve, r.link, ROUTE_LINKS)
                ln = Chain(m, dve, link, 3)

                def normalise(n, b):
                    ln.begin(n)
                    at = lambda t: m.X3[:, bass.ds(n * GT + t, 1), :].rearrange("p a c -> p (a c)")
                    layernorm(m, dve, ln, n, at, stats[b], mv[b], var[b], var_done, std[b], sqrted, rstd[b], norm[b],
                              turned, normed)

                normalise(0, 0)
                for n, b, i in rounds(dve, GROUPS, 2, head=2, tail=2):
                    route_choose(r, dve, chain, n, b, psN, nat)
                    mine = bass.ds(n * GT, GT)
                    nc.vector.tensor_tensor(m.X[:, mine, :], m.X[:, mine, :], m.X3[:, mine, :], ALU.add)
                    if not is_last(n, GROUPS):
                        normalise(n + 1, 1 - b)
                    route_index(r, dve, chain, n, b, i, rank)

            @block.scalar
            def _(act):
                def root(n, b):
                    act.wait_ge(var_done, n + 1)
                    nc.scalar.activation(std[b][:], var[b][:], ACT.Sqrt).then_inc(sqrted, 1)

                def scale(n, b):
                    act.wait_ge(turned, n + 1)
                    wait(act, nat, n - 1)
                    nc.scalar.activation(hT[b][:], psH[:], ACT.Identity, bias=m.vec[:, V_LN2B:V_LN2B + 1],
                                         scale=m.vec[:, V_LN2G:V_LN2G + 1]).then_inc(hT_done, 1)

                root(0, 0)
                for n, b, i in rounds(act, GROUPS, 2, head=2, tail=2):
                    scale(n, b)
                    act.wait_ge(r.got, n + 1)
                    wait(act, r.scattered[b], r.sends * i)
                    nc.scalar.activation(r.row[b][:].rearrange("p (a c) w -> p a c w", a=2),
                                         psN[:, :, 0:2 * (P + E)].rearrange("p a (c w) -> p a c w", c=2)[:, :, :, 0:P],
                                         ACT.Copy).then_inc(nat_copied, 1)
                    if not is_last(n, GROUPS):
                        root(n + 1, 1 - b)

            @block.tensor
            def _(pe):
                pe.wait_ge(ld, 32)
                for n, b, i in rounds(pe, GROUPS, 2, head=2):
                    pe.wait_ge(normed, n + 1)
                    wait(pe, hT_done, n)
                    for t in range(GT):
                        ins = nc.tensor.transpose(psH[:, t * P:(t + 1) * P], norm[b][:, t, :], m.ident)
                    ins.then_inc(turned, 1)
                    pe.wait_ge(hT_done, n + 1)
                    wait(pe, nat_copied, n)
                    for t in range(GT):
                        w = (t % 2) * (P + E)
                        ins = nc.tensor.matmul(psN[:, t // 2, w:w + P + E], hT[b][:, t * P:(t + 1) * P], IG[:],
                                               start=True, stop=True, skip_group_check=True)
                    ins.then_inc(nat, 1)
                    route_rank(r, pe, n, b, rank)


def experts1(m, d):
    nc = m.nc
    WIDE = KT1 * P
    with ExitStack() as ctx:
        sb = lambda n, s, dt=F32: m.sb(n, s, dt, ctx)
        wb = [sb(f"wb{b}", [P, 2 * WIDE + KT1]) for b in range(EB)]
        b2 = [sb(f"b2_{b}", [P, P]) for b in range(EB)]
        xs = [sb(f"xt{b}", [P, 2, P]) for b in range(EB)]
        out = [sb(f"fo_{b}", [P, 2, P]) for b in range(EB)]
        xsT = [sb(f"xtT{q}", [P, SLOTS]) for q in range(2)]
        h = [sb(f"fh{q}", [P, KT1, SLOTS]) for q in range(2)]
        psT = m.ps("psT1", [P, 2, 512], ctx)
        psA = m.ps("psA1", [P, 4, 512], ctx)
        psO = m.ps("psO1", [P, 2, 512], ctx)
        ld = [m.sem(f"e1_ld{b}") for b in range(EB)]
        st = [m.sem(f"e1_st{b}") for b in range(EB)]
        turned, copied, up_a, up_b, relu_a, relu_b, down, evac = m.sems(
            "e1_turned", "e1_copied", "e1_up_a", "e1_up_b", "e1_relu_a", "e1_relu_b", "e1_down", "e1_evac")
        with nc.Block() as block:
            @block.sync
            def _(sp):
                for n, b, i in rounds(sp, ETILES, EB, head=EB):
                    e = sp.value_load(m.table[0:1, bass.ds(n, 1)], min_val=0, max_val=E - 1)
                    row = sp.value_load(m.table[0:1, bass.ds(n + ETILES, 1)], min_val=0, max_val=E * REGION)
                    hold(m, sp, down, n - EB + 1)
                    hold(m, sp, evac, n - EB + 1)
                    sp.dma_start(xs[b][:], m.xbuf[bass.ds(row, SLOTS), :].rearrange("(a p) c -> p a c", p=P)
                                 ).then_inc(ld[b], 16)
                    sp.dma_start(wb[b][:], d["W1b"][bass.ds(e, 1)].rearrange("e p h -> (e p) h")).then_inc(ld[b], 16)
                    sp.dma_start(b2[b][:], d["b2"][bass.ds(e, 1)].to_broadcast([P, P])).then_inc(ld[b], 16)

            @block.tensor
            def _(pe):
                def turn(n, b, i):
                    q = b % 2
                    pe.wait_ge(ld[b], 48 * (i + 1))
                    wait(pe, copied, n - 1)
                    for a in range(2):
                        ins = nc.tensor.transpose(psT[:, q, a * P:(a + 1) * P], xs[b][:, a, :], m.ident)
                    ins.then_inc(turned, 1)

                def up(n, b):
                    q = b % 2
                    pe.wait_ge(copied, n + 1)
                    for half, free, done in ((0, relu_a, up_a), (1, relu_b, up_b)):
                        wait(pe, free, 2 * (n - 1))
                        for a in range(2):
                            k = 2 * half + a
                            ins = nc.tensor.matmul(psA[:, 2 * q + half, a * SLOTS:(a + 1) * SLOTS], wb[b][:, k * P:(k + 1) * P],
                                                   xsT[q][:], start=True, stop=True, skip_group_check=True)
                        ins.then_inc(done, 1)

                turn(0, 0, 0)
                up(0, 0)
                for n, b, i in rounds(pe, ETILES, EB, head=EB, tail=EB):
                    nxt = (n + 1, (b + 1) % EB)
                    if not is_last(n, ETILES):
                        turn(*nxt, i + (b + 1) // EB)
                        up(*nxt)
                    q = b % 2
                    pe.wait_ge(relu_a, 2 * (n + 1))
                    pe.wait_ge(relu_b, 2 * (n + 1))
                    wait(pe, evac, n - 1)
                    for a in range(2):
                        for k in range(KT1):
                            ins = nc.tensor.matmul(psO[:, q, a * P:(a + 1) * P], h[q][:, k, a * P:(a + 1) * P],
                                                   wb[b][:, WIDE + k * P:WIDE + (k + 1) * P],
                                                   start=(k == 0), stop=(k == KT1 - 1), skip_group_check=True)
                    ins.then_inc(down, 1)

            @block.vector
            def _(dve):
                def copy(n, b):
                    dve.wait_ge(turned, n + 1)
                    wait(dve, up_b, n - 1)
                    nc.vector.tensor_copy(xsT[b % 2][:], psT[:, b % 2, 0:SLOTS]).then_inc(copied, 1)

                def leave(n, b, i):
                    dve.wait_ge(down, n + 1)
                    wait(dve, st[b], 16 * i)
                    nc.vector.tensor_tensor(out[b][:], psO[:, b % 2, 0:SLOTS].rearrange("p (a c) -> p a c", a=2),
                                            bc(b2[b][:].unsqueeze(1), P, 2, P), ALU.add).then_inc(evac, 1)

                copy(0, 0)
                for n, b, i in rounds(dve, ETILES, EB, head=EB, tail=EB):
                    if not is_last(n, ETILES):
                        copy(n + 1, (b + 1) % EB)
                    q = b % 2
                    dve.wait_ge(up_b, n + 1)
                    wait(dve, down, n - 1)
                    for a in range(2):
                        nc.vector.tensor_scalar(h[q][:, 2 + a, :], psA[:, 2 * q + 1, a * SLOTS:(a + 1) * SLOTS],
                                                wb[b][:, 2 * WIDE + 2 + a:2 * WIDE + 3 + a], 0.0, ALU.add, ALU.max
                                                ).then_inc(relu_b, 1)
                    if not first(n):
                        leave(n - 1, (b - 1) % EB, i if b else i - 1)
                leave(ETILES - 1, EB - 1, ETILES // EB - 1)

            @block.scalar
            def _(act):
                def store(n, b):
                    act.wait_ge(evac, n + 1)
                    act.dma_start(m.ybuf[bass.ds(n * SLOTS, SLOTS), :].rearrange("(a p) c -> p a c", p=P), out[b][:]
                                  ).then_inc(st[b], 16)

                for n, b, i in rounds(act, ETILES, EB, head=EB):
                    q = b % 2
                    act.wait_ge(up_a, n + 1)
                    wait(act, down, n - 1)
                    for a in range(2):
                        nc.scalar.activation(h[q][:, a, :], psA[:, 2 * q, a * SLOTS:(a + 1) * SLOTS], ACT.Relu,
                                             bias=wb[b][:, 2 * WIDE + a:2 * WIDE + a + 1]).then_inc(relu_a, 1)
                    if not first(n):
                        store(n - 1, (b - 1) % EB)
                store(ETILES - 1, EB - 1)
                for b in range(EB):
                    act.wait_ge(st[b], 16 * (ETILES // EB))


def build(nc, d, out):
    with ExitStack() as ctx:
        m = Machine(nc, ctx)
        allocate(m, d)
        setup(m, d)
        layer0(m, d)
        tile_table(m, "0")
        experts0(m, d)
        pre_attention(m, d)
        attention(m, d)
        post_attention(m, d)
        tile_table(m, "1")
        experts1(m, d)
        finish(m, d, out)



def laid_out(a):
    x = np.ascontiguousarray(a["x"]).reshape(TOK, P)
    W3 = a["L0_ffn_W3"].reshape(E, 2, HALF, P).transpose(0, 2, 1, 3).reshape(E, HALF, 2 * P)
    W2b = a["L1_ffn_W2"].reshape(E, KT1, P, P).transpose(0, 2, 1, 3).reshape(E, P, KT1 * P)
    b1 = a["L1_ffn_b1"].reshape(E, KT1, P).transpose(0, 2, 1)
    b_qkv = a["L1_ffn_b_qkv"]
    vec = [a["L0_cond_bias"], a["L0_cond_affine_b"], a["L1_ffn_ln1_g"], a["L1_ffn_ln1_b"], a["L1_ffn_ln2_g"],
           a["L1_ffn_ln2_b"], b_qkv[0:P], b_qkv[P:2 * P]]
    out = {
        "x": x, "xT": x.T, "const": constants(),
        "condT": a["cond_512"].T, "affT": a["L0_cond_affine_w"].T, "WT": a["L0_cond_weight"].T,
        "vec": np.stack(vec, axis=1),
        "rows": np.concatenate([b_qkv[2 * P:], a["L1_ffn_b_o"], a["L1_ffn_gate_b"]])[None, :],
        "gb": np.concatenate([a["L1_cond_down_gamma"], a["L1_cond_down_beta"],
                              a["L1_cond_up_gamma"], a["L1_cond_up_beta"]], axis=1),
        "Wg": a["L0_ffn_Wg"], "W12": np.concatenate([a["L0_ffn_W1"], a["L0_ffn_W2"]], axis=2), "W3": W3,
        "Ws1": a["L0_ffn_Ws1"], "Ws2": a["L0_ffn_Ws2"], "Ws3": a["L0_ffn_Ws3"],
        "dproj": a["L1_cond_down_project"], "uproj": a["L1_cond_up_project"],
        "wqkv": a["L1_ffn_w_qkv"], "wo": a["L1_ffn_w_o"], "gate": a["L1_ffn_gate_w"],
        "W1b": np.concatenate([a["L1_ffn_W1"], W2b, b1], axis=2), "b2": a["L1_ffn_b2"],
    }
    return {k: np.ascontiguousarray(v) for k, v in out.items()}


def kernel(**inputs):
    import concourse.bacc as bacc
    from concourse.bass_utils import run_bass_kernel_spmd

    nc = bacc.Bacc("TRN2", target_bir_lowering=False, num_devices=1)
    arrays = {f"in_{k}": v for k, v in laid_out({k: np.asarray(v) for k, v in inputs.items()}).items()}
    d = {k[3:]: nc.dram_tensor(k, v.shape, mybir.dt.from_np(v.dtype), kind="ExternalInput").ap()
         for k, v in arrays.items()}
    out = nc.dram_tensor("out", (SEQS, P, P), F32, kind="ExternalOutput").ap()
    build(nc, d, out)
    r = run_bass_kernel_spmd(nc, [arrays], core_ids=[0])
    return r.results[0]["out"]
```

```python
from contextlib import ExitStack

import numpy as np

import concourse.bass as bass
from concourse import mybir

F32 = mybir.dt.float32
F32R = mybir.dt.float32r
BF16 = mybir.dt.bfloat16
U32 = mybir.dt.uint32
I32 = mybir.dt.int32
ALU = mybir.AluOpType
ACT = mybir.ActivationFunctionType
AX_X = mybir.AxisListType.X

P = 128
SEQS = 32
TOK = SEQS * P
GT = 4
GROUPS = SEQS // GT
GW = GT * P
E = 8
TOPK = 2
COND = 64
SLOTS = 256
REGION = TOK + SLOTS
ETILES = TOK * TOPK // SLOTS + E
MAXT = TOK // SLOTS
ROW = P + 1
HALF = 88
HS = 352
DOWN = 32
HEADS = 16
HG = 4
KT1 = 4
SHARED = [P, P, HS - 2 * P]
CLAMP = 256.0
EPS = 1e-5
ATT_SCALE = float(1.0 / np.sqrt(8.0))

C_ID = 0
C_TRI = C_ID + P
C_ONESB = C_TRI + P
C_SEL = C_ONESB + P
C_MASK = C_SEL + 4
C_EXP = C_MASK + 4
C_REG = C_EXP + E + 1
C_TILE = C_REG + E + 1
C_STEP = C_TILE + ETILES
C_TOK = C_STEP + MAXT
C_TAIL = C_TOK + SEQS * TOPK
C_END = C_TAIL + 4 * E

V_BIAS, V_AFFB, V_LN1G, V_LN1B, V_LN2G, V_LN2B, V_BQ, V_BK = range(8)
R_BV, R_BO, R_GB = 0, P, 2 * P
R_END = 2 * P + E


def constants():
    c = np.zeros((P, C_END), np.float32)
    p = np.arange(P)
    c[:, C_ID:C_ID + P] = np.eye(P)
    c[:, C_TRI:C_TRI + P] = p[:, None] < p[None, :]
    col = np.arange(32)
    for j in range(4):
        c[:, C_ONESB + 32 * j:C_ONESB + 32 * j + 32] = (col // 8 == j)[None, :]
        c[:, C_SEL + j] = (p // 32 == j) & (p % 32 < 8)
        c[:, C_MASK + j] = (p % 32) // 8 == j
    c[:, C_EXP:C_EXP + E + 1] = np.arange(E + 1)
    c[:, C_REG:C_REG + E + 1] = np.arange(E + 1) * REGION
    c[:, C_TOK:C_TOK + SEQS * TOPK] = 2 * p[:, None] + (np.arange(SEQS)[:, None] * 2 * P + np.arange(2)).reshape(1, -1)
    c[:, C_TAIL:C_TAIL + 4 * E] = 2 * TOK + p[:, None] + np.arange(4 * E)[None, :] * P
    c[:, C_TILE:C_TILE + ETILES] = np.arange(ETILES)
    c[:, C_STEP:C_STEP + MAXT] = np.arange(MAXT) * SLOTS
    return c


def rounds(engine, total, unroll, head=0, tail=0):
    for n in range(head):
        yield n, n % unroll, n // unroll
    with engine.Fori(0, (total - head - tail) // unroll) as i:
        for u in range(unroll):
            yield i * unroll + (head + u), u, i + head // unroll
    for n in range(total - tail, total):
        yield n, n % unroll, n // unroll


def first(n):
    return isinstance(n, int) and n == 0


def is_last(n, total):
    return isinstance(n, int) and n == total - 1


def wait(engine, sem, value):
    if not (isinstance(value, int) and value <= 0):
        engine.wait_ge(sem, value)


def hold(m, engine, sem, value):
    wait(engine, sem, value)
    if not isinstance(value, int):
        engine.sem_inc(m.passed, 1)


class Chain:

    def __init__(self, m, engine, sem, per=0):
        self.m = m
        self.engine, self.sem, self.per, self.base, self.count = engine, sem, per, 0, 0

    def begin(self, n):
        self.base, self.count = n * self.per, 0

    def __call__(self, instruction):
        self.count += 1
        instruction.then_inc(self.sem, 1)
        hold(self.m, self.engine, self.sem, self.base + self.count)


def late(n, ahead=2):
    return isinstance(n, int) and n >= GROUPS - ahead


def bc(ap, *shape):
    return ap.to_broadcast(list(shape))


class Machine:

    def __init__(self, nc, ctx):
        self.nc, self.ctx = nc, ctx

    def sb(self, name, shape, dt=F32, ctx=None):
        return (ctx or self.ctx).enter_context(self.nc.sbuf_tensor(name, shape, dt))

    def ps(self, name, shape, ctx, dt=F32):
        return ctx.enter_context(self.nc.psum_tensor(name, shape, dt))

    def sem(self, name):
        return self.ctx.enter_context(self.nc.semaphore(name))

    def sems(self, *names):
        return [self.sem(n) for n in names]


def allocate(m, d):
    nc = m.nc
    m.passed = m.sem("passed")
    m.X = m.sb("X", [P, SEQS, P])
    m.X3 = m.sb("X3", [P, SEQS, P])
    m.V = m.sb("V", [P, SEQS, P])
    m.const = m.sb("const", [P, C_END])
    m.vec = m.sb("vec", [P, 8])
    m.rows = m.sb("rows", [P, R_END])
    m.tri = m.sb("tri", [P, P], BF16)
    m.ones = m.sb("ones", [P, P], BF16)
    m.ident = m.const[:, C_ID:C_ID + P]
    m.diff = m.sb("diff", [P, SEQS])
    m.pw = m.sb("pw", [P, SEQS, TOPK])
    m.ids = m.sb("ids", [P, SEQS, TOPK], U32)
    m.base = m.sb("base", [P, E + 1])
    m.tail = m.sb("tail", [P, 2 * E, 2, ROW])
    m.table = m.sb("table", [P, 2 * ETILES + E], I32)
    m.styles = m.sb("styles", [P, SEQS])
    m.dcoef = m.sb("dcoef", [P, SEQS])
    m.gbD = m.sb("gbD", [P, SEQS, 2 * DOWN])
    m.wqkv = m.sb("wqkv", [P, 3 * P])
    m.dproj = m.sb("dproj", [P, DOWN])
    m.uproj = m.sb("uproj", [DOWN, P])
    m.wo = m.sb("wo", [P, P])
    m.gate = m.sb("gate", [P, E])
    m.late_ld, m.gb_in = m.sems("late_ld", "gb_in")
    m.xbuf = nc.dram_tensor("dispatch_rows", (E * REGION + E * SLOTS, ROW), F32, kind="Internal").ap()
    m.ybuf = nc.dram_tensor("expert_rows", (TOPK * TOK + 2 * E * SLOTS, P), F32, kind="Internal").ap()
    m.gb_dram = nc.dram_tensor("cond_rows", (SEQS, 2 * DOWN + 2 * P), F32, kind="Internal").ap()
    m.qk_dram = nc.dram_tensor("qk_parts", (4, P, TOK), F32, kind="Internal").ap()



FIRST_LOADS = 16 * 7
LATE_LOADS = 16 * 6


def layer0_loads(m, ctx):
    sb = lambda n, s: m.sb(n, s, ctx=ctx)
    return (sb("xT", [P, TOK]), sb("WT", [P, P]), sb("IG0", [P, P + E]), sb("Ws1", [P, HS]), sb("Ws2", [P, HS]),
            sb("Ws3", [P, 3, P]), m.sem("first_ld"), m.sem("rest_ld"), m.sem("x_ld"))


def setup(m, d, loads):
    nc = m.nc
    xT, WT, IG, Ws1, Ws2, Ws3, first_ld, rest_ld, x_ld = loads
    with ExitStack() as ctx:
        condT = m.sb("condT", [COND, SEQS], ctx=ctx)
        affT = m.sb("affT", [COND, P], ctx=ctx)
        gb = m.sb("gb", [COND, 2 * DOWN + 2 * P], ctx=ctx)
        sq = m.sb("sq", [P, P], ctx=ctx)
        ssq = m.sb("ssq", [P, SEQS], ctx=ctx)
        dsum = m.sb("dsum", [P, SEQS], ctx=ctx)
        root, guess = m.sb("root", [P, SEQS], ctx=ctx), m.sb("guess", [P, SEQS], ctx=ctx)
        gbrow = m.sb("gbrow", [SEQS, 2 * DOWN + 2 * P], ctx=ctx)
        ps = m.ps("ps_setup", [P, 3, 512], ctx)
        (loaded, styled, squared, pe_st, pe_dc, pe_gb, gb_copied, summed, rooted, gb_out, cleared, newton) = m.sems(
            "loaded", "styled", "squared", "pe_st", "pe_dc", "pe_gb", "gb_copied", "summed", "rooted", "gb_out",
            "set_cleared", "newton")
        with nc.Block() as block:
            @block.sync
            def _(sp):
                for dst, src in [(condT[:], d["condT"]), (affT[:], d["affT"]), (WT[:], d["WT"]), (m.vec[:], d["vec"]),
                                 (gb[:], d["gb"]), (m.const[:], d["const"])]:
                    sp.dma_start(dst, src).then_inc(loaded, 16)
                def load(*transfers):
                    for dst, src, sem in transfers:
                        sp.dma_start(dst, src).then_inc(sem, 16)

                load((xT[:, 0:2 * GW], d["xT"][:, 0:2 * GW], first_ld),
                        (IG[:, 0:P], d["const"][:, C_ID:C_ID + P], first_ld), (IG[:, P:], d["Wg"], first_ld),
                        (Ws1[:], d["Ws1"], first_ld), (Ws2[:], d["Ws2"], first_ld),
                        (Ws3[:, 0:2, :], d["Ws3"][0:2 * P, :].rearrange("(k p) c -> p k c", p=P), first_ld),
                        (Ws3[0:SHARED[2], 2, :], d["Ws3"][2 * P:HS, :], first_ld))
                sp.wait_ge(gb_copied, 1)
                load((xT[:, 2 * GW:], d["xT"][:, 2 * GW:], rest_ld),
                        (m.X[:], d["x"].rearrange("(s p) c -> p s c", p=P), x_ld),
                        (m.rows[:], d["rows"].to_broadcast([P, R_END]), m.late_ld),
                        (m.wqkv[:], d["wqkv"], m.late_ld), (m.dproj[:], d["dproj"], m.late_ld),
                        (m.uproj[:], d["uproj"], m.late_ld), (m.wo[:], d["wo"], m.late_ld),
                        (m.gate[:], d["gate"], m.late_ld))

            @block.gpsimd
            def _(pool):
                nc.gpsimd.memset(m.ones[:], 1.0)
                nc.gpsimd.memset(m.tail[:], 0.0).then_inc(cleared, 1)

            @block.tensor
            def _(pe):
                pe.wait_ge(loaded, 16 * 6)
                nc.tensor.matmul(ps[:, 0, 0:SEQS], affT[:], condT[:], start=True, stop=True).then_inc(pe_st, 1)
                nc.tensor.matmul(ps[0:SEQS, 1, 0:2 * DOWN + 2 * P], condT[:], gb[:], start=True,
                                 stop=True).then_inc(pe_gb, 1)
                pe.wait_ge(squared, 2)
                nc.tensor.matmul(ps[:, 2, 0:SEQS], sq[:], ssq[:], start=True, stop=True).then_inc(pe_dc, 1)

            @block.scalar
            def _(act):
                act.wait_ge(gb_copied, 1)
                act.dma_start(m.gb_dram, gbrow[:]).then_inc(gb_out, 16)
                act.wait_ge(summed, 1)
                nc.scalar.activation(root[:], dsum[:], ACT.Sqrt).then_inc(rooted, 1)
                act.wait_ge(gb_out, 16)
                act.dma_start(m.gbD[:], m.gb_dram[:, 0:2 * DOWN].unsqueeze(0).to_broadcast(
                    [P, SEQS, 2 * DOWN])).then_inc(m.gb_in, 16)

            @block.vector
            def _(dve):
                c = Chain(m, dve, newton)
                dve.wait_ge(loaded, 16 * 6)
                nc.vector.tensor_tensor(sq[:], WT[:], WT[:], ALU.mult).then_inc(squared, 1)
                dve.wait_ge(pe_st, 1)
                nc.vector.tensor_scalar(m.styles[:], ps[:, 0, 0:SEQS], float(1 / np.sqrt(COND)),
                                        m.vec[:, V_AFFB:V_AFFB + 1], ALU.mult, ALU.add).then_inc(styled, 1)
                dve.wait_ge(pe_gb, 1)
                nc.vector.tensor_copy(gbrow[:], ps[0:SEQS, 1, 0:2 * DOWN + 2 * P]).then_inc(gb_copied, 1)
                dve.wait_ge(styled, 1)
                nc.vector.tensor_tensor(ssq[:], m.styles[:], m.styles[:], ALU.mult).then_inc(squared, 1)
                nc.vector.tensor_copy(m.tri[:], m.const[:, C_TRI:C_TRI + P])
                nc.vector.tensor_copy(m.base[:], m.const[:, C_REG:C_REG + E + 1])
                dve.wait_ge(pe_dc, 1)
                nc.vector.tensor_scalar(dsum[:], ps[:, 2, 0:SEQS], 1e-8, None, ALU.add).then_inc(summed, 1)
                nc.vector.tensor_copy(m.ids[:].rearrange("p s k -> p (s k)"), m.const[:, C_TOK:C_TOK + SEQS * TOPK])
                dve.wait_ge(cleared, 1)
                nc.vector.tensor_copy(m.tail[:, :, :, P:].bitcast(U32),
                                      m.const[:, C_TAIL:C_TAIL + 4 * E].rearrange("p (e a o) -> p e a o", a=2, o=1))
                dve.wait_ge(rooted, 1)
                c(nc.vector.reciprocal(guess[:], root[:]))
                c(nc.vector.tensor_tensor(root[:], guess[:], guess[:], ALU.mult))
                c(nc.vector.tensor_tensor(root[:], root[:], dsum[:], ALU.mult))
                c(nc.vector.tensor_scalar(root[:], root[:], -0.5, 1.5, ALU.mult, ALU.add))
                nc.vector.tensor_tensor(m.dcoef[:], root[:], guess[:], ALU.mult)



ROUTE_LINKS = 5


class Router:

    def __init__(self, m, ctx, tag, bias):
        self.m, self.bias = m, bias
        self.logits = [m.sb(f"logits{tag}{b}", [P, GT, E], ctx=ctx) for b in range(2)]
        self.best = [m.sb(f"best{tag}{b}", [P, GT, 8], ctx=ctx) for b in range(2)]
        self.choice = [m.sb(f"choice{tag}{b}", [P, GT, 8], U32, ctx=ctx) for b in range(2)]
        self.mask = [m.sb(f"mask{tag}{b}", [P, GT, E], BF16, ctx=ctx) for b in range(2)]
        self.slot = [m.sb(f"slot{tag}{b}", [P, GT, E], ctx=ctx) for b in range(2)]
        self.prod = [m.sb(f"prod{tag}{b}", [P, GT, TOPK, E], ctx=ctx) for b in range(2)]
        self.index = [m.sb(f"index{tag}{b}", [P, GT * TOPK], U32, ctx=ctx) for b in range(2)]
        self.hot = [m.sb(f"hot{tag}{b}", [P, GT, TOPK, E], ctx=ctx) for b in range(2)]
        self.row = [m.sb(f"row{tag}{b}", [P, GT, TOPK, ROW], ctx=ctx) for b in range(2)]
        (self.link, self.got, self.masked, self.ranked,
         self.indexed) = m.sems(*(f"{s}{tag}" for s in ("rt_link", "rt_got", "rt_masked", "rt_ranked", "rt_indexed")))
        self.scattered = m.sems(f"rt_scattered{tag}_0", f"rt_scattered{tag}_1")
        self.sends = 16 * GT * TOPK


def route_choose(r, dve, chain, n, b, nat, nat_ready):
    m, nc = r.m, r.m.nc
    tiles = bass.ds(n * GT, GT)
    chain.begin(n)
    dve.wait_ge(nat_ready, n + 1)
    lg = r.logits[b][:].rearrange("p (a c) e -> p a c e", a=2)
    src = nat[:, :, 0:2 * (P + E)].rearrange("p a (c w) -> p a c w", c=2)[:, :, :, P:P + E]
    if r.bias is None:
        ins = nc.vector.tensor_copy(lg, src)
    else:
        ins = nc.vector.tensor_tensor(lg, src, bc(r.bias.unsqueeze(1).unsqueeze(1), P, 2, 2, E), ALU.add)
    ins.then_inc(r.got, 1)
    hold(m, dve, r.got, n + 1)
    for t in range(GT):
        ins = nc.vector.max(r.best[b][:, t, :], r.logits[b][:, t, :])
    chain(ins)
    for t in range(GT):
        ins = nc.vector.max_index(r.choice[b][:, t, :], r.best[b][:, t, :], r.logits[b][:, t, :])
    chain(ins)
    nc.vector.tensor_tensor(m.diff[:, tiles], r.best[b][:, :, 1], r.best[b][:, :, 0], ALU.subtract)
    chain(nc.vector.tensor_tensor(
        r.hot[b][:], bc(r.choice[b][:, :, 0:TOPK].unsqueeze(3), P, GT, TOPK, E),
        bc(m.const[:, C_EXP:C_EXP + E].unsqueeze(1).unsqueeze(1), P, GT, TOPK, E), ALU.is_equal))
    nc.vector.tensor_tensor(r.mask[b][:], r.hot[b][:, :, 0, :], r.hot[b][:, :, 1, :], ALU.add).then_inc(r.masked, 1)


def route_rank(r, pe, n, b, rank):
    m, nc = r.m, r.m.nc
    pe.wait_ge(r.masked, n + 1)
    wait(pe, r.indexed, n)
    for t in range(GT + 1):
        out = rank[:, t * E:(t + 1) * E]
        for u in range(min(t + 1, GT)):
            ins = nc.tensor.matmul(out, m.tri[:] if u == t else m.ones[:], r.mask[b][:, u, :],
                                   start=(u == 0), stop=(u == min(t, GT - 1)), skip_group_check=True)
    ins.then_inc(r.ranked, 1)


def route_index(r, dve, chain, n, b, i, rank):
    m, nc = r.m, r.m.nc
    tiles = bass.ds(n * GT, GT)
    dve.wait_ge(r.ranked, n + 1)
    chain(nc.vector.tensor_tensor(r.slot[b][:], rank[:, 0:GT * E].rearrange("p (t e) -> p t e", t=GT),
                                  bc(m.base[:, 0:E].unsqueeze(1), P, GT, E), ALU.add))
    nc.vector.tensor_tensor(m.base[:, 0:E], m.base[:, 0:E], rank[:, GT * E:(GT + 1) * E], ALU.add)
    chain(nc.vector.tensor_tensor(r.prod[b][:], r.hot[b][:],
                                  bc(r.slot[b][:].unsqueeze(2), P, GT, TOPK, E), ALU.mult))
    hold(m, dve, r.scattered[b], r.sends * i)
    nc.vector.tensor_copy(r.row[b][:, :, :, P:].bitcast(U32), m.ids[:, tiles, :].unsqueeze(3))
    with nc.allow_low_precision(reason="whole numbers below 2^24"):
        nc.vector.tensor_reduce(r.index[b][:].rearrange("p (t k) -> p t k", t=GT), r.prod[b][:], AX_X, ALU.add
                                ).then_inc(r.indexed, 1)


def route_rows(r, b, nat, copied):
    for k in range(TOPK):
        ins = r.m.nc.scalar.activation(
            r.row[b][:, :, k, 0:P].rearrange("p (a c) w -> p a c w", a=2),
            nat[:, :, 0:2 * (P + E)].rearrange("p a (c w) -> p a c w", c=2)[:, :, :, 0:P], ACT.Copy)
    ins.then_inc(copied, 1)


def route_scatter(r, pool, n, b, rows_ready):
    m = r.m
    pool.wait_ge(r.indexed, n + 1)
    hold(m, pool, rows_ready, n + 1)
    for t in range(GT):
        for k in range(TOPK):
            c = t * TOPK + k
            pool.indirect_dma_start(
                out=m.xbuf, out_offset=bass.IndirectOffsetOnAxis(ap=r.index[b][:, c:c + 1], axis=0),
                in_=r.row[b][:, t, k, :], in_offset=None).then_inc(r.scattered[b], 16)


def tile_table(m, tag):
    nc = m.nc
    E1 = E + 1
    with ExitStack() as ctx:
        sb = lambda name, shape: m.sb(name + tag, shape, ctx=ctx)
        cnt, need, one, incl, excl, delta = (sb(x, [P, E1]) for x in ("cnt", "need", "one", "incl", "excl", "delta"))
        over = sb("over", [P, E1, MAXT])
        cmp = sb("cmp", [P, ETILES, E])
        expert = sb("expert", [P, ETILES])
        is_e = sb("is_e", [P, ETILES, E1])
        val, val2 = sb("val", [P, ETILES, E1]), sb("val2", [P, ETILES, E1])
        ex, total = sb("ex", [P, SEQS]), sb("total", [P, SEQS])
        link, ended, tabled, exped, tails, spare = m.sems(*(s + tag for s in (
            "tt_link", "ended", "tabled", "exped", "tails", "spare")))
        exps = m.const[:, C_EXP:C_EXP + E1]
        regs = m.const[:, C_REG:C_REG + E1]
        tl = m.const[:, C_TILE:C_TILE + ETILES]
        steps = m.const[:, C_STEP:C_STEP + MAXT]

        def fill(engine, experts):
            engine.wait_ge(ended, 1)
            for e in experts:
                at = engine.value_load(m.table[0:1, 2 * ETILES + e:2 * ETILES + e + 1],
                                       min_val=e * REGION, max_val=e * REGION + TOK)
                engine.dma_start(m.xbuf[bass.ds(at, SLOTS), :].rearrange("(a p) c -> p a c", p=P), m.tail[:, e]
                                 ).then_inc(tails, 16)

        with nc.Block() as block:
            @block.scalar
            def _(act):
                nc.scalar.activation(ex[:], m.diff[:], ACT.Exp).then_inc(exped, 1)
                fill(act, range(E // 2, E))

            @block.sync
            def _(sp):
                sp.dma_start(m.xbuf[E * REGION:].rearrange("(e a p) c -> p e a c", a=2, p=P), m.tail[:, E:]
                             ).then_inc(spare, 16)
                fill(sp, range(E // 2))
                sp.wait_ge(tails, 16 * E)
                sp.wait_ge(spare, 16)

            @block.vector
            def _(dve):
                v = nc.vector
                c = Chain(m, dve, link)
                v.tensor_copy(m.table[:, 2 * ETILES:], m.base[:, 0:E]).then_inc(ended, 1)
                v.memset(one[:], 1.0)
                c(v.tensor_tensor(cnt[:], m.base[:], regs, ALU.subtract))
                c(v.tensor_tensor(over[:], bc(cnt[:].unsqueeze(2), P, E1, MAXT),
                                  bc(steps.unsqueeze(1), P, E1, MAXT), ALU.is_gt))
                c(v.tensor_reduce(need[:], over[:], AX_X, ALU.add))
                c(v.tensor_tensor_scan(incl[:], one[:], need[:], 0.0, ALU.mult, ALU.add))
                c(v.tensor_tensor(excl[:], incl[:], need[:], ALU.subtract))
                c(v.scalar_tensor_tensor(out=delta[:], in0=excl[:], scalar=float(SLOTS), in1=regs,
                                         op0=ALU.mult, op1=ALU.subtract))
                c(v.tensor_tensor(cmp[:], bc(incl[:, 0:E].unsqueeze(1), P, ETILES, E),
                                  bc(tl.unsqueeze(2), P, ETILES, E), ALU.is_le))
                c(v.tensor_reduce(expert[:], cmp[:], AX_X, ALU.add))
                c(v.tensor_tensor(is_e[:], bc(expert[:].unsqueeze(2), P, ETILES, E1),
                                  bc(exps.unsqueeze(1), P, ETILES, E1), ALU.is_equal))
                c(v.scalar_tensor_tensor(out=val[:], in0=bc(tl.unsqueeze(2), P, ETILES, E1), scalar=float(SLOTS),
                                         in1=bc(delta[:].unsqueeze(1), P, ETILES, E1),
                                         op0=ALU.mult, op1=ALU.subtract))
                c(v.tensor_tensor(val2[:], val[:], is_e[:], ALU.mult))
                v.tensor_scalar(m.table[:, 0:ETILES], expert[:], float(E - 1), None, ALU.min)
                with nc.allow_low_precision(reason="whole numbers below 2^24"):
                    v.tensor_reduce(m.table[:, ETILES:2 * ETILES], val2[:], AX_X, ALU.add).then_inc(tabled, 1)
                dve.wait_ge(exped, 1)
                c(v.tensor_scalar(total[:], ex[:], 1.0, None, ALU.add))
                c(v.reciprocal(m.pw[:, :, 0], total[:]))
                v.tensor_tensor(m.pw[:, :, 1], m.pw[:, :, 0], ex[:], ALU.mult)
                dve.wait_ge(tabled, 1)
                c(v.tensor_copy(m.base[:], regs))



def layer0(m, loads):
    nc = m.nc
    xT, WT, IG, Ws1, Ws2, Ws3, first_ld, rest_ld, x_ld = loads
    MS = SHARED
    with ExitStack() as ctx:
        sb = lambda n, s, dt=F32: m.sb(n, s, dt, ctx)
        xm = [sb(f"xm{b}", [P, GT, P]) for b in range(2)]
        y = [sb(f"y{b}", [P, GW]) for b in range(2)]
        xf = [sb(f"xf{b}", [P, GW]) for b in range(2)]
        s = [sb(f"s{q}", [P, GW]) for q in range(2)]
        h = [[sb(f"h{b}{k}", [P, GW]) for k in range(3)] for b in range(2)]
        psY = m.ps("psY", [P, 512], ctx)
        psN = m.ps("psN", [P, 2, 512], ctx)
        psO = m.ps("psO", [P, 512], ctx)
        psA = m.ps("psA", [P, 2, 512], ctx)
        psB = m.ps("psB", [P, 2, 512], ctx)
        rank = psO[:, 0:(GT + 1) * E]
        r = Router(m, ctx, "0", None)
        (scaled, projected, biased, clipped, nat, nat_copied, up_a, up_b, silu, gated, down,
         added) = m.sems("scaled", "projected", "biased", "clipped", "nat0", "nat_copied0",
                         "up_a", "up_b", "silu", "gated", "down", "added")
        with nc.Block() as block:
            @block.gpsimd
            def _(pool):
                for n, b, _ in rounds(pool, GROUPS, 2):
                    route_scatter(r, pool, n, b, nat_copied)
                for b in range(2):
                    pool.wait_ge(r.scattered[b], r.sends * GROUPS // 2)

            @block.vector
            def _(dve):
                chain = Chain(m, dve, r.link, ROUTE_LINKS)

                def scale(n, b):
                    wait(dve, projected, n - 1)
                    nc.vector.tensor_tensor(
                        xm[b][:], xT[:, bass.ds(n * GW, GW)].rearrange("p (s t) -> p s t", s=GT),
                        bc(m.styles[:, bass.ds(n * GT, GT)].unsqueeze(2), P, GT, P), ALU.mult).then_inc(scaled, 1)

                def clip(n, b):
                    dve.wait_ge(biased, n + 1)
                    wait(dve, down, n - 1)
                    nc.vector.tensor_scalar(xf[b][:], y[b][:], CLAMP, -CLAMP, ALU.min, ALU.max).then_inc(clipped, 1)

                def add(n):
                    mine = bass.ds(n * GT, GT)
                    dve.wait_ge(down, n + 1)
                    nc.vector.tensor_tensor(m.X[:, mine, :], m.X[:, mine, :], psO[:].rearrange("p (s c) -> p s c", s=GT),
                                            ALU.add).then_inc(added, 1)

                def gate(n, b, k):
                    c, q = 3 * n + k, (3 * b + k) % 2
                    dve.wait_ge(up_b, c + 1)
                    dve.wait_ge(silu, c + 1)
                    wait(dve, down, n - 1)
                    nc.vector.tensor_tensor(h[b][k][0:MS[k], :], psB[0:MS[k], q, :], s[q][0:MS[k], :],
                                            ALU.mult).then_inc(gated, 1)

                dve.wait_ge(first_ld, FIRST_LOADS)
                scale(0, 0)
                scale(1, 1)
                clip(0, 0)
                for n, b, i in rounds(dve, GROUPS, 2, head=2, tail=2):
                    route_choose(r, dve, chain, n, b, psN, nat)
                    if not first(n):
                        add(n - 1)
                    gate(n, b, 0)
                    gate(n, b, 1)
                    route_index(r, dve, chain, n, b, i, rank)
                    if not is_last(n, GROUPS):
                        clip(n + 1, 1 - b)
                    gate(n, b, 2)
                    if first(n):
                        dve.wait_ge(rest_ld, 16)
                        dve.wait_ge(x_ld, 16)
                    if not late(n):
                        scale(n + 2, b)
                add(GROUPS - 1)

            @block.scalar
            def _(act):
                def bias(n, b):
                    act.wait_ge(projected, n + 1)
                    wait(act, clipped, n - 1)
                    for t in range(GT):
                        ins = nc.scalar.activation(y[b][:, t * P:(t + 1) * P], psY[:, t * P:(t + 1) * P], ACT.Identity,
                                                   bias=m.vec[:, V_BIAS:V_BIAS + 1],
                                                   scale=m.dcoef[:, bass.ds(n * GT + t, 1)])
                    ins.then_inc(biased, 1)

                act.wait_ge(first_ld, FIRST_LOADS)
                bias(0, 0)
                for n, b, i in rounds(act, GROUPS, 2, head=2, tail=2):
                    act.wait_ge(r.got, n + 1)
                    wait(act, r.scattered[b], r.sends * i)
                    route_rows(r, b, psN, nat_copied)
                    for k in range(3):
                        c, q = 3 * n + k, (3 * b + k) % 2
                        act.wait_ge(up_a, c + 1)
                        wait(act, gated, c - 1)
                        nc.scalar.activation(s[q][0:MS[k], :], psA[0:MS[k], q, :], ACT.Silu).then_inc(silu, 1)
                        if k == 1 and not is_last(n, GROUPS):
                            bias(n + 1, 1 - b)

            @block.tensor
            def _(pe):
                def project(n, b):
                    pe.wait_ge(scaled, n + 1)
                    wait(pe, biased, n)
                    nc.tensor.matmul(psY[:], WT[:], xm[b][:].rearrange("p s t -> p (s t)"),
                                     start=True, stop=True).then_inc(projected, 1)

                def up(n, b, k):
                    c, q = 3 * n + k, (3 * b + k) % 2
                    wait(pe, silu, c - 1)
                    nc.tensor.matmul(psA[0:MS[k], q, :], Ws1[:, k * P:k * P + MS[k]], xf[b][:],
                                     start=True, stop=True).then_inc(up_a, 1)
                    wait(pe, gated, c - 1)
                    nc.tensor.matmul(psB[0:MS[k], q, :], Ws2[:, k * P:k * P + MS[k]], xf[b][:],
                                     start=True, stop=True).then_inc(up_b, 1)

                def natural(n, b):
                    pe.wait_ge(clipped, n + 1)
                    wait(pe, nat_copied, n)
                    for t in range(GT):
                        w = (t % 2) * (P + E)
                        ins = nc.tensor.matmul(psN[:, t // 2, w:w + P + E], xf[b][:, t * P:(t + 1) * P], IG[:],
                                               start=True, stop=True, skip_group_check=True)
                    ins.then_inc(nat, 1)

                pe.wait_ge(first_ld, FIRST_LOADS)
                project(0, 0)
                natural(0, 0)
                up(0, 0, 0)
                for n, b, _ in rounds(pe, GROUPS, 2, head=2, tail=2):
                    if not is_last(n, GROUPS):
                        project(n + 1, 1 - b)
                    up(n, b, 1)
                    wait(pe, added, n)
                    route_rank(r, pe, n, b, rank)
                    up(n, b, 2)
                    if not is_last(n, GROUPS):
                        natural(n + 1, 1 - b)
                        up(n + 1, 1 - b, 0)
                    pe.wait_ge(r.indexed, n + 1)
                    pe.wait_ge(gated, 3 * n + 3)
                    for t in range(GT):
                        for k in range(3):
                            ins = nc.tensor.matmul(psO[:, t * P:(t + 1) * P], h[b][k][0:MS[k], t * P:(t + 1) * P],
                                                   Ws3[0:MS[k], k, :], start=(k == 0), stop=(k == 2),
                                                   skip_group_check=True)
                    ins.then_inc(down, 1)



EB = 8


def nearly(n):
    return isinstance(n, int) and n >= ETILES - 2


def turn_rows(m, pe, n, b, i, ld, xs, psT, copied, turned):
    q = b % 2
    pe.wait_ge(ld[b], 48 * (i + 1))
    wait(pe, copied, n - 1)
    for a in range(2):
        ins = m.nc.tensor.transpose(psT[:, q, a * P:(a + 1) * P], xs[b][:, a, 0:P], m.ident)
    ins.then_inc(turned, 1)


def copy_rows(m, dve, n, b, i, psT, xsT, xs, to, turned, used, sent, copied):
    q = b % 2
    dve.wait_ge(turned, n + 1)
    hold(m, dve, sent[b], 32 * i)
    m.nc.vector.tensor_copy(to[b][:].unsqueeze(2), xs[b][:, :, P:].bitcast(U32))
    wait(dve, used, n - 1)
    m.nc.vector.tensor_copy(xsT[q][:], psT[:, q, 0:SLOTS]).then_inc(copied, 1)


def send_rows(m, pool, n, b, ready, out, to, sent):
    hold(m, pool, ready, n + 1)
    for a in range(2):
        pool.indirect_dma_start(
            out=m.ybuf, out_offset=bass.IndirectOffsetOnAxis(ap=to[b][:, a:a + 1], axis=0),
            in_=out[b][:, a, :], in_offset=None).then_inc(sent[b], 16)


def experts0(m, d):
    nc = m.nc
    with ExitStack() as ctx:
        sb = lambda n, s, dt=F32: m.sb(n, s, dt, ctx)
        w12 = [sb(f"w12_{b}", [P, 4, HALF]) for b in range(EB)]
        w3 = [sb(f"w3_{b}", [HALF, 2, P]) for b in range(EB)]
        xs = [sb(f"xs{b}", [P, 2, ROW]) for b in range(EB)]
        out = [sb(f"eo{b}", [P, 2, P]) for b in range(EB)]
        to = [sb(f"to{b}", [P, 2], U32) for b in range(EB)]
        xsT = [sb(f"xsT{q}", [P, SLOTS]) for q in range(2)]
        s = [sb(f"es{q}", [HALF, 2, SLOTS]) for q in range(2)]
        h = [sb(f"eh{q}", [HALF, 2, SLOTS]) for q in range(2)]
        psT = m.ps("psT", [P, 2, 512], ctx)
        psA = m.ps("psA0", [P, 2, 512], ctx)
        psB = m.ps("psB0", [P, 2, 512], ctx)
        psO = m.ps("psO0", [P, 2, 512], ctx)
        m.ld = ld = [m.sem(f"e_ld{b}") for b in range(EB)]
        m.st = st = [m.sem(f"e_st{b}") for b in range(EB)]
        (turned, copied, up_a, up_b, silu, gated, down, evac) = m.sems(
            "e0_turned", "e0_copied", "e0_up_a", "e0_up_b", "e0_silu", "e0_gated", "e0_down", "e0_evac")
        with nc.Block() as block:
            @block.sync
            def _(sp):
                for n, b, i in rounds(sp, ETILES, EB, head=EB):
                    e = sp.value_load(m.table[0:1, bass.ds(n, 1)], min_val=0, max_val=E - 1)
                    row = sp.value_load(m.table[0:1, bass.ds(n + ETILES, 1)], min_val=0, max_val=E * REGION + (E - 1) * SLOTS)
                    hold(m, sp, down, n - EB + 1)
                    hold(m, sp, copied, n - EB + 1)
                    sp.dma_start(xs[b][:], m.xbuf[bass.ds(row, SLOTS), :].rearrange("(a p) c -> p a c", p=P)
                                 ).then_inc(ld[b], 16)
                    sp.dma_start(w12[b][:], d["W12"][bass.ds(e, 1)].rearrange("e p (a h) -> (e p) a h", a=4)
                                 ).then_inc(ld[b], 16)
                    sp.dma_start(w3[b][:], d["W3"][bass.ds(e, 1)].rearrange("e p (a h) -> (e p) a h", a=2)
                                 ).then_inc(ld[b], 16)

            @block.tensor
            def _(pe):
                def up(n, b):
                    q = b % 2
                    pe.wait_ge(copied, n + 1)
                    wait(pe, silu, n - 1)
                    for a in range(2):
                        ins = nc.tensor.matmul(psA[0:HALF, q, a * SLOTS:(a + 1) * SLOTS], w12[b][:, a, :], xsT[q][:],
                                               start=True, stop=True, skip_group_check=True)
                    ins.then_inc(up_a, 1)
                    wait(pe, gated, n - 1)
                    for a in range(2):
                        ins = nc.tensor.matmul(psB[0:HALF, q, a * SLOTS:(a + 1) * SLOTS], w12[b][:, 2 + a, :], xsT[q][:],
                                               start=True, stop=True, skip_group_check=True)
                    ins.then_inc(up_b, 1)

                turn_rows(m, pe, 0, 0, 0, ld, xs, psT, copied, turned)
                turn_rows(m, pe, 1, 1, 0, ld, xs, psT, copied, turned)
                up(0, 0)
                for n, b, i in rounds(pe, ETILES, EB, head=EB, tail=EB):
                    if not nearly(n):
                        turn_rows(m, pe, n + 2, (b + 2) % EB, i + (b + 2) // EB, ld, xs, psT, copied, turned)
                    if not is_last(n, ETILES):
                        up(n + 1, (b + 1) % EB)
                    q = b % 2
                    pe.wait_ge(gated, n + 1)
                    wait(pe, evac, n - 1)
                    for a in range(2):
                        for k in range(2):
                            ins = nc.tensor.matmul(psO[:, q, a * P:(a + 1) * P], h[q][:, k, a * P:(a + 1) * P],
                                                   w3[b][:, k, :], start=(k == 0), stop=(k == 1), skip_group_check=True)
                    ins.then_inc(down, 1)

            @block.vector
            def _(dve):
                copy_rows(m, dve, 0, 0, 0, psT, xsT, xs, to, turned, up_b, st, copied)
                copy_rows(m, dve, 1, 1, 0, psT, xsT, xs, to, turned, up_b, st, copied)
                for n, b, i in rounds(dve, ETILES, EB, head=EB, tail=EB):
                    q = b % 2
                    dve.wait_ge(up_b, n + 1)
                    dve.wait_ge(silu, n + 1)
                    wait(dve, down, n - 1)
                    nc.vector.tensor_tensor(h[q][:], psB[0:HALF, q, :].rearrange("p (a t) -> p a t", a=2), s[q][:],
                                            ALU.mult).then_inc(gated, 1)
                    if not nearly(n):
                        copy_rows(m, dve, n + 2, (b + 2) % EB, i + (b + 2) // EB, psT, xsT, xs, to, turned, up_b, st,
                                  copied)

            @block.scalar
            def _(act):
                def store(n, b, i):
                    act.wait_ge(down, n + 1)
                    wait(act, st[b], 32 * i)
                    nc.scalar.activation(out[b][:], psO[:, b % 2, 0:SLOTS].rearrange("p (a c) -> p a c", a=2), ACT.Copy
                                         ).then_inc(evac, 1)

                for n, b, i in rounds(act, ETILES, EB, head=EB):
                    act.wait_ge(up_a, n + 1)
                    wait(act, gated, n - 1)
                    nc.scalar.activation(s[b % 2][:], psA[0:HALF, b % 2, :].rearrange("p (a t) -> p a t", a=2),
                                         ACT.Silu).then_inc(silu, 1)
                    if not first(n):
                        store(n - 1, (b - 1) % EB, i if b else i - 1)
                store(ETILES - 1, EB - 1, ETILES // EB - 1)

            @block.gpsimd
            def _(pool):
                for n, b, i in rounds(pool, ETILES, EB, head=EB):
                    send_rows(m, pool, n, b, evac, out, to, st)
                for b in range(EB):
                    pool.wait_ge(st[b], 32 * (ETILES // EB))



def fetch_rows(m, eng, n, b, rows, came, free, free_at):
    hold(m, eng, free, free_at)
    eng.dma_start(rows[b][:], m.ybuf[bass.ds(n * GT * P * TOPK, GT * P * TOPK), :].rearrange(
        "(t p k) c -> p t k c", p=P, k=TOPK)).then_inc(came[b], 16)


def finish(m, d, out):
    nc = m.nc
    with ExitStack() as ctx:
        rows = [m.sb(f"fr{b}", [P, GT, TOPK, P], F32, ctx) for b in range(2)]
        part = [m.sb(f"fp{b}", [P, GT, P], F32, ctx) for b in range(2)]
        res = [m.sb(f"fo{b}", [P, GT, P], F32, ctx) for b in range(2)]
        halfway, summed = m.sems("f_halfway", "f_summed")
        came = m.sems("f_came0", "f_came1")
        stored = m.sems("f_stored0", "f_stored1")
        with nc.Block() as block:
            @block.sync
            def _(sp):
                for n, b, i in rounds(sp, GROUPS, 2, head=2):
                    fetch_rows(m, sp, n, b, rows, came, summed, n - 1)

            @block.vector
            def _(dve):
                for n, b, i in rounds(dve, GROUPS, 2, head=2):
                    dve.wait_ge(came[b], 16 * (i + 1))
                    weighted(m, n, part[b], rows[b], 0, m.X[:, bass.ds(n * GT, GT), :]).then_inc(halfway, 1)
                    dve.wait_ge(halfway, n + 1)
                    wait(dve, stored[b], 16 * i)
                    weighted(m, n, res[b], rows[b], 1, part[b][:]).then_inc(summed, 1)

            @block.scalar
            def _(act):
                for n, b, i in rounds(act, GROUPS, 2, head=2):
                    hold(m, act, summed, n + 1)
                    act.dma_start(out[bass.ds(n * GT, GT)].rearrange("s p c -> p s c"), res[b][:]).then_inc(stored[b], 16)
                for b in range(2):
                    act.wait_ge(stored[b], 16 * (GROUPS // 2))



PRE_LINKS = 3


def pre_attention(m, d):
    nc = m.nc
    with ExitStack() as ctx:
        sb = lambda n, s, dt=F32: m.sb(n, s, dt, ctx)
        two = lambda n, s, dt=F32: [m.sb(f"{n}{b}", s, dt, ctx) for b in range(2)]
        rows = two("gr", [P, GT, TOPK, P])
        part = two("part", [P, GT, P])
        x1, x2 = two("x1_", [P, GT, P]), two("x2_", [P, GT, P])
        gbu = two("gbu", [DOWN, GT, 2 * P])
        wd, wdt = two("wd", [P, GT, DOWN]), two("wdt", [P, GT, DOWN])
        wu, wut = two("wu", [P, GT, P]), two("wut", [DOWN, GT, P])
        x1T = two("x1T", [P, GW])
        aT = two("aT", [P, GW])
        stats = two("stats", [P, GT, 6])
        mv = two("mv", [P, GT, 2])
        var, std, rstd = two("var", [P, GT]), two("std", [P, GT]), two("rstd", [P, GT])
        norm = two("norm", [P, GT, P])
        hT = two("hT", [P, GW])
        qk = two("qk", [P, 4, GW], F32R)
        psX, psD, psU = m.ps("psX", [P, 512], ctx), m.ps("psD", [P, 512], ctx), m.ps("psU", [P, 512], ctx)
        psH, psV = m.ps("psH", [P, 512], ctx), m.ps("psV", [P, 512], ctx)
        psQK = m.ps("psQK", [P, 2, 512], ctx)
        (cleared, blend1, blended, mod1, modded, turned, x1T_done, downed, relu, upped, x2_done,
         biased, link, sqrted, var_done, normed, turned2, hT_done, q_done, k_done, v_done, high, low, v_kept) = m.sems(
            "p_cleared", "p_blend1", "p_blended", "p_mod1", "p_modded", "p_turned", "p_x1T",
            "p_downed", "p_relu", "p_upped", "p_x2", "p_biased", "p_link", "p_sqrted", "p_var", "p_normed", "p_turned2",
            "p_hT", "p_q", "p_k", "p_v", "p_high", "p_low", "p_v_kept")
        came = m.sems("p_came0", "p_came1")
        gbu_in = m.sems("p_gbu0", "p_gbu1")
        qk_out = m.sems("p_qk_out0", "p_qk_out1")
        qk_view = m.qk_dram.rearrange("a p t -> p a t")
        gb_up = m.gb_dram[:, 2 * DOWN:]
        with nc.Block() as block:
            @block.sync
            def _(sp):
                def modulation(n, b):
                    hold(m, sp, modded, n - 1)
                    sp.dma_start(gbu[b][:], gb_up[bass.ds(n * GT, GT), :].unsqueeze(0).to_broadcast(
                        [DOWN, GT, 2 * P])).then_inc(gbu_in[b], 16)

                for n in range(3):
                    modulation(n, n % 2)
                    fetch_rows(m, sp, n, n % 2, rows, came, blended, n - 1)
                for n, b, i in rounds(sp, GROUPS, 2, head=2, tail=4):
                    if not late(n, 3):
                        modulation(n + 3, 1 - b)
                        fetch_rows(m, sp, n + 3, 1 - b, rows, came, blended, n + 2)
                    sp.wait_ge(high, 2 * (n + 1))
                    hold(m, sp, low, 2 * (n + 1))
                    sp.dma_start(qk_view[:, :, bass.ds(n * GW, GW)], qk[b][:].bitcast(F32)).then_inc(qk_out[b], 16)
                for b in range(2):
                    sp.wait_ge(qk_out[b], 16 * GROUPS // 2)

            @block.gpsimd
            def _(pool):
                def keep(n, b):
                    mine = bass.ds(n * GT, GT)
                    pool.wait_ge(x2_done, n + 1)
                    nc.gpsimd.tensor_copy(m.X[:, mine, :], x1[b][:])
                    nc.gpsimd.tensor_tensor(m.X3[:, mine, :], x2[b][:], bc(m.rows[:, R_BO:R_BO + P].unsqueeze(1), P, GT, P),
                                            ALU.add).then_inc(biased, 1)

                for b in range(2):
                    nc.gpsimd.memset(aT[b][:], 0.0)
                    nc.gpsimd.memset(wu[b][:], 0.0).then_inc(cleared, 1)
                for n, b, i in rounds(pool, GROUPS, 2, head=2):
                    keep(n, b)

            @block.vector
            def _(dve):
                chain = Chain(m, dve, link, PRE_LINKS)

                def blend(n, b, i):
                    dve.wait_ge(came[b], 16 * (i + 1))
                    wait(dve, biased, n - 1)
                    weighted(m, n, part[b], rows[b], 0, m.X[:, bass.ds(n * GT, GT), :]).then_inc(blend1, 1)
                    dve.wait_ge(blend1, n + 1)
                    wait(dve, turned, n - 1)
                    weighted(m, n, x1[b], rows[b], 1, part[b][:]).then_inc(blended, 1)

                def modulate(n, b, i):
                    gd = m.gbD[:, bass.ds(n * GT, GT), :]
                    dve.wait_ge(gbu_in[b], 16 * (i + 1))
                    wait(dve, upped, n - 1)
                    nc.vector.tensor_tensor(wdt[b][:], bc(m.dproj[:].unsqueeze(1), P, GT, DOWN), gd[:, :, 0:DOWN], ALU.mult)
                    nc.vector.tensor_tensor(wut[b][:], bc(m.uproj[:].unsqueeze(1), DOWN, GT, P), gbu[b][:, :, 0:P],
                                            ALU.mult).then_inc(mod1, 1)
                    dve.wait_ge(mod1, n + 1)
                    nc.vector.tensor_tensor(wd[b][:], wdt[b][:], gd[:, :, DOWN:], ALU.add)
                    nc.vector.tensor_tensor(wu[b][0:DOWN], wut[b][:], gbu[b][:, :, P:], ALU.add).then_inc(modded, 1)

                dve.wait_ge(m.late_ld, LATE_LOADS)
                dve.wait_ge(m.gb_in, 16)
                dve.wait_ge(cleared, 2)
                for n in range(2):
                    modulate(n, n, 0)
                    blend(n, n, 0)
                for n, b, i in rounds(dve, GROUPS, 2, head=2, tail=2):
                    chain.begin(n)
                    mine = bass.ds(n * GT, GT)
                    dve.wait_ge(upped, n + 1)
                    wait(dve, biased, n - 1)
                    nc.vector.tensor_tensor(x2[b][:], psU[:].rearrange("p (t c) -> p t c", t=GT), x1[b][:],
                                            ALU.add).then_inc(x2_done, 1)
                    dve.wait_ge(x2_done, n + 1)
                    layernorm(m, dve, chain, n, lambda t: x2[b][:, t, :], stats[b], mv[b], var[b], var_done, std[b], sqrted, rstd[b], norm[b],
                              turned2, normed)
                    if not late(n):
                        modulate(n + 2, b, i + 1)
                        blend(n + 2, b, i + 1)
                    for w in range(2):
                        dve.wait_ge(high, 2 * n + w + 1)
                        nc.vector.scalar_tensor_tensor(
                            out=qk[b][:, 2 * w + 1, :], in0=psQK[:, w, :], scalar=m.vec[:, V_BQ + w:V_BQ + w + 1],
                            in1=qk[b][:, 2 * w, :].bitcast(F32), op0=ALU.add, op1=ALU.subtract).then_inc(low, 1)
                    dve.wait_ge(v_done, n + 1)
                    nc.vector.tensor_tensor(m.V[:, mine, :], psV[:].rearrange("p (t c) -> p t c", t=GT),
                                            bc(m.rows[:, R_BV:R_BV + P].unsqueeze(1), P, GT, P), ALU.add
                                            ).then_inc(v_kept, 1)

            @block.scalar
            def _(act):
                def early(n, b):
                    act.wait_ge(turned, n + 1)
                    wait(act, downed, n - 1)
                    nc.scalar.activation(x1T[b][:], psX[:], ACT.Copy).then_inc(x1T_done, 1)
                    act.wait_ge(downed, n + 1)
                    wait(act, upped, n - 1)
                    nc.scalar.activation(aT[b][0:DOWN, :], psD[0:DOWN, :], ACT.Relu).then_inc(relu, 1)

                act.wait_ge(cleared, 2)
                early(0, 0)
                for n, b, i in rounds(act, GROUPS, 2, head=2, tail=2):
                    if not is_last(n, GROUPS):
                        early(n + 1, 1 - b)
                    act.wait_ge(var_done, n + 1)
                    nc.scalar.activation(std[b][:], var[b][:], ACT.Sqrt).then_inc(sqrted, 1)
                    act.wait_ge(turned2, n + 1)
                    wait(act, v_done, n - 1)
                    nc.scalar.activation(hT[b][:], psH[:], ACT.Identity, bias=m.vec[:, V_LN1B:V_LN1B + 1],
                                         scale=m.vec[:, V_LN1G:V_LN1G + 1]).then_inc(hT_done, 1)
                    wait(act, qk_out[b], 16 * i)
                    for w, ready in ((0, q_done), (1, k_done)):
                        act.wait_ge(ready, n + 1)
                        nc.scalar.activation(qk[b][:, 2 * w, :], psQK[:, w, :], ACT.Identity,
                                             bias=m.vec[:, V_BQ + w:V_BQ + w + 1]).then_inc(high, 1)

            @block.tensor
            def _(pe):
                def early(n, b):
                    pe.wait_ge(blended, n + 1)
                    wait(pe, x1T_done, n)
                    for t in range(GT):
                        ins = nc.tensor.transpose(psX[:, t * P:(t + 1) * P], x1[b][:, t, :], m.ident)
                    ins.then_inc(turned, 1)
                    pe.wait_ge(x1T_done, n + 1)
                    pe.wait_ge(modded, n + 1)
                    wait(pe, relu, n)
                    for t in range(GT):
                        ins = nc.tensor.matmul(psD[0:DOWN, t * P:(t + 1) * P], wd[b][:, t, :], x1T[b][:, t * P:(t + 1) * P],
                                               start=True, stop=True, skip_group_check=True)
                    ins.then_inc(downed, 1)
                    pe.wait_ge(relu, n + 1)
                    wait(pe, x2_done, n)
                    for t in range(GT):
                        ins = nc.tensor.matmul(psU[:, t * P:(t + 1) * P], aT[b][:, t * P:(t + 1) * P], wu[b][:, t, :],
                                               start=True, stop=True, skip_group_check=True)
                    ins.then_inc(upped, 1)

                pe.wait_ge(m.late_ld, LATE_LOADS)
                early(0, 0)
                for n, b, i in rounds(pe, GROUPS, 2, head=2, tail=2):
                    if not is_last(n, GROUPS):
                        early(n + 1, 1 - b)
                    pe.wait_ge(normed, n + 1)
                    wait(pe, hT_done, n)
                    for t in range(GT):
                        ins = nc.tensor.transpose(psH[:, t * P:(t + 1) * P], norm[b][:, t, :], m.ident)
                    ins.then_inc(turned2, 1)
                    pe.wait_ge(hT_done, n + 1)
                    for w, ready in ((0, q_done), (1, k_done)):
                        wait(pe, low, 2 * n - 1 + w)
                        nc.tensor.matmul(psQK[:, w, :], m.wqkv[:, w * P:(w + 1) * P], hT[b][:], start=True, stop=True
                                         ).then_inc(ready, 1)
                    wait(pe, v_kept, n)
                    for t in range(GT):
                        ins = nc.tensor.matmul(psV[:, t * P:(t + 1) * P], hT[b][:, t * P:(t + 1) * P], m.wqkv[:, 2 * P:],
                                               start=True, stop=True, skip_group_check=True)
                    ins.then_inc(v_done, 1)


def weighted(m, n, out, rows, k, plus):
    for t in range(GT):
        ins = m.nc.vector.scalar_tensor_tensor(
            out=out[:, t, :], in0=rows[:, t, k, :],
            scalar=m.pw[:, bass.ds(n * GT + t, 1), k:k + 1].rearrange("p a k -> p (a k)"),
            in1=plus[:, t, :], op0=ALU.mult, op1=ALU.add)
    return ins


def layernorm(m, dve, chain, n, at, stats, mv, var, var_done, std, sqrted, rstd, norm, used, normed):
    nc = m.nc
    for t in range(GT):
        ins = nc.vector.bn_stats(stats[:, t, :], at(t))
    chain(ins)
    for t in range(GT):
        ins = nc.vector.bn_aggr(mv[:, t, :], stats[:, t, :])
    chain(ins)
    nc.vector.tensor_scalar(var[:], mv[:, :, 1], EPS, None, ALU.add).then_inc(var_done, 1)
    dve.wait_ge(sqrted, n + 1)
    chain(nc.vector.reciprocal(rstd[:], std[:]))
    wait(dve, used, n - 1)
    for t in range(GT):
        ins = nc.vector.tensor_scalar(norm[:, t, :], at(t), mv[:, t, 0:1], rstd[:, t:t + 1], ALU.subtract, ALU.mult)
    ins.then_inc(normed, 1)



PAIR = 2 * P
KM_POOL = 1


def soon(s, behind=2):
    return isinstance(s, int) and s < behind


def attention(m, d):
    nc = m.nc
    with ExitStack() as ctx:
        sb = lambda n, s, dt=F32: m.sb(n, s, dt, ctx)
        two = lambda n, s, dt=F32: [m.sb(f"{n}{b}", s, dt, ctx) for b in range(2)]
        selr = sb("selr", [P, HG, P], F32R)
        qp = two("qp", [96, HG, PAIR], F32R)
        kp = two("kp", [96, HG, PAIR], F32R)
        qm = two("qm", [96, HG, 4, P], F32R)
        km = two("km", [96, HG, 4, P], F32R)
        vb = two("vb", [P, HEADS, 32])
        mneg = two("mneg", [P, HG, 4])
        xm = two("xmx", [P, 4, P])
        mxT = two("mxT", [P, 4 * P], F32R)
        prob = two("prob", [P, HG, 4 * P])
        rec = two("rec", [P, P])
        oT = two("oT", [P, P])
        ps1, ps2 = m.ps("ps1", [P, 2, 512], ctx), m.ps("ps2", [P, 2, 512], ctx)
        psM, psW = m.ps("psM", [P, 512], ctx), m.ps("psW", [P, 512], ctx)
        psO = m.ps("psAO", [P, 2, 512], ctx)
        (cleared, made, qm_done, km_pool, km_act, vb_done, scored, maxed, link, parted, turned, mxT_done, shifted,
         exped, mixed, divided, projected, kept) = m.sems(
            "a_cleared", "a_made", "a_qm", "a_km_pool", "a_km_act", "a_vb", "a_scored", "a_maxed", "a_link", "a_parted",
            "a_turned", "a_mxT", "a_shifted", "a_exped", "a_mixed", "a_divided", "a_projected", "a_kept")
        pair_in = m.sems("a_pair0", "a_pair1")
        mask = lambda j: m.const[0:96, C_MASK + j:C_MASK + j + 1]
        tok = lambda s4: slice((s4 % 2) * P, (s4 % 2 + 1) * P)
        PAIRS = SEQS // 2

        with nc.Block() as block:
            @block.sync
            def _(sp):
                for n, b, i in rounds(sp, PAIRS, 2, head=2):
                    hold(m, sp, shifted, 8 * (n - 1))
                    hold(m, sp, qm_done, 2 * (n - 1))
                    hold(m, sp, km_pool, 2 * (n - 1))
                    hold(m, sp, km_act, 2 * (n - 1))
                    for side, parts in ((qp[b], (0, 1, 0)), (kp[b], (2, 2, 3))):
                        for r, a in enumerate(parts):
                            sp.dma_start(side[32 * r:32 * r + 32].bitcast(F32),
                                         m.qk_dram[a, :, bass.ds(n * PAIR, PAIR)].rearrange("(g r) t -> r g t", g=HG)
                                         ).then_inc(pair_in[b], 16)

            @block.gpsimd
            def _(pool):
                for b in range(2):
                    nc.gpsimd.memset(vb[b][:], 0.0)
                    nc.gpsimd.memset(xm[b][:], 0.0).then_inc(cleared, 1)
                pool.wait_ge(cleared, 2)
                def mask_k(s, u, i):
                    p, b = u % 2, u // 2
                    if p == 0:
                        pool.wait_ge(pair_in[b], 96 * (i + 1))
                    hold(m, pool, scored, 4 * (s - 1))
                    for j in range(KM_POOL):
                        ins = nc.gpsimd.tensor_scalar(km[p][:, :, j, :], kp[b][:, :, tok(u)].bitcast(F32), mask(j), None,
                                                      ALU.mult)
                    ins.then_inc(km_pool, 1)

                def spread_v(s, p):
                    wait(pool, mixed, s - 1)
                    for g in range(HG):
                        v = vb[p][:, 4 * g:4 * g + 4, :]
                        diag = bass.AP(v.tensor, v.offset, [list(v.ap[0]), [40, 4], [1, 8]])
                        ins = nc.gpsimd.tensor_copy(diag, m.V[:, bass.ds(s, 1), 32 * g:32 * g + 32].rearrange(
                            "p a (j e) -> p (a j) e", j=4))
                    ins.then_inc(vb_done, 1)

                for s, u, i in rounds(pool, SEQS, 4, head=4):
                    mask_k(s, u, i)
                    if not first(s):
                        spread_v(s - 1, (u - 1) % 2)
                spread_v(SEQS - 1, 1)

            @block.vector
            def _(dve):
                def maxima(s, u, i):
                    p = u % 2
                    for g in range(HG):
                        dve.wait_ge(scored, 4 * s + g + 1)
                        ins = nc.vector.tensor_reduce(mneg[p][:, g, :], ps1[:, g % 2, :].rearrange("p (j k) -> p j k", j=4),
                                                      AX_X, ALU.max, negate=True)
                        ins.then_inc(maxed, 1)
                    dve.wait_ge(maxed, 4 * s + 4)
                    wait(dve, turned, s - 1)
                    x = xm[p][:]
                    hi, lo = (bass.AP(x.tensor, x.offset + w, [list(x.ap[0]), [32, 4], [130, 4]]) for w in range(2))
                    nc.vector.tensor_copy(hi.bitcast(F32R), mneg[p][:]).then_inc(link, 1)
                    dve.wait_ge(link, s + 1)
                    nc.vector.tensor_tensor(lo, mneg[p][:], hi, ALU.subtract).then_inc(parted, 1)

                def mask_q(s, u, i):
                    p, b = u % 2, u // 2
                    if p == 0:
                        dve.wait_ge(pair_in[b], 96 * (i + 1))
                    wait(dve, shifted, 4 * (s - 1))
                    for j in range(4):
                        ins = nc.vector.tensor_scalar(qm[p][:, :, j, :], qp[b][:, :, tok(u)].bitcast(F32), mask(j), None,
                                                      ALU.mult)
                    ins.then_inc(qm_done, 1)

                def divide(s, u):
                    p = u % 2
                    dve.wait_ge(mixed, s + 1)
                    nc.vector.reciprocal(rec[p][:], psO[:, p, P:2 * P]).then_inc(made, 1)
                    dve.wait_ge(made, s + 1)
                    wait(dve, projected, s - 1)
                    nc.vector.tensor_tensor(oT[p][:], psO[:, p, 0:P], rec[p][:], ALU.mult).then_inc(divided, 1)

                def keep(s, u):
                    dve.wait_ge(projected, s + 1)
                    x3 = m.X3[:, bass.ds(s, 1), :].rearrange("p a c -> p (a c)")
                    nc.vector.tensor_tensor(x3, psW[:, 0:P], x3, ALU.add).then_inc(kept, 1)

                dve.wait_ge(cleared, 2)
                for g in range(HG):
                    ins = nc.vector.tensor_copy(selr[:, g, :], bc(m.const[:, C_SEL + g:C_SEL + g + 1], P, P))
                mask_q(0, 0, 0)
                maxima(0, 0, 0)
                for s, u, i in rounds(dve, SEQS, 4, head=4, tail=4):
                    nxt = (s + 1, (u + 1) % 4, i + (u + 1) // 4)
                    if not is_last(s, SEQS):
                        maxima(*nxt)
                        mask_q(*nxt)
                    if not soon(s):
                        divide(s - 2, u)
                    if not soon(s, 3):
                        keep(s - 3, u)
                divide(SEQS - 2, 0)
                divide(SEQS - 1, 1)
                for s in range(SEQS - 3, SEQS):
                    keep(s, s)

            @block.scalar
            def _(act):
                def copy_max(s, u):
                    act.wait_ge(turned, s + 1)
                    wait(act, shifted, 4 * (s - 1))
                    nc.scalar.activation(mxT[u % 2][:], psM[:], ACT.Copy).then_inc(mxT_done, 1)

                def mask_k(s, u, i):
                    p, b = u % 2, u // 2
                    if p == 0:
                        act.wait_ge(pair_in[b], 96 * (i + 1))
                    wait(act, scored, 4 * (s - 1))
                    for j in range(KM_POOL, 4):
                        ins = nc.scalar.activation(km[p][:, :, j, :], kp[b][:, :, tok(u)].bitcast(F32), ACT.Copy,
                                                   scale=mask(j))
                    ins.then_inc(km_act, 1)

                mask_k(0, 0, 0)
                mask_k(1, 1, 0)
                copy_max(0, 0)
                for s, u, i in rounds(act, SEQS, 4, head=4, tail=4):
                    p = u % 2
                    wait(act, mixed, s - 1)
                    for g in range(HG):
                        act.wait_ge(shifted, 4 * s + g + 1)
                        nc.scalar.activation(prob[p][:, g, :], ps2[:, g % 2, :], ACT.Exp, scale=ATT_SCALE
                                             ).then_inc(exped, 1)
                    if not (isinstance(s, int) and s >= SEQS - 2):
                        mask_k(s + 2, (u + 2) % 4, i + (u + 2) // 4)
                    if not is_last(s, SEQS):
                        copy_max(s + 1, u + 1)

            @block.tensor
            def _(pe):
                def score(s, u, i, g):
                    p, b = u % 2, u // 2
                    wait(pe, maxed, 4 * s + g - 1)
                    nc.tensor.matmul(ps1[:, g % 2, :], qp[b][:, g, tok(u)], km[p][:, g].rearrange("p j k -> p (j k)"),
                                     start=True, stop=True).then_inc(scored, 1)

                def shift(s, u, g):
                    p, b = u % 2, u // 2
                    wait(pe, exped, 4 * s + g - 1)
                    nc.tensor.matmul(ps2[:, g % 2, :], kp[b][:, g, tok(u)], qm[p][:, g].rearrange("p j k -> p (j k)"),
                                     start=True, stop=False)
                    nc.tensor.matmul(ps2[:, g % 2, :], selr[:, g, :], mxT[p][:], start=False, stop=True
                                     ).then_inc(shifted, 1)

                def turn_max(s, u):
                    pe.wait_ge(parted, s + 1)
                    wait(pe, mxT_done, s)
                    for j in range(4):
                        ins = nc.tensor.transpose(psM[:, j * P:(j + 1) * P], xm[u % 2][:, j, :], m.ident)
                    ins.then_inc(turned, 1)

                def mix(s, u):
                    p = u % 2
                    pe.wait_ge(exped, 4 * s + 4)
                    pe.wait_ge(vb_done, s + 1)
                    wait(pe, divided, s - 1)
                    for j in range(4):
                        for g in range(HG):
                            nc.tensor.matmul(psO[32 * g:32 * g + 32, p, 0:P], vb[p][:, 4 * g + j, :],
                                             prob[p][:, g, j * P:(j + 1) * P], start=(j == 0), stop=(j == 3),
                                             skip_group_check=True)

                def total(s, u):
                    p = u % 2
                    for j in range(4):
                        for g in range(HG):
                            ins = nc.tensor.matmul(psO[32 * g:32 * g + 32, p, P:2 * P],
                                                   m.const[:, C_ONESB + 32 * j:C_ONESB + 32 * j + 32],
                                                   prob[p][:, g, j * P:(j + 1) * P], start=(j == 0), stop=(j == 3),
                                                   skip_group_check=True)
                    ins.then_inc(mixed, 1)

                def project(s, u):
                    pe.wait_ge(divided, s + 1)
                    wait(pe, kept, s)
                    nc.tensor.matmul(psW[:, 0:P], oT[u % 2][:], m.wo[:], start=True, stop=True).then_inc(projected, 1)

                def ready(s, u, i):
                    if u % 2 == 0:
                        pe.wait_ge(pair_in[u // 2], 96 * (i + 1))
                    pe.wait_ge(km_pool, s + 1)
                    pe.wait_ge(km_act, s + 1)

                ready(0, 0, 0)
                for g in range(HG):
                    score(0, 0, 0, g)
                turn_max(0, 0)
                for s, u, i in rounds(pe, SEQS, 4, head=4, tail=4):
                    nxt = (s + 1, (u + 1) % 4, i + (u + 1) // 4)
                    more = not is_last(s, SEQS)
                    if more:
                        ready(*nxt)
                    for g in range(HG):
                        if more:
                            score(*nxt, g)
                        if g == 0:
                            pe.wait_ge(qm_done, s + 1)
                            pe.wait_ge(mxT_done, s + 1)
                        shift(s, u, g)
                    if not soon(s, 3):
                        project(s - 3, u + 1)
                    if not first(s):
                        mix(s - 1, u - 1)
                    if more:
                        turn_max(s + 1, u + 1)
                    if not first(s):
                        total(s - 1, u - 1)
                project(SEQS - 3, 1)
                mix(SEQS - 1, 1)
                total(SEQS - 1, 1)
                project(SEQS - 2, 0)
                project(SEQS - 1, 1)



def post_attention(m, d):
    nc = m.nc
    with ExitStack() as ctx:
        two = lambda n, s, dt=F32: [m.sb(f"{n}{b}", s, dt, ctx) for b in range(2)]
        stats = two("stats2", [P, GT, 6])
        mv = two("mv2", [P, GT, 2])
        var, std, rstd = two("var2", [P, GT]), two("std2", [P, GT]), two("rstd2", [P, GT])
        norm = two("norm2", [P, GT, P])
        hT = two("h2T", [P, GW])
        psH = m.ps("psH2", [P, 512], ctx)
        psN = m.ps("psN2", [P, 2, 512], ctx)
        psR = m.ps("psR2", [P, 512], ctx)
        rank = psR[:, 0:(GT + 1) * E]
        r = Router(m, ctx, "1", m.rows[:, R_GB:R_GB + E])
        link, var_done, sqrted, normed, turned, hT_done, nat, nat_copied, summed = m.sems(
            "q_link", "q_var", "q_sqrted", "q_normed", "q_turned", "q_hT", "q_nat", "q_nat_copied", "q_summed")
        with nc.Block() as block:
            @block.gpsimd
            def _(pool):
                for n, b, i in rounds(pool, GROUPS, 2):
                    route_scatter(r, pool, n, b, nat_copied)
                for b in range(2):
                    pool.wait_ge(r.scattered[b], r.sends * GROUPS // 2)

            @block.vector
            def _(dve):
                chain = Chain(m, dve, r.link, ROUTE_LINKS)
                ln = Chain(m, dve, link, 3)

                def normalise(n, b):
                    ln.begin(n)
                    at = lambda t: m.X3[:, bass.ds(n * GT + t, 1), :].rearrange("p a c -> p (a c)")
                    layernorm(m, dve, ln, n, at, stats[b], mv[b], var[b], var_done, std[b], sqrted, rstd[b], norm[b],
                              turned, normed)

                normalise(0, 0)
                normalise(1, 1)
                for n, b, i in rounds(dve, GROUPS, 2, head=2, tail=2):
                    route_choose(r, dve, chain, n, b, psN, nat)
                    mine = bass.ds(n * GT, GT)
                    nc.vector.tensor_tensor(m.X[:, mine, :], m.X[:, mine, :], m.X3[:, mine, :], ALU.add)
                    route_index(r, dve, chain, n, b, i, rank)
                    if not late(n):
                        normalise(n + 2, b)

            @block.scalar
            def _(act):
                def root(n, b):
                    act.wait_ge(var_done, n + 1)
                    nc.scalar.activation(std[b][:], var[b][:], ACT.Sqrt).then_inc(sqrted, 1)

                def scale(n, b):
                    act.wait_ge(turned, n + 1)
                    wait(act, nat, n - 1)
                    nc.scalar.activation(hT[b][:], psH[:], ACT.Identity, bias=m.vec[:, V_LN2B:V_LN2B + 1],
                                         scale=m.vec[:, V_LN2G:V_LN2G + 1]).then_inc(hT_done, 1)

                root(0, 0)
                root(1, 1)
                scale(0, 0)
                for n, b, i in rounds(act, GROUPS, 2, head=2, tail=2):
                    if not is_last(n, GROUPS):
                        scale(n + 1, 1 - b)
                    act.wait_ge(r.got, n + 1)
                    wait(act, r.scattered[b], r.sends * i)
                    route_rows(r, b, psN, nat_copied)
                    if not late(n):
                        root(n + 2, b)

            @block.tensor
            def _(pe):
                def turn(n, b):
                    pe.wait_ge(normed, n + 1)
                    wait(pe, hT_done, n)
                    for t in range(GT):
                        ins = nc.tensor.transpose(psH[:, t * P:(t + 1) * P], norm[b][:, t, :], m.ident)
                    ins.then_inc(turned, 1)

                def natural(n, b):
                    pe.wait_ge(hT_done, n + 1)
                    wait(pe, nat_copied, n)
                    for t in range(GT):
                        w = (t % 2) * (P + E)
                        for part, rhs in ((slice(w, w + P), m.ident), (slice(w + P, w + P + E), m.gate[:])):
                            ins = nc.tensor.matmul(psN[:, t // 2, part], hT[b][:, t * P:(t + 1) * P], rhs,
                                                   start=True, stop=True, skip_group_check=True)
                    ins.then_inc(nat, 1)

                turn(0, 0)
                natural(0, 0)
                for n, b, i in rounds(pe, GROUPS, 2, head=2, tail=2):
                    if not is_last(n, GROUPS):
                        turn(n + 1, 1 - b)
                    route_rank(r, pe, n, b, rank)
                    if not is_last(n, GROUPS):
                        natural(n + 1, 1 - b)


def experts1(m, d):
    nc = m.nc
    WIDE = KT1 * P
    with ExitStack() as ctx:
        sb = lambda n, s, dt=F32: m.sb(n, s, dt, ctx)
        wb = [sb(f"wb{b}", [P, 2 * WIDE + KT1]) for b in range(EB)]
        b2 = [sb(f"b2_{b}", [P, P]) for b in range(EB)]
        xs = [sb(f"xt{b}", [P, 2, ROW]) for b in range(EB)]
        out = [sb(f"fo_{b}", [P, 2, P]) for b in range(EB)]
        to = [sb(f"to1_{b}", [P, 2], U32) for b in range(EB)]
        xsT = [sb(f"xtT{q}", [P, SLOTS]) for q in range(2)]
        h = [sb(f"fh{q}", [P, KT1, SLOTS]) for q in range(2)]
        psT = m.ps("psT1", [P, 2, 512], ctx)
        psA = m.ps("psA1", [P, 4, 512], ctx)
        psO = m.ps("psO1", [P, 2, 512], ctx)
        ld, st = m.ld, m.st
        past = ETILES // EB
        turned, copied, up_a, up_b, relu_a, relu_b, down, evac = m.sems(
            "e1_turned", "e1_copied", "e1_up_a", "e1_up_b", "e1_relu_a", "e1_relu_b", "e1_down", "e1_evac")
        with nc.Block() as block:
            @block.sync
            def _(sp):
                for n, b, i in rounds(sp, ETILES, EB, head=EB):
                    e = sp.value_load(m.table[0:1, bass.ds(n, 1)], min_val=0, max_val=E - 1)
                    row = sp.value_load(m.table[0:1, bass.ds(n + ETILES, 1)], min_val=0, max_val=E * REGION + (E - 1) * SLOTS)
                    hold(m, sp, down, n - EB + 1)
                    hold(m, sp, copied, n - EB + 1)
                    hold(m, sp, evac, n - EB + 1)
                    sp.dma_start(xs[b][:], m.xbuf[bass.ds(row, SLOTS), :].rearrange("(a p) c -> p a c", p=P)
                                 ).then_inc(ld[b], 16)
                    sp.dma_start(wb[b][:], d["W1b"][bass.ds(e, 1)].rearrange("e p h -> (e p) h")).then_inc(ld[b], 16)
                    sp.dma_start(b2[b][:], d["b2"][bass.ds(e, 1)].to_broadcast([P, P])).then_inc(ld[b], 16)

            @block.tensor
            def _(pe):
                def up(n, b):
                    q = b % 2
                    pe.wait_ge(copied, n + 1)
                    for half, free, done in ((0, relu_a, up_a), (1, relu_b, up_b)):
                        wait(pe, free, 2 * (n - 1))
                        for a in range(2):
                            k = 2 * half + a
                            ins = nc.tensor.matmul(psA[:, 2 * q + half, a * SLOTS:(a + 1) * SLOTS], wb[b][:, k * P:(k + 1) * P],
                                                   xsT[q][:], start=True, stop=True, skip_group_check=True)
                        ins.then_inc(done, 1)

                turn_rows(m, pe, 0, 0, past, ld, xs, psT, copied, turned)
                turn_rows(m, pe, 1, 1, past, ld, xs, psT, copied, turned)
                up(0, 0)
                for n, b, i in rounds(pe, ETILES, EB, head=EB, tail=EB):
                    if not nearly(n):
                        turn_rows(m, pe, n + 2, (b + 2) % EB, i + (b + 2) // EB + past, ld, xs, psT, copied, turned)
                    if not is_last(n, ETILES):
                        up(n + 1, (b + 1) % EB)
                    q = b % 2
                    pe.wait_ge(relu_a, 2 * (n + 1))
                    pe.wait_ge(relu_b, 2 * (n + 1))
                    wait(pe, evac, n - 1)
                    for a in range(2):
                        for k in range(KT1):
                            ins = nc.tensor.matmul(psO[:, q, a * P:(a + 1) * P], h[q][:, k, a * P:(a + 1) * P],
                                                   wb[b][:, WIDE + k * P:WIDE + (k + 1) * P],
                                                   start=(k == 0), stop=(k == KT1 - 1), skip_group_check=True)
                    ins.then_inc(down, 1)

            @block.vector
            def _(dve):
                def leave(n, b, i):
                    dve.wait_ge(down, n + 1)
                    wait(dve, st[b], 32 * i)
                    nc.vector.tensor_tensor(out[b][:], psO[:, b % 2, 0:SLOTS].rearrange("p (a c) -> p a c", a=2),
                                            bc(b2[b][:].unsqueeze(1), P, 2, P), ALU.add).then_inc(evac, 1)

                copy_rows(m, dve, 0, 0, past, psT, xsT, xs, to, turned, up_b, st, copied)
                copy_rows(m, dve, 1, 1, past, psT, xsT, xs, to, turned, up_b, st, copied)
                for n, b, i in rounds(dve, ETILES, EB, head=EB, tail=EB):
                    q = b % 2
                    dve.wait_ge(up_b, n + 1)
                    wait(dve, down, n - 1)
                    for a in range(2):
                        nc.vector.tensor_scalar(h[q][:, 2 + a, :], psA[:, 2 * q + 1, a * SLOTS:(a + 1) * SLOTS],
                                                wb[b][:, 2 * WIDE + 2 + a:2 * WIDE + 3 + a], 0.0, ALU.add, ALU.max
                                                ).then_inc(relu_b, 1)
                    if not nearly(n):
                        copy_rows(m, dve, n + 2, (b + 2) % EB, i + (b + 2) // EB + past, psT, xsT, xs, to, turned, up_b, st,
                                  copied)
                    if not first(n):
                        leave(n - 1, (b - 1) % EB, (i if b else i - 1) + past)
                leave(ETILES - 1, EB - 1, 2 * past - 1)

            @block.gpsimd
            def _(pool):
                for n, b, i in rounds(pool, ETILES, EB, head=EB):
                    send_rows(m, pool, n, b, evac, out, to, st)
                for b in range(EB):
                    pool.wait_ge(st[b], 32 * 2 * past)

            @block.scalar
            def _(act):
                for n, b, i in rounds(act, ETILES, EB, head=EB):
                    q = b % 2
                    act.wait_ge(up_a, n + 1)
                    wait(act, down, n - 1)
                    for a in range(2):
                        nc.scalar.activation(h[q][:, a, :], psA[:, 2 * q, a * SLOTS:(a + 1) * SLOTS], ACT.Relu,
                                             bias=wb[b][:, 2 * WIDE + a:2 * WIDE + a + 1]).then_inc(relu_a, 1)



def build(nc, d, out):
    with ExitStack() as ctx:
        m = Machine(nc, ctx)
        allocate(m, d)
        with ExitStack() as front:
            loads = layer0_loads(m, front)
            setup(m, d, loads)
            layer0(m, loads)
        tile_table(m, "0")
        experts0(m, d)
        pre_attention(m, d)
        attention(m, d)
        post_attention(m, d)
        tile_table(m, "1")
        experts1(m, d)
        finish(m, d, out)



def laid_out(a):
    x = np.ascontiguousarray(a["x"]).reshape(TOK, P)
    W3 = a["L0_ffn_W3"].reshape(E, 2, HALF, P).transpose(0, 2, 1, 3).reshape(E, HALF, 2 * P)
    W2b = a["L1_ffn_W2"].reshape(E, KT1, P, P).transpose(0, 2, 1, 3).reshape(E, P, KT1 * P)
    b1 = a["L1_ffn_b1"].reshape(E, KT1, P).transpose(0, 2, 1)
    b_qkv = a["L1_ffn_b_qkv"]
    vec = [a["L0_cond_bias"], a["L0_cond_affine_b"], a["L1_ffn_ln1_g"], a["L1_ffn_ln1_b"], a["L1_ffn_ln2_g"],
           a["L1_ffn_ln2_b"], b_qkv[0:P], b_qkv[P:2 * P]]
    out = {
        "x": x, "xT": x.T, "const": constants(),
        "condT": a["cond_512"].T, "affT": a["L0_cond_affine_w"].T, "WT": a["L0_cond_weight"].T,
        "vec": np.stack(vec, axis=1),
        "rows": np.concatenate([b_qkv[2 * P:], a["L1_ffn_b_o"], a["L1_ffn_gate_b"]])[None, :],
        "gb": np.concatenate([a["L1_cond_down_gamma"], a["L1_cond_down_beta"],
                              a["L1_cond_up_gamma"], a["L1_cond_up_beta"]], axis=1),
        "Wg": a["L0_ffn_Wg"], "W12": np.concatenate([a["L0_ffn_W1"], a["L0_ffn_W2"]], axis=2), "W3": W3,
        "Ws1": a["L0_ffn_Ws1"], "Ws2": a["L0_ffn_Ws2"], "Ws3": a["L0_ffn_Ws3"],
        "dproj": a["L1_cond_down_project"], "uproj": a["L1_cond_up_project"],
        "wqkv": a["L1_ffn_w_qkv"], "wo": a["L1_ffn_w_o"], "gate": a["L1_ffn_gate_w"],
        "W1b": np.concatenate([a["L1_ffn_W1"], W2b, b1], axis=2), "b2": a["L1_ffn_b2"],
    }
    return {k: np.ascontiguousarray(v) for k, v in out.items()}


def kernel(**inputs):
    import concourse.bacc as bacc
    from concourse.bass_utils import run_bass_kernel_spmd

    nc = bacc.Bacc("TRN2", target_bir_lowering=False, num_devices=1)
    arrays = {f"in_{k}": v for k, v in laid_out({k: np.asarray(v) for k, v in inputs.items()}).items()}
    d = {k[3:]: nc.dram_tensor(k, v.shape, mybir.dt.from_np(v.dtype), kind="ExternalInput").ap()
         for k, v in arrays.items()}
    out = nc.dram_tensor("out", (SEQS, P, P), F32, kind="ExternalOutput").ap()
    build(nc, d, out)
    r = run_bass_kernel_spmd(nc, [arrays], core_ids=[0])
    return r.results[0]["out"]
```

```python
from contextlib import ExitStack

import numpy as np

import concourse.bass as bass
from concourse import mybir

F32 = mybir.dt.float32
F32R = mybir.dt.float32r
BF16 = mybir.dt.bfloat16
U32 = mybir.dt.uint32
I32 = mybir.dt.int32
ALU = mybir.AluOpType
ACT = mybir.ActivationFunctionType
AX_X = mybir.AxisListType.X

P = 128
SEQS = 32
TOK = SEQS * P
GT = 4
GROUPS = SEQS // GT
GW = GT * P
E = 8
TOPK = 2
COND = 64
PAIR = 2 * P
SLOTS = 256
REGION = TOK + SLOTS
ETILES = TOK * TOPK // SLOTS + E
MAXT = TOK // SLOTS
ROW = P + 1
HALF = 88
HS = 352
DOWN = 32
HEADS = 16
HG = 4
KT1 = 4
SHARED = [P, P, HS - 2 * P]
CLAMP = 256.0
EPS = 1e-5
ATT_SCALE = float(1.0 / np.sqrt(8.0))

C_ID = 0
C_TRI = C_ID + P
C_ONESB = C_TRI + P
C_SEL = C_ONESB + P
C_MASK = C_SEL + 4
C_EXP = C_MASK + 4
C_REG = C_EXP + E + 1
C_TILE = C_REG + E + 1
C_STEP = C_TILE + ETILES
C_TOK = C_STEP + MAXT
C_TAIL = C_TOK + SEQS * TOPK
C_END = C_TAIL + 4 * E

V_BIAS, V_AFFB, V_LN1G, V_LN1B, V_LN2G, V_LN2B, V_BQ, V_BK = range(8)
R_BV, R_BO, R_GB = 0, P, 2 * P
R_END = 2 * P + E


def constants():
    c = np.zeros((P, C_END), np.float32)
    p = np.arange(P)
    c[:, C_ID:C_ID + P] = np.eye(P)
    c[:, C_TRI:C_TRI + P] = p[:, None] < p[None, :]
    col = np.arange(32)
    for j in range(4):
        c[:, C_ONESB + 32 * j:C_ONESB + 32 * j + 32] = (col // 8 == j)[None, :]
        c[:, C_SEL + j] = (p // 32 == j) & (p % 32 < 8)
        c[:, C_MASK + j] = (p % 32) // 8 == j
    c[:, C_EXP:C_EXP + E + 1] = np.arange(E + 1)
    c[:, C_REG:C_REG + E + 1] = np.arange(E + 1) * REGION
    c[:, C_TOK:C_TOK + SEQS * TOPK] = 2 * p[:, None] + (np.arange(SEQS)[:, None] * 2 * P + np.arange(2)).reshape(1, -1)
    c[:, C_TAIL:C_TAIL + 4 * E] = 2 * TOK + p[:, None] + np.arange(4 * E)[None, :] * P
    c[:, C_TILE:C_TILE + ETILES] = np.arange(ETILES)
    c[:, C_STEP:C_STEP + MAXT] = np.arange(MAXT) * SLOTS
    return c


def rounds(engine, total, unroll, head=0, tail=0):
    for n in range(head):
        yield n, n % unroll, n // unroll
    with engine.Fori(0, (total - head - tail) // unroll) as i:
        for u in range(unroll):
            yield i * unroll + (head + u), u, i + head // unroll
    for n in range(total - tail, total):
        yield n, n % unroll, n // unroll


def first(n):
    return isinstance(n, int) and n == 0


def is_last(n, total):
    return isinstance(n, int) and n == total - 1


def wait(engine, sem, value):
    if not (isinstance(value, int) and value <= 0):
        engine.wait_ge(sem, value)


def hold(m, engine, sem, value):
    wait(engine, sem, value)
    if not isinstance(value, int):
        engine.sem_inc(m.passed, 1)


class Chain:

    def __init__(self, m, engine, sem, per=0):
        self.m = m
        self.engine, self.sem, self.per, self.base, self.count = engine, sem, per, 0, 0

    def begin(self, n):
        self.base, self.count = n * self.per, 0

    def __call__(self, instruction):
        self.count += 1
        instruction.then_inc(self.sem, 1)
        hold(self.m, self.engine, self.sem, self.base + self.count)


def late(n, ahead=2):
    return isinstance(n, int) and n >= GROUPS - ahead


def bc(ap, *shape):
    return ap.to_broadcast(list(shape))


class Machine:

    def __init__(self, nc, ctx):
        self.nc, self.ctx = nc, ctx

    def sb(self, name, shape, dt=F32, ctx=None):
        return (ctx or self.ctx).enter_context(self.nc.sbuf_tensor(name, shape, dt))

    def ps(self, name, shape, ctx, dt=F32):
        return ctx.enter_context(self.nc.psum_tensor(name, shape, dt))

    def sem(self, name):
        return self.ctx.enter_context(self.nc.semaphore(name))

    def sems(self, *names):
        return [self.sem(n) for n in names]


def allocate(m, d):
    nc = m.nc
    m.passed = m.sem("passed")
    m.X = m.sb("X", [P, SEQS, P])
    m.X3 = m.sb("X3", [P, SEQS, P])
    m.V = m.sb("V", [P, SEQS, P])
    m.const = m.sb("const", [P, C_END])
    m.vec = m.sb("vec", [P, 8])
    m.rows = m.sb("rows", [P, R_END])
    m.tri = m.sb("tri", [P, P], BF16)
    m.ones = m.sb("ones", [P, P], BF16)
    m.ident = m.const[:, C_ID:C_ID + P]
    m.diff = m.sb("diff", [P, SEQS])
    m.pw = m.sb("pw", [P, SEQS, TOPK])
    m.ids = m.sb("ids", [P, SEQS, TOPK], U32)
    m.base = m.sb("base", [P, E + 1])
    m.tail = m.sb("tail", [P, 2 * E, 2, ROW])
    m.table = m.sb("table", [P, 2 * ETILES + E], I32)
    m.styles = m.sb("styles", [P, SEQS])
    m.dcoef = m.sb("dcoef", [P, SEQS])
    m.gbD = m.sb("gbD", [P, SEQS, 2 * DOWN])
    m.wqkv = m.sb("wqkv", [P, 3 * P])
    m.dproj = m.sb("dproj", [P, DOWN])
    m.uproj = m.sb("uproj", [DOWN, P])
    m.wo = m.sb("wo", [P, P])
    m.IG = m.sb("IG1", [P, P + E])
    m.late_ld, m.gb_in = m.sems("late_ld", "gb_in")
    m.xbuf = nc.dram_tensor("dispatch_rows", (E * REGION + E * SLOTS, ROW), F32, kind="Internal").ap()
    m.ybuf = nc.dram_tensor("expert_rows", (TOPK * TOK + 2 * E * SLOTS, P), F32, kind="Internal").ap()
    m.gb_dram = nc.dram_tensor("cond_rows", (SEQS, 2 * DOWN + 2 * P), F32, kind="Internal").ap()
    m.qk_dram = nc.dram_tensor("qk_parts", (4, P, TOK), F32, kind="Internal").ap()



FIRST_LOADS = 16 * 7
LATE_LOADS = 16 * 7


def layer0_loads(m, ctx):
    sb = lambda n, s: m.sb(n, s, ctx=ctx)
    return (sb("xT", [P, TOK]), sb("WT", [P, P]), sb("IG0", [P, P + E]), sb("Ws1", [P, HS]), sb("Ws2", [P, HS]),
            sb("Ws3", [P, 3, P]), m.sem("first_ld"), m.sem("rest_ld"), m.sem("x_ld"))


def setup(m, d, loads):
    nc = m.nc
    xT, WT, IG, Ws1, Ws2, Ws3, first_ld, rest_ld, x_ld = loads
    with ExitStack() as ctx:
        condT = m.sb("condT", [COND, SEQS], ctx=ctx)
        affT = m.sb("affT", [COND, P], ctx=ctx)
        gb = m.sb("gb", [COND, 2 * DOWN + 2 * P], ctx=ctx)
        sq = m.sb("sq", [P, P], ctx=ctx)
        ssq = m.sb("ssq", [P, SEQS], ctx=ctx)
        dsum = m.sb("dsum", [P, SEQS], ctx=ctx)
        root, guess = m.sb("root", [P, SEQS], ctx=ctx), m.sb("guess", [P, SEQS], ctx=ctx)
        gbrow = m.sb("gbrow", [SEQS, 2 * DOWN + 2 * P], ctx=ctx)
        ps = m.ps("ps_setup", [P, 3, 512], ctx)
        (loaded, styled, squared, pe_st, pe_dc, pe_gb, gb_copied, summed, rooted, gb_out, cleared, newton) = m.sems(
            "loaded", "styled", "squared", "pe_st", "pe_dc", "pe_gb", "gb_copied", "summed", "rooted", "gb_out",
            "set_cleared", "newton")
        with nc.Block() as block:
            @block.sync
            def _(sp):
                for dst, src in [(condT[:], d["condT"]), (affT[:], d["affT"]), (WT[:], d["WT"]), (m.vec[:], d["vec"]),
                                 (gb[:], d["gb"]), (m.const[:], d["const"])]:
                    sp.dma_start(dst, src).then_inc(loaded, 16)
                def load(*transfers):
                    for dst, src, sem in transfers:
                        sp.dma_start(dst, src).then_inc(sem, 16)

                load((xT[:, 0:2 * GW], d["xT"][:, 0:2 * GW], first_ld),
                        (IG[:, 0:P], d["const"][:, C_ID:C_ID + P], first_ld), (IG[:, P:], d["Wg"], first_ld),
                        (Ws1[:], d["Ws1"], first_ld), (Ws2[:], d["Ws2"], first_ld),
                        (Ws3[:, 0:2, :], d["Ws3"][0:2 * P, :].rearrange("(k p) c -> p k c", p=P), first_ld),
                        (Ws3[0:SHARED[2], 2, :], d["Ws3"][2 * P:HS, :], first_ld))
                sp.wait_ge(gb_copied, 1)
                load((xT[:, 2 * GW:], d["xT"][:, 2 * GW:], rest_ld),
                        (m.X[:], d["x"].rearrange("(s p) c -> p s c", p=P), x_ld),
                        (m.rows[:], d["rows"].to_broadcast([P, R_END]), m.late_ld),
                        (m.wqkv[:], d["wqkv"], m.late_ld), (m.dproj[:], d["dproj"], m.late_ld),
                        (m.uproj[:], d["uproj"], m.late_ld), (m.wo[:], d["wo"], m.late_ld),
                        (m.IG[:, 0:P], d["const"][:, C_ID:C_ID + P], m.late_ld), (m.IG[:, P:], d["gate"], m.late_ld))

            @block.gpsimd
            def _(pool):
                nc.gpsimd.memset(m.ones[:], 1.0)
                nc.gpsimd.memset(m.tail[:], 0.0).then_inc(cleared, 1)

            @block.tensor
            def _(pe):
                pe.wait_ge(loaded, 16 * 6)
                nc.tensor.matmul(ps[:, 0, 0:SEQS], affT[:], condT[:], start=True, stop=True).then_inc(pe_st, 1)
                nc.tensor.matmul(ps[0:SEQS, 1, 0:2 * DOWN + 2 * P], condT[:], gb[:], start=True,
                                 stop=True).then_inc(pe_gb, 1)
                pe.wait_ge(squared, 2)
                nc.tensor.matmul(ps[:, 2, 0:SEQS], sq[:], ssq[:], start=True, stop=True).then_inc(pe_dc, 1)

            @block.scalar
            def _(act):
                act.wait_ge(gb_copied, 1)
                act.dma_start(m.gb_dram, gbrow[:]).then_inc(gb_out, 16)
                act.wait_ge(summed, 1)
                nc.scalar.activation(root[:], dsum[:], ACT.Sqrt).then_inc(rooted, 1)
                act.wait_ge(gb_out, 16)
                act.dma_start(m.gbD[:], m.gb_dram[:, 0:2 * DOWN].unsqueeze(0).to_broadcast(
                    [P, SEQS, 2 * DOWN])).then_inc(m.gb_in, 16)

            @block.vector
            def _(dve):
                c = Chain(m, dve, newton)
                dve.wait_ge(loaded, 16 * 6)
                nc.vector.tensor_tensor(sq[:], WT[:], WT[:], ALU.mult).then_inc(squared, 1)
                dve.wait_ge(pe_st, 1)
                nc.vector.tensor_scalar(m.styles[:], ps[:, 0, 0:SEQS], float(1 / np.sqrt(COND)),
                                        m.vec[:, V_AFFB:V_AFFB + 1], ALU.mult, ALU.add).then_inc(styled, 1)
                dve.wait_ge(pe_gb, 1)
                nc.vector.tensor_copy(gbrow[:], ps[0:SEQS, 1, 0:2 * DOWN + 2 * P]).then_inc(gb_copied, 1)
                dve.wait_ge(styled, 1)
                nc.vector.tensor_tensor(ssq[:], m.styles[:], m.styles[:], ALU.mult).then_inc(squared, 1)
                nc.vector.tensor_copy(m.tri[:], m.const[:, C_TRI:C_TRI + P])
                nc.vector.tensor_copy(m.base[:], m.const[:, C_REG:C_REG + E + 1])
                dve.wait_ge(pe_dc, 1)
                nc.vector.tensor_scalar(dsum[:], ps[:, 2, 0:SEQS], 1e-8, None, ALU.add).then_inc(summed, 1)
                nc.vector.tensor_copy(m.ids[:].rearrange("p s k -> p (s k)"), m.const[:, C_TOK:C_TOK + SEQS * TOPK])
                dve.wait_ge(cleared, 1)
                nc.vector.tensor_copy(m.tail[:, :, :, P:].bitcast(U32),
                                      m.const[:, C_TAIL:C_TAIL + 4 * E].rearrange("p (e a o) -> p e a o", a=2, o=1))
                dve.wait_ge(rooted, 1)
                c(nc.vector.reciprocal(guess[:], root[:]))
                c(nc.vector.tensor_tensor(root[:], guess[:], guess[:], ALU.mult))
                c(nc.vector.tensor_tensor(root[:], root[:], dsum[:], ALU.mult))
                c(nc.vector.tensor_scalar(root[:], root[:], -0.5, 1.5, ALU.mult, ALU.add))
                nc.vector.tensor_tensor(m.dcoef[:], root[:], guess[:], ALU.mult)



ROUTE_LINKS = 5


class Router:

    def __init__(self, m, ctx, tag, bias):
        self.m, self.bias = m, bias
        self.logits = [m.sb(f"logits{tag}{b}", [P, GT, E], ctx=ctx) for b in range(2)]
        self.best = [m.sb(f"best{tag}{b}", [P, GT, 8], ctx=ctx) for b in range(2)]
        self.choice = [m.sb(f"choice{tag}{b}", [P, GT, 8], U32, ctx=ctx) for b in range(2)]
        self.mask = [m.sb(f"mask{tag}{b}", [P, GT, E], BF16, ctx=ctx) for b in range(2)]
        self.slot = [m.sb(f"slot{tag}{b}", [P, GT, E], ctx=ctx) for b in range(2)]
        self.prod = [m.sb(f"prod{tag}{b}", [P, GT, TOPK, E], ctx=ctx) for b in range(2)]
        self.index = [m.sb(f"index{tag}{b}", [P, GT * TOPK], U32, ctx=ctx) for b in range(2)]
        self.hot = [m.sb(f"hot{tag}{b}", [P, GT, TOPK, E], ctx=ctx) for b in range(2)]
        self.row = [m.sb(f"row{tag}{b}", [P, GT, TOPK, ROW], ctx=ctx) for b in range(2)]
        (self.link, self.got, self.masked, self.ranked,
         self.indexed) = m.sems(*(f"{s}{tag}" for s in ("rt_link", "rt_got", "rt_masked", "rt_ranked", "rt_indexed")))
        self.scattered = m.sems(f"rt_scattered{tag}_0", f"rt_scattered{tag}_1")
        self.sends = 16 * GT * TOPK


def route_logits(r, dve, n, b, nat, nat_ready):
    nc = r.m.nc
    dve.wait_ge(nat_ready, n + 1)
    for a in range(2):
        lg = r.logits[b][:, 2 * a:2 * a + 2, :]
        src = nat[a].rearrange("p (c w) -> p c w", c=2)[:, :, P:P + E]
        if r.bias is None:
            ins = nc.vector.tensor_copy(lg, src)
        else:
            ins = nc.vector.tensor_tensor(lg, src, bc(r.bias.unsqueeze(1), P, 2, E), ALU.add)
    ins.then_inc(r.got, 1)


def route_choose(r, dve, chain, n, b):
    m, nc = r.m, r.m.nc
    tiles = bass.ds(n * GT, GT)
    chain.begin(n)
    hold(m, dve, r.got, n + 1)
    for t in range(GT):
        ins = nc.vector.max(r.best[b][:, t, :], r.logits[b][:, t, :])
    chain(ins)
    for t in range(GT):
        ins = nc.vector.max_index(r.choice[b][:, t, :], r.best[b][:, t, :], r.logits[b][:, t, :])
    chain(ins)
    nc.vector.tensor_tensor(m.diff[:, tiles], r.best[b][:, :, 1], r.best[b][:, :, 0], ALU.subtract)
    chain(nc.vector.tensor_tensor(
        r.hot[b][:], bc(r.choice[b][:, :, 0:TOPK].unsqueeze(3), P, GT, TOPK, E),
        bc(m.const[:, C_EXP:C_EXP + E].unsqueeze(1).unsqueeze(1), P, GT, TOPK, E), ALU.is_equal))
    nc.vector.tensor_tensor(r.mask[b][:], r.hot[b][:, :, 0, :], r.hot[b][:, :, 1, :], ALU.add).then_inc(r.masked, 1)


def route_rank(r, pe, n, b, rank):
    m, nc = r.m, r.m.nc
    pe.wait_ge(r.masked, n + 1)
    wait(pe, r.indexed, n)
    for t in range(GT + 1):
        out = rank[:, t * E:(t + 1) * E]
        for u in range(min(t + 1, GT)):
            ins = nc.tensor.matmul(out, m.tri[:] if u == t else m.ones[:], r.mask[b][:, u, :],
                                   start=(u == 0), stop=(u == min(t, GT - 1)), skip_group_check=True)
    ins.then_inc(r.ranked, 1)


def route_index(r, dve, chain, n, b, i, rank):
    m, nc = r.m, r.m.nc
    tiles = bass.ds(n * GT, GT)
    dve.wait_ge(r.ranked, n + 1)
    chain(nc.vector.tensor_tensor(r.slot[b][:], rank[:, 0:GT * E].rearrange("p (t e) -> p t e", t=GT),
                                  bc(m.base[:, 0:E].unsqueeze(1), P, GT, E), ALU.add))
    nc.vector.tensor_tensor(m.base[:, 0:E], m.base[:, 0:E], rank[:, GT * E:(GT + 1) * E], ALU.add)
    chain(nc.vector.tensor_tensor(r.prod[b][:], r.hot[b][:],
                                  bc(r.slot[b][:].unsqueeze(2), P, GT, TOPK, E), ALU.mult))
    hold(m, dve, r.scattered[b], r.sends * i)
    nc.vector.tensor_copy(r.row[b][:, :, :, P:].bitcast(U32), m.ids[:, tiles, :].unsqueeze(3))
    with nc.allow_low_precision(reason="whole numbers below 2^24"):
        nc.vector.tensor_reduce(r.index[b][:].rearrange("p (t k) -> p t k", t=GT), r.prod[b][:], AX_X, ALU.add
                                ).then_inc(r.indexed, 1)


def route_rows(r, b, nat, copied, copies=TOPK):
    for a in range(2):
        for k in range(copies):
            ins = r.m.nc.scalar.activation(r.row[b][:, 2 * a:2 * a + 2, k, 0:P],
                                           nat[a].rearrange("p (c w) -> p c w", c=2)[:, :, 0:P], ACT.Copy)
    ins.then_inc(copied, 1)


def route_scatter(r, pool, n, b, rows_ready, part=range(GT * TOPK)):
    m = r.m
    pool.wait_ge(r.indexed, n + 1)
    hold(m, pool, rows_ready, n + 1)
    for c in part:
        pool.indirect_dma_start(
            out=m.xbuf, out_offset=bass.IndirectOffsetOnAxis(ap=r.index[b][:, c:c + 1], axis=0),
            in_=r.row[b][:, c // TOPK, c % TOPK, :], in_offset=None).then_inc(r.scattered[b], 16)


class TileTable:

    def __init__(self, m, ctx, tag, indexed):
        self.m, self.indexed = m, indexed
        E1 = E + 1
        sb = lambda name, shape: m.sb(name + tag, shape, ctx=ctx)
        self.cnt, self.need, self.one, self.incl, self.excl, self.delta = (
            sb(x, [P, E1]) for x in ("cnt", "need", "one", "incl", "excl", "delta"))
        self.over = sb("over", [P, E1, MAXT])
        self.cmp = sb("cmp", [P, ETILES, E])
        self.expert = sb("expert", [P, ETILES])
        self.is_e, self.val, self.val2 = (sb(x, [P, ETILES, E1]) for x in ("is_e", "val", "val2"))
        self.ex, self.total = sb("ex", [P, SEQS]), sb("total", [P, SEQS])
        self.link, self.ended, self.tabled, self.exped, self.tails, self.spare = m.sems(*(s + tag for s in (
            "tt_link", "ended", "tabled", "exped", "tails", "spare")))


def table_fill(w, engine, experts):
    m = w.m
    engine.wait_ge(w.ended, 1)
    for e in experts:
        at = engine.value_load(m.table[0:1, 2 * ETILES + e:2 * ETILES + e + 1],
                               min_val=e * REGION, max_val=e * REGION + TOK)
        engine.dma_start(m.xbuf[bass.ds(at, SLOTS), :].rearrange("(a p) c -> p a c", p=P), m.tail[:, e]
                         ).then_inc(w.tails, 16)


def table_sync(w, sp):
    m = w.m
    sp.dma_start(m.xbuf[E * REGION:].rearrange("(e a p) c -> p e a c", a=2, p=P), m.tail[:, E:]).then_inc(w.spare, 16)
    table_fill(w, sp, range(E // 2))
    sp.wait_ge(w.tails, 16 * E)
    sp.wait_ge(w.spare, 16)


def table_scalar(w, act):
    act.wait_ge(w.indexed, GROUPS)
    w.m.nc.scalar.activation(w.ex[:], w.m.diff[:], ACT.Exp).then_inc(w.exped, 1)
    table_fill(w, act, range(E // 2, E))


def table_vector(w, dve):
    m, v, E1 = w.m, w.m.nc.vector, E + 1
    exps = m.const[:, C_EXP:C_EXP + E1]
    regs = m.const[:, C_REG:C_REG + E1]
    tl = m.const[:, C_TILE:C_TILE + ETILES]
    steps = m.const[:, C_STEP:C_STEP + MAXT]
    c = Chain(m, dve, w.link)
    dve.wait_ge(w.indexed, GROUPS)
    v.tensor_copy(m.table[:, 2 * ETILES:], m.base[:, 0:E]).then_inc(w.ended, 1)
    v.memset(w.one[:], 1.0)
    c(v.tensor_tensor(w.cnt[:], m.base[:], regs, ALU.subtract))
    c(v.tensor_tensor(w.over[:], bc(w.cnt[:].unsqueeze(2), P, E1, MAXT), bc(steps.unsqueeze(1), P, E1, MAXT), ALU.is_gt))
    c(v.tensor_reduce(w.need[:], w.over[:], AX_X, ALU.add))
    c(v.tensor_tensor_scan(w.incl[:], w.one[:], w.need[:], 0.0, ALU.mult, ALU.add))
    c(v.tensor_tensor(w.excl[:], w.incl[:], w.need[:], ALU.subtract))
    c(v.scalar_tensor_tensor(out=w.delta[:], in0=w.excl[:], scalar=float(SLOTS), in1=regs,
                             op0=ALU.mult, op1=ALU.subtract))
    c(v.tensor_tensor(w.cmp[:], bc(w.incl[:, 0:E].unsqueeze(1), P, ETILES, E), bc(tl.unsqueeze(2), P, ETILES, E),
                      ALU.is_le))
    c(v.tensor_reduce(w.expert[:], w.cmp[:], AX_X, ALU.add))
    c(v.tensor_tensor(w.is_e[:], bc(w.expert[:].unsqueeze(2), P, ETILES, E1), bc(exps.unsqueeze(1), P, ETILES, E1),
                      ALU.is_equal))
    c(v.scalar_tensor_tensor(out=w.val[:], in0=bc(tl.unsqueeze(2), P, ETILES, E1), scalar=float(SLOTS),
                             in1=bc(w.delta[:].unsqueeze(1), P, ETILES, E1), op0=ALU.mult, op1=ALU.subtract))
    c(v.tensor_tensor(w.val2[:], w.val[:], w.is_e[:], ALU.mult))
    v.tensor_scalar(m.table[:, 0:ETILES], w.expert[:], float(E - 1), None, ALU.min)
    with m.nc.allow_low_precision(reason="whole numbers below 2^24"):
        v.tensor_reduce(m.table[:, ETILES:2 * ETILES], w.val2[:], AX_X, ALU.add).then_inc(w.tabled, 1)
    dve.wait_ge(w.exped, 1)
    c(v.tensor_scalar(w.total[:], w.ex[:], 1.0, None, ALU.add))
    c(v.reciprocal(m.pw[:, :, 0], w.total[:]))
    v.tensor_tensor(m.pw[:, :, 1], m.pw[:, :, 0], w.ex[:], ALU.mult)
    dve.wait_ge(w.tabled, 1)
    c(v.tensor_copy(m.base[:], regs))



def layer0(m, loads):
    nc = m.nc
    xT, WT, IG, Ws1, Ws2, Ws3, first_ld, rest_ld, x_ld = loads
    MS = SHARED
    with ExitStack() as ctx:
        sb = lambda n, s, dt=F32: m.sb(n, s, dt, ctx)
        xm = [sb(f"xm{b}", [P, GT, P]) for b in range(2)]
        y = [sb(f"y{b}", [P, GW]) for b in range(2)]
        xf = [sb(f"xf{b}", [P, GW]) for b in range(2)]
        s = [sb(f"s{q}", [P, GW]) for q in range(2)]
        h = [[sb(f"h{b}{k}", [P, GW]) for k in range(3)] for b in range(2)]
        psY = m.ps("psY", [P, 512], ctx)
        psN = m.ps("psN", [P, 2, 512], ctx)
        psO = m.ps("psO", [P, 512], ctx)
        psA = m.ps("psA", [P, 2, 512], ctx)
        psB = m.ps("psB", [P, 2, 512], ctx)
        natural_banks = [psN[:, a, 0:2 * (P + E)] for a in range(2)]
        rank = psO[:, 0:(GT + 1) * E]
        r = Router(m, ctx, "0", None)
        tiles = TileTable(m, ctx, "0", r.indexed)
        (scaled, projected, biased, clipped, nat, nat_copied, up_a, up_b, silu, gated, down,
         added) = m.sems("scaled", "projected", "biased", "clipped", "nat0", "nat_copied0",
                         "up_a", "up_b", "silu", "gated", "down", "added")
        with nc.Block() as block:
            @block.sync
            def _(sp):
                table_sync(tiles, sp)

            @block.gpsimd
            def _(pool):
                for n, b, _ in rounds(pool, GROUPS, 2):
                    route_scatter(r, pool, n, b, nat_copied)
                for b in range(2):
                    pool.wait_ge(r.scattered[b], r.sends * GROUPS // 2)

            @block.vector
            def _(dve):
                chain = Chain(m, dve, r.link, ROUTE_LINKS)

                def scale(n, b):
                    wait(dve, projected, n - 1)
                    nc.vector.tensor_tensor(
                        xm[b][:], xT[:, bass.ds(n * GW, GW)].rearrange("p (s t) -> p s t", s=GT),
                        bc(m.styles[:, bass.ds(n * GT, GT)].unsqueeze(2), P, GT, P), ALU.mult).then_inc(scaled, 1)

                def clip(n, b):
                    dve.wait_ge(biased, n + 1)
                    wait(dve, down, n - 1)
                    nc.vector.tensor_scalar(xf[b][:], y[b][:], CLAMP, -CLAMP, ALU.min, ALU.max).then_inc(clipped, 1)

                def add(n):
                    mine = bass.ds(n * GT, GT)
                    dve.wait_ge(down, n + 1)
                    nc.vector.tensor_tensor(m.X[:, mine, :], m.X[:, mine, :], psO[:].rearrange("p (s c) -> p s c", s=GT),
                                            ALU.add).then_inc(added, 1)

                def gate(n, b, k):
                    c, q = 3 * n + k, (3 * b + k) % 2
                    dve.wait_ge(up_b, c + 1)
                    dve.wait_ge(silu, c + 1)
                    wait(dve, down, n - 1)
                    nc.vector.tensor_tensor(h[b][k][0:MS[k], :], psB[0:MS[k], q, :], s[q][0:MS[k], :],
                                            ALU.mult).then_inc(gated, 1)

                dve.wait_ge(first_ld, FIRST_LOADS)
                scale(0, 0)
                scale(1, 1)
                clip(0, 0)
                for n, b, i in rounds(dve, GROUPS, 2, head=2, tail=2):
                    route_logits(r, dve, n, b, natural_banks, nat)
                    route_choose(r, dve, chain, n, b)
                    if not first(n):
                        add(n - 1)
                    gate(n, b, 0)
                    gate(n, b, 1)
                    route_index(r, dve, chain, n, b, i, rank)
                    if not is_last(n, GROUPS):
                        clip(n + 1, 1 - b)
                    gate(n, b, 2)
                    if first(n):
                        dve.wait_ge(rest_ld, 16)
                        dve.wait_ge(x_ld, 16)
                    if not late(n):
                        scale(n + 2, b)
                add(GROUPS - 1)
                table_vector(tiles, dve)

            @block.scalar
            def _(act):
                def bias(n, b):
                    act.wait_ge(projected, n + 1)
                    wait(act, clipped, n - 1)
                    for t in range(GT):
                        ins = nc.scalar.activation(y[b][:, t * P:(t + 1) * P], psY[:, t * P:(t + 1) * P], ACT.Identity,
                                                   bias=m.vec[:, V_BIAS:V_BIAS + 1],
                                                   scale=m.dcoef[:, bass.ds(n * GT + t, 1)])
                    ins.then_inc(biased, 1)

                act.wait_ge(first_ld, FIRST_LOADS)
                bias(0, 0)
                for n, b, i in rounds(act, GROUPS, 2, head=2, tail=2):
                    act.wait_ge(r.got, n + 1)
                    wait(act, r.scattered[b], r.sends * i)
                    route_rows(r, b, natural_banks, nat_copied)
                    for k in range(3):
                        c, q = 3 * n + k, (3 * b + k) % 2
                        act.wait_ge(up_a, c + 1)
                        wait(act, gated, c - 1)
                        nc.scalar.activation(s[q][0:MS[k], :], psA[0:MS[k], q, :], ACT.Silu).then_inc(silu, 1)
                        if k == 1 and not is_last(n, GROUPS):
                            bias(n + 1, 1 - b)
                table_scalar(tiles, act)

            @block.tensor
            def _(pe):
                def project(n, b):
                    pe.wait_ge(scaled, n + 1)
                    wait(pe, biased, n)
                    nc.tensor.matmul(psY[:], WT[:], xm[b][:].rearrange("p s t -> p (s t)"),
                                     start=True, stop=True).then_inc(projected, 1)

                def up(n, b, k):
                    c, q = 3 * n + k, (3 * b + k) % 2
                    wait(pe, silu, c - 1)
                    nc.tensor.matmul(psA[0:MS[k], q, :], Ws1[:, k * P:k * P + MS[k]], xf[b][:],
                                     start=True, stop=True).then_inc(up_a, 1)
                    wait(pe, gated, c - 1)
                    nc.tensor.matmul(psB[0:MS[k], q, :], Ws2[:, k * P:k * P + MS[k]], xf[b][:],
                                     start=True, stop=True).then_inc(up_b, 1)

                def natural(n, b):
                    pe.wait_ge(clipped, n + 1)
                    wait(pe, nat_copied, n)
                    for t in range(GT):
                        w = (t % 2) * (P + E)
                        ins = nc.tensor.matmul(psN[:, t // 2, w:w + P + E], xf[b][:, t * P:(t + 1) * P], IG[:],
                                               start=True, stop=True, skip_group_check=True)
                    ins.then_inc(nat, 1)

                pe.wait_ge(first_ld, FIRST_LOADS)
                project(0, 0)
                natural(0, 0)
                up(0, 0, 0)
                for n, b, _ in rounds(pe, GROUPS, 2, head=2, tail=2):
                    if not is_last(n, GROUPS):
                        project(n + 1, 1 - b)
                    up(n, b, 1)
                    wait(pe, added, n)
                    route_rank(r, pe, n, b, rank)
                    up(n, b, 2)
                    if not is_last(n, GROUPS):
                        natural(n + 1, 1 - b)
                        up(n + 1, 1 - b, 0)
                    pe.wait_ge(r.indexed, n + 1)
                    pe.wait_ge(gated, 3 * n + 3)
                    for t in range(GT):
                        for k in range(3):
                            ins = nc.tensor.matmul(psO[:, t * P:(t + 1) * P], h[b][k][0:MS[k], t * P:(t + 1) * P],
                                                   Ws3[0:MS[k], k, :], start=(k == 0), stop=(k == 2),
                                                   skip_group_check=True)
                    ins.then_inc(down, 1)



EB = 8
OB = EB // 2


def sent_before(b, i):
    return 32 * (EB // OB * i + b // OB)


def nearly(n):
    return isinstance(n, int) and n >= ETILES - 2


def turn_rows(m, pe, n, b, i, ld, xs, psT, copied, turned):
    q = b % 2
    pe.wait_ge(ld[b], 32 * (i + 1))
    wait(pe, copied, n - 1)
    for a in range(2):
        ins = m.nc.tensor.transpose(psT[:, q, a * P:(a + 1) * P], xs[b][:, a, 0:P], m.ident)
    ins.then_inc(turned, 1)


class Split:

    def __init__(self, m, ctx, tag, wide, ld, xs, raw, psT, turned, used, sent):
        self.m, self.wide, self.ld, self.xs, self.raw, self.psT = m, wide, ld, xs, raw, psT
        self.turned, self.used, self.sent = turned, used, sent
        two = lambda n, w: [m.sb(f"{n}{tag}_{q}", [P, w], F32R, ctx) for q in range(2)]
        self.xh, self.xl = two("xh", SLOTS), two("xl", SLOTS)
        self.wh, self.wl = two("wh", wide), two("wl", wide)
        self.to = [m.sb(f"to{tag}_{b}", [P, 2], U32, ctx) for b in range(OB)]
        self.w_high, self.x_high, self.copied = m.sems(f"w_high{tag}", f"x_high{tag}", f"copied{tag}")


def split_high(z, act, n, b, i):
    act.wait_ge(z.ld[b], 32 * (i + 1))
    wait(act, z.used, n - 1)
    z.m.nc.scalar.activation(z.wh[b % 2][:], z.raw[b][:, 0:z.wide], ACT.Copy).then_inc(z.w_high, 1)


def split_copy(z, dve, n, b, i):
    q, v = b % 2, z.m.nc.vector
    dve.wait_ge(z.turned, n + 1)
    wait(dve, z.used, n - 1)
    v.tensor_copy(z.xh[q][:], z.psT[:, q, 0:SLOTS]).then_inc(z.x_high, 1)
    dve.wait_ge(z.w_high, n + 1)
    v.tensor_tensor(z.wl[q][:], z.raw[b][:, 0:z.wide], z.wh[q][:].bitcast(F32), ALU.subtract)
    dve.wait_ge(z.x_high, n + 1)
    v.tensor_tensor(z.xl[q][:], z.psT[:, q, 0:SLOTS], z.xh[q][:].bitcast(F32), ALU.subtract
                    ).then_inc(z.copied, 1)


def split_places(z, dve, b, i):
    hold(z.m, dve, z.sent[b % OB], sent_before(b, i))
    z.m.nc.vector.tensor_copy(z.to[b % OB][:].unsqueeze(2), z.xs[b][:, :, P:].bitcast(U32))


def split_product(z, out, q, columns):
    w, x = (z.wh, z.wh, z.wl), (z.xh, z.xl, z.xh)
    for k in range(3):
        ins = z.m.nc.tensor.matmul(out, w[k][q][:, columns], x[k][q][:], start=(k == 0), stop=(k == 2),
                                      skip_group_check=True)
    return ins


def send_rows(m, pool, n, b, ready, out, to, sent):
    hold(m, pool, ready, n + 1)
    for a in range(2):
        pool.indirect_dma_start(
            out=m.ybuf, out_offset=bass.IndirectOffsetOnAxis(ap=to[b][:, a:a + 1], axis=0),
            in_=out[b][:, a, :], in_offset=None).then_inc(sent[b], 16)


def experts0(m, d):
    nc = m.nc
    with ExitStack() as ctx:
        sb = lambda n, s, dt=F32: m.sb(n, s, dt, ctx)
        w = [sb(f"w_{b}", [P, 4 * HALF + 2 * P]) for b in range(EB)]
        xs = [sb(f"xs{b}", [P, 2, ROW]) for b in range(EB)]
        out = [sb(f"eo{b}", [P, 2, P]) for b in range(OB)]
        s = [sb(f"es{q}", [HALF, 2, SLOTS]) for q in range(2)]
        h = [sb(f"eh{q}", [HALF, 2, SLOTS]) for q in range(2)]
        psT = m.ps("psT", [P, 2, 512], ctx)
        psA = m.ps("psA0", [P, 2, 512], ctx)
        psB = m.ps("psB0", [P, 2, 512], ctx)
        psO = m.ps("psO0", [P, 2, 512], ctx)
        m.ld = ld = [m.sem(f"e_ld{b}") for b in range(EB)]
        m.st = st = [m.sem(f"e_st{b}") for b in range(OB)]
        (turned, up_a, up_b, silu, gated, down, evac) = m.sems(
            "e0_turned", "e0_up_a", "e0_up_b", "e0_silu", "e0_gated", "e0_down", "e0_evac")
        parts = Split(m, ctx, "0", 4 * HALF, ld, xs, w, psT, turned, up_b, st)
        copied = parts.copied
        with nc.Block() as block:
            @block.sync
            def _(sp):
                for n, b, i in rounds(sp, ETILES, EB, head=EB):
                    e = sp.value_load(m.table[0:1, bass.ds(n, 1)], min_val=0, max_val=E - 1)
                    row = sp.value_load(m.table[0:1, bass.ds(n + ETILES, 1)], min_val=0, max_val=E * REGION + (E - 1) * SLOTS)
                    hold(m, sp, down, n - EB + 1)
                    hold(m, sp, copied, n - EB + 1)
                    sp.dma_start(xs[b][:], m.xbuf[bass.ds(row, SLOTS), :].rearrange("(a p) c -> p a c", p=P)
                                 ).then_inc(ld[b], 16)
                    sp.dma_start(w[b][:], d["W123"][bass.ds(e, 1)].rearrange("e p h -> (e p) h")
                                 ).then_inc(ld[b], 16)

            @block.tensor
            def _(pe):
                def up(n, b):
                    q = b % 2
                    pe.wait_ge(copied, n + 1)
                    wait(pe, silu, n - 1)
                    for a in range(2):
                        ins = split_product(parts, psA[0:HALF, q, a * SLOTS:(a + 1) * SLOTS], q,
                                            slice(a * HALF, HALF + a * HALF))
                    ins.then_inc(up_a, 1)
                    wait(pe, gated, n - 1)
                    for a in range(2):
                        ins = split_product(parts, psB[0:HALF, q, a * SLOTS:(a + 1) * SLOTS], q,
                                            slice(2 * HALF + a * HALF, 3 * HALF + a * HALF))
                    ins.then_inc(up_b, 1)

                turn_rows(m, pe, 0, 0, 0, ld, xs, psT, copied, turned)
                turn_rows(m, pe, 1, 1, 0, ld, xs, psT, copied, turned)
                up(0, 0)
                for n, b, i in rounds(pe, ETILES, EB, head=EB, tail=EB):
                    if not nearly(n):
                        turn_rows(m, pe, n + 2, (b + 2) % EB, i + (b + 2) // EB, ld, xs, psT, copied, turned)
                    if not is_last(n, ETILES):
                        up(n + 1, (b + 1) % EB)
                    q = b % 2
                    pe.wait_ge(gated, n + 1)
                    wait(pe, evac, n - 1)
                    for a in range(2):
                        for k in range(2):
                            ins = nc.tensor.matmul(psO[:, q, a * P:(a + 1) * P], h[q][:, k, a * P:(a + 1) * P],
                                                   w[b][0:HALF, 4 * HALF + k * P:4 * HALF + (k + 1) * P], start=(k == 0), stop=(k == 1), skip_group_check=True)
                    ins.then_inc(down, 1)

            @block.vector
            def _(dve):
                split_copy(parts, dve, 0, 0, 0)
                split_copy(parts, dve, 1, 1, 0)
                for n, b, i in rounds(dve, ETILES, EB, head=EB, tail=EB):
                    q = b % 2
                    split_places(parts, dve, b, i)
                    dve.wait_ge(up_b, n + 1)
                    dve.wait_ge(silu, n + 1)
                    wait(dve, down, n - 1)
                    nc.vector.tensor_tensor(h[q][:], psB[0:HALF, q, :].rearrange("p (a t) -> p a t", a=2), s[q][:],
                                            ALU.mult).then_inc(gated, 1)
                    if not nearly(n):
                        split_copy(parts, dve, n + 2, (b + 2) % EB, i + (b + 2) // EB)

            @block.scalar
            def _(act):
                def store(n, b, i):
                    act.wait_ge(down, n + 1)
                    wait(act, st[b % OB], sent_before(b, i))
                    nc.scalar.activation(out[b % OB][:], psO[:, b % 2, 0:SLOTS].rearrange("p (a c) -> p a c", a=2), ACT.Copy
                                         ).then_inc(evac, 1)

                split_high(parts, act, 0, 0, 0)
                split_high(parts, act, 1, 1, 0)
                for n, b, i in rounds(act, ETILES, EB, head=EB, tail=EB):
                    act.wait_ge(up_a, n + 1)
                    wait(act, gated, n - 1)
                    nc.scalar.activation(s[b % 2][:], psA[0:HALF, b % 2, :].rearrange("p (a t) -> p a t", a=2),
                                         ACT.Silu).then_inc(silu, 1)
                    if not nearly(n):
                        split_high(parts, act, n + 2, (b + 2) % EB, i + (b + 2) // EB)
                    if not first(n):
                        store(n - 1, (b - 1) % EB, i if b else i - 1)
                store(ETILES - 1, EB - 1, ETILES // EB - 1)

            @block.gpsimd
            def _(pool):
                for n, b, i in rounds(pool, ETILES, EB, head=EB):
                    send_rows(m, pool, n, b % OB, evac, out, parts.to, st)
                for b in range(OB):
                    pool.wait_ge(st[b], 32 * (ETILES // OB))



def fetch_rows(m, eng, n, b, rows, came, free, free_at):
    hold(m, eng, free, free_at)
    eng.dma_start(rows[b][:], m.ybuf[bass.ds(n * GT * P * TOPK, GT * P * TOPK), :].rearrange(
        "(t p k) c -> p t k c", p=P, k=TOPK)).then_inc(came[b], 16)


FB = 4


def finish(m, d, out):
    nc = m.nc
    with ExitStack() as ctx:
        rows = [m.sb(f"fr{b}", [P, GT, TOPK, P], F32, ctx) for b in range(FB)]
        part = [m.sb(f"fp{b}", [P, GT, P], F32, ctx) for b in range(FB)]
        res = [m.sb(f"fo{b}", [P, GT, P], F32, ctx) for b in range(FB)]
        halfway, summed = m.sems("f_halfway", "f_summed")
        came, stored = m.ld[0:FB], m.ld[FB:2 * FB]
        came_before = stored_before = 2 * 32 * (ETILES // EB)
        with nc.Block() as block:
            @block.sync
            def _(sp):
                for n, b, i in rounds(sp, GROUPS, FB, head=FB):
                    fetch_rows(m, sp, n, b, rows, came, summed, n - FB + 1)

            @block.vector
            def _(dve):
                for n, b, i in rounds(dve, GROUPS, FB, head=FB):
                    dve.wait_ge(came[b], came_before + 16 * (i + 1))
                    weighted(m, n, part[b], rows[b], 0, m.X[:, bass.ds(n * GT, GT), :]).then_inc(halfway, 1)
                    dve.wait_ge(halfway, n + 1)
                    wait(dve, stored[b], stored_before + 16 * i)
                    weighted(m, n, res[b], rows[b], 1, part[b][:]).then_inc(summed, 1)

            @block.scalar
            def _(act):
                for n, b, i in rounds(act, GROUPS, FB, head=FB):
                    hold(m, act, summed, n + 1)
                    act.dma_start(out[bass.ds(n * GT, GT)].rearrange("s p c -> p s c"), res[b][:]).then_inc(stored[b], 16)
                for b in range(FB):
                    act.wait_ge(stored[b], stored_before + 16 * (GROUPS // FB))



def load_pair(m, sp, n, b):
    for side, parts in ((m.qp[b], (0, 1, 0)), (m.kp[b], (2, 2, 3))):
        for r, a in enumerate(parts):
            sp.dma_start(side[32 * r:32 * r + 32].bitcast(F32),
                         m.qk_dram[a, :, bass.ds(n * PAIR, PAIR)].rearrange("(g r) t -> r g t", g=HG)
                         ).then_inc(m.pair_in[b], 16)


PRE_LINKS = 3


def pre_attention(m, d):
    nc = m.nc
    with ExitStack() as ctx:
        sb = lambda n, s, dt=F32: m.sb(n, s, dt, ctx)
        two = lambda n, s, dt=F32: [m.sb(f"{n}{b}", s, dt, ctx) for b in range(2)]
        rows = two("gr", [P, GT, TOPK, P])
        part = two("part", [P, GT, P])
        x1, x2 = two("x1_", [P, GT, P]), two("x2_", [P, GT, P])
        gbu = two("gbu", [DOWN, GT, 2 * P])
        wd, wdt = two("wd", [P, GT, DOWN]), two("wdt", [P, GT, DOWN])
        wu, wut = two("wu", [P, GT, P]), two("wut", [DOWN, GT, P])
        x1T = two("x1T", [P, GW])
        aT = two("aT", [P, GW])
        stats = two("stats", [P, GT, 6])
        mv = two("mv", [P, GT, 2])
        var, std, rstd = two("var", [P, GT]), two("std", [P, GT]), two("rstd", [P, GT])
        norm = two("norm", [P, GT, P])
        hT = two("hT", [P, GW])
        qk = two("qk", [P, 4, GW], F32R)
        psX, psD, psU = m.ps("psX", [P, 512], ctx), m.ps("psD", [P, 512], ctx), m.ps("psU", [P, 512], ctx)
        psH, psV = m.ps("psH", [P, 512], ctx), m.ps("psV", [P, 512], ctx)
        psQK = m.ps("psQK", [P, 2, 512], ctx)
        (cleared, blend1, blended, mod1, modded, turned, x1T_done, downed, relu, upped, x2_done,
         biased, link, sqrted, var_done, normed, turned2, hT_done, q_done, k_done, v_done, high, low, v_kept) = m.sems(
            "p_cleared", "p_blend1", "p_blended", "p_mod1", "p_modded", "p_turned", "p_x1T",
            "p_downed", "p_relu", "p_upped", "p_x2", "p_biased", "p_link", "p_sqrted", "p_var", "p_normed", "p_turned2",
            "p_hT", "p_q", "p_k", "p_v", "p_high", "p_low", "p_v_kept")
        came = m.sems("p_came0", "p_came1")
        gbu_in = m.sems("p_gbu0", "p_gbu1")
        qk_out = m.sems("p_qk_out0", "p_qk_out1")
        qk_view = m.qk_dram.rearrange("a p t -> p a t")
        gb_up = m.gb_dram[:, 2 * DOWN:]
        with nc.Block() as block:
            @block.sync
            def _(sp):
                def modulation(n, b):
                    hold(m, sp, modded, n - 1)
                    sp.dma_start(gbu[b][:], gb_up[bass.ds(n * GT, GT), :].unsqueeze(0).to_broadcast(
                        [DOWN, GT, 2 * P])).then_inc(gbu_in[b], 16)

                def store(n, b):
                    sp.wait_ge(high, 2 * (n + 1))
                    hold(m, sp, low, 2 * (n + 1))
                    sp.dma_start(qk_view[:, :, bass.ds(n * GW, GW)], qk[b][:].bitcast(F32)).then_inc(qk_out[b], 16)

                for n in range(3):
                    modulation(n, n % 2)
                    fetch_rows(m, sp, n, n % 2, rows, came, blended, n - 1)
                for n, b, i in rounds(sp, GROUPS, 2, head=2, tail=4):
                    if not first(n):
                        store(n - 1, 1 - b)
                    if not late(n, 3):
                        modulation(n + 3, 1 - b)
                        fetch_rows(m, sp, n + 3, 1 - b, rows, came, blended, n + 2)
                    if is_last(n, GROUPS - 3):
                        sp.wait_ge(qk_out[0], 16)
                        for pair in range(2):
                            load_pair(m, sp, pair, pair)
                store(GROUPS - 1, 1)
                for b in range(2):
                    sp.wait_ge(qk_out[b], 16 * GROUPS // 2)

            @block.gpsimd
            def _(pool):
                def keep(n, b):
                    mine = bass.ds(n * GT, GT)
                    pool.wait_ge(x2_done, n + 1)
                    nc.gpsimd.tensor_copy(m.X[:, mine, :], x1[b][:])
                    nc.gpsimd.tensor_tensor(m.X3[:, mine, :], x2[b][:], bc(m.rows[:, R_BO:R_BO + P].unsqueeze(1), P, GT, P),
                                            ALU.add).then_inc(biased, 1)

                def modulate(n, b, i):
                    gd = m.gbD[:, bass.ds(n * GT, GT), :]
                    pool.wait_ge(gbu_in[b], 16 * (i + 1))
                    wait(pool, upped, n - 1)
                    nc.gpsimd.tensor_tensor(wdt[b][:], bc(m.dproj[:].unsqueeze(1), P, GT, DOWN), gd[:, :, 0:DOWN], ALU.mult)
                    nc.gpsimd.tensor_tensor(wut[b][:], bc(m.uproj[:].unsqueeze(1), DOWN, GT, P), gbu[b][:, :, 0:P],
                                            ALU.mult).then_inc(mod1, 1)
                    pool.wait_ge(mod1, n + 1)
                    nc.gpsimd.tensor_tensor(wd[b][:], wdt[b][:], gd[:, :, DOWN:], ALU.add)
                    nc.gpsimd.tensor_tensor(wu[b][0:DOWN], wut[b][:], gbu[b][:, :, P:], ALU.add).then_inc(modded, 1)

                for b in range(2):
                    nc.gpsimd.memset(aT[b][:], 0.0)
                    nc.gpsimd.memset(wu[b][:], 0.0).then_inc(cleared, 1)
                pool.wait_ge(m.late_ld, LATE_LOADS)
                pool.wait_ge(m.gb_in, 16)
                pool.wait_ge(cleared, 2)
                modulate(0, 0, 0)
                modulate(1, 1, 0)
                for n, b, i in rounds(pool, GROUPS, 2, head=2, tail=2):
                    keep(n, b)
                    if not late(n):
                        modulate(n + 2, b, i + 1)

            @block.vector
            def _(dve):
                chain = Chain(m, dve, link, PRE_LINKS)

                def blend(n, b, i):
                    dve.wait_ge(came[b], 16 * (i + 1))
                    wait(dve, biased, n - 1)
                    weighted(m, n, part[b], rows[b], 0, m.X[:, bass.ds(n * GT, GT), :]).then_inc(blend1, 1)
                    dve.wait_ge(blend1, n + 1)
                    wait(dve, turned, n - 1)
                    weighted(m, n, x1[b], rows[b], 1, part[b][:]).then_inc(blended, 1)

                def lows(n, b):
                    for w in range(2):
                        dve.wait_ge(high, 2 * n + w + 1)
                        nc.vector.scalar_tensor_tensor(
                            out=qk[b][:, 2 * w + 1, :], in0=psQK[:, w, :], scalar=m.vec[:, V_BQ + w:V_BQ + w + 1],
                            in1=qk[b][:, 2 * w, :].bitcast(F32), op0=ALU.add, op1=ALU.subtract).then_inc(low, 1)

                def values(n):
                    dve.wait_ge(v_done, n + 1)
                    nc.vector.tensor_tensor(m.V[:, bass.ds(n * GT, GT), :], psV[:].rearrange("p (t c) -> p t c", t=GT),
                                            bc(m.rows[:, R_BV:R_BV + P].unsqueeze(1), P, GT, P), ALU.add
                                            ).then_inc(v_kept, 1)

                dve.wait_ge(m.late_ld, LATE_LOADS)
                for n in range(2):
                    blend(n, n, 0)
                for n, b, i in rounds(dve, GROUPS, 2, head=2, tail=2):
                    chain.begin(n)
                    mine = bass.ds(n * GT, GT)
                    dve.wait_ge(upped, n + 1)
                    wait(dve, biased, n - 1)
                    nc.vector.tensor_tensor(x2[b][:], psU[:].rearrange("p (t c) -> p t c", t=GT), x1[b][:],
                                            ALU.add).then_inc(x2_done, 1)
                    dve.wait_ge(x2_done, n + 1)
                    layernorm(m, dve, chain, n, lambda t: x2[b][:, t, :], stats[b], mv[b], var[b], var_done, std[b], sqrted, rstd[b], norm[b],
                              turned2, normed)
                    if not first(n):
                        lows(n - 1, 1 - b)
                    if not late(n):
                        blend(n + 2, b, i + 1)
                    if not first(n):
                        values(n - 1)
                lows(GROUPS - 1, 1)
                values(GROUPS - 1)

            @block.scalar
            def _(act):
                def turned_x1(n, b):
                    act.wait_ge(turned, n + 1)
                    wait(act, downed, n - 1)
                    nc.scalar.activation(x1T[b][:], psX[:], ACT.Copy).then_inc(x1T_done, 1)

                def adapter(n, b):
                    act.wait_ge(downed, n + 1)
                    wait(act, upped, n - 1)
                    nc.scalar.activation(aT[b][0:DOWN, :], psD[0:DOWN, :], ACT.Relu).then_inc(relu, 1)

                def high_part(n, b, i, w, ready):
                    if w == 0:
                        wait(act, qk_out[b], 16 * i)
                    act.wait_ge(ready, n + 1)
                    nc.scalar.activation(qk[b][:, 2 * w, :], psQK[:, w, :], ACT.Identity,
                                         bias=m.vec[:, V_BQ + w:V_BQ + w + 1]).then_inc(high, 1)

                act.wait_ge(cleared, 2)
                turned_x1(0, 0)
                adapter(0, 0)
                for n, b, i in rounds(act, GROUPS, 2, head=4, tail=2):
                    before = (n - 1, 1 - b, i if b else i - 1)
                    if not is_last(n, GROUPS):
                        turned_x1(n + 1, 1 - b)
                    if not first(n):
                        high_part(*before, 0, q_done)
                    act.wait_ge(var_done, n + 1)
                    nc.scalar.activation(std[b][:], var[b][:], ACT.Sqrt).then_inc(sqrted, 1)
                    if not is_last(n, GROUPS):
                        adapter(n + 1, 1 - b)
                    if not first(n):
                        high_part(*before, 1, k_done)
                    act.wait_ge(turned2, n + 1)
                    wait(act, v_done, n - 1)
                    nc.scalar.activation(hT[b][:], psH[:], ACT.Identity, bias=m.vec[:, V_LN1B:V_LN1B + 1],
                                         scale=m.vec[:, V_LN1G:V_LN1G + 1]).then_inc(hT_done, 1)
                high_part(GROUPS - 1, 1, GROUPS // 2 - 1, 0, q_done)
                high_part(GROUPS - 1, 1, GROUPS // 2 - 1, 1, k_done)

            @block.tensor
            def _(pe):
                def turn(n, b):
                    pe.wait_ge(blended, n + 1)
                    wait(pe, x1T_done, n)
                    for t in range(GT):
                        ins = nc.tensor.transpose(psX[:, t * P:(t + 1) * P], x1[b][:, t, :], m.ident)
                    ins.then_inc(turned, 1)

                def down(n, b):
                    pe.wait_ge(x1T_done, n + 1)
                    pe.wait_ge(modded, n + 1)
                    wait(pe, relu, n)
                    for t in range(GT):
                        ins = nc.tensor.matmul(psD[0:DOWN, t * P:(t + 1) * P], wd[b][:, t, :], x1T[b][:, t * P:(t + 1) * P],
                                               start=True, stop=True, skip_group_check=True)
                    ins.then_inc(downed, 1)

                def up(n, b):
                    pe.wait_ge(relu, n + 1)
                    wait(pe, x2_done, n)
                    for t in range(GT):
                        ins = nc.tensor.matmul(psU[:, t * P:(t + 1) * P], aT[b][:, t * P:(t + 1) * P], wu[b][:, t, :],
                                               start=True, stop=True, skip_group_check=True)
                    ins.then_inc(upped, 1)

                def turn_norm(n, b):
                    pe.wait_ge(normed, n + 1)
                    wait(pe, hT_done, n)
                    for t in range(GT):
                        ins = nc.tensor.transpose(psH[:, t * P:(t + 1) * P], norm[b][:, t, :], m.ident)
                    ins.then_inc(turned2, 1)

                def query_key(n, b, w, ready):
                    pe.wait_ge(hT_done, n + 1)
                    wait(pe, low, 2 * n - 1 + w)
                    nc.tensor.matmul(psQK[:, w, :], m.wqkv[:, w * P:(w + 1) * P], hT[b][:], start=True, stop=True
                                     ).then_inc(ready, 1)

                def value(n, b):
                    wait(pe, v_kept, n)
                    for t in range(GT):
                        ins = nc.tensor.matmul(psV[:, t * P:(t + 1) * P], hT[b][:, t * P:(t + 1) * P], m.wqkv[:, 2 * P:],
                                               start=True, stop=True, skip_group_check=True)
                    ins.then_inc(v_done, 1)

                pe.wait_ge(m.late_ld, LATE_LOADS)
                turn(0, 0)
                down(0, 0)
                up(0, 0)
                for n, b, i in rounds(pe, GROUPS, 2, head=2, tail=2):
                    more = not is_last(n, GROUPS)
                    if more:
                        turn(n + 1, 1 - b)
                    if not first(n):
                        query_key(n - 1, 1 - b, 0, q_done)
                    if more:
                        down(n + 1, 1 - b)
                    if not first(n):
                        query_key(n - 1, 1 - b, 1, k_done)
                    if more:
                        up(n + 1, 1 - b)
                    turn_norm(n, b)
                    if not first(n):
                        value(n - 1, 1 - b)
                query_key(GROUPS - 1, 1, 0, q_done)
                query_key(GROUPS - 1, 1, 1, k_done)
                value(GROUPS - 1, 1)


def weighted(m, n, out, rows, k, plus):
    for t in range(GT):
        ins = m.nc.vector.scalar_tensor_tensor(
            out=out[:, t, :], in0=rows[:, t, k, :],
            scalar=m.pw[:, bass.ds(n * GT + t, 1), k:k + 1].rearrange("p a k -> p (a k)"),
            in1=plus[:, t, :], op0=ALU.mult, op1=ALU.add)
    return ins


def layernorm(m, dve, chain, n, at, stats, mv, var, var_done, std, sqrted, rstd, norm, used, normed):
    nc = m.nc
    for t in range(GT):
        ins = nc.vector.bn_stats(stats[:, t, :], at(t))
    chain(ins)
    for t in range(GT):
        ins = nc.vector.bn_aggr(mv[:, t, :], stats[:, t, :])
    chain(ins)
    nc.vector.tensor_scalar(var[:], mv[:, :, 1], EPS, None, ALU.add).then_inc(var_done, 1)
    dve.wait_ge(sqrted, n + 1)
    chain(nc.vector.reciprocal(rstd[:], std[:]))
    wait(dve, used, n - 1)
    for t in range(GT):
        ins = nc.vector.tensor_scalar(norm[:, t, :], at(t), mv[:, t, 0:1], rstd[:, t:t + 1], ALU.subtract, ALU.mult)
    ins.then_inc(normed, 1)



KM_POOL = 1


LAST_GROUPS = ((GROUPS - 2, 1, 0), (GROUPS - 1, 0, GROUPS - 2))


class Post:

    def __init__(self, m, ctx, bank_a, bank_b):
        self.m, self.bank_a, self.bank_b = m, bank_a, bank_b
        sb = lambda n, s, dt=F32: m.sb(n, s, dt, ctx)
        self.stats, self.mv = sb("stats2", [P, GT, 6]), sb("mv2", [P, GT, 2])
        self.var, self.rstd, self.minus_half = sb("var2", [P, GT]), sb("rstd2", [P, GT]), sb("minus_half", [P, GT])
        self.norm = sb("norm2", [P, GT, P])
        self.hT = sb("h2T", [P, GW])
        self.router = Router(m, ctx, "1", m.rows[:, R_GB:R_GB + E])
        self.natural_banks = [bank_a[:, 0:2 * (P + E)], bank_b[:, 0:2 * (P + E)]]
        self.rank_out = bank_a[:, 0:(GT + 1) * E]
        (self.link, self.var_done, self.rooted, self.normed, self.turned, self.hT_done, self.nat, self.nat_copied,
         self.rows_done) = m.sems("q_link", "q_var", "q_rooted", "q_normed", "q_turned", "q_hT", "q_nat",
                                  "q_nat_copied", "q_rows")


def post_chains(q, dve):
    q.ln = Chain(q.m, dve, q.link, 2)
    q.choices = Chain(q.m, dve, q.router.link, ROUTE_LINKS)


def post_stream(q, n, t):
    return q.m.X3[:, bass.ds(n * GT + t, 1), :].rearrange("p a c -> p (a c)")


def post_variances(q, dve, n, kept):
    v = q.m.nc.vector
    q.ln.begin(n)
    hold(q.m, dve, kept, GT * (n + 1))
    for t in range(GT):
        ins = v.bn_stats(q.stats[:, t, :], post_stream(q, n, t))
    q.ln(ins)
    for t in range(GT):
        ins = v.bn_aggr(q.mv[:, t, :], q.stats[:, t, :])
    q.ln(ins)
    wait(dve, q.rooted, n)
    v.tensor_scalar(q.var[:], q.mv[:, :, 1], EPS, None, ALU.add).then_inc(q.var_done, 1)


def post_root(q, pool, n):
    pool.wait_ge(q.var_done, n + 1)
    wait(pool, q.normed, n)
    q.m.nc.gpsimd.tensor_tensor(q.rstd[:], q.var[:], q.minus_half[:], ALU.pow).then_inc(q.rooted, 1)


def post_join(q, pool, n):
    m, mine = q.m, bass.ds(n * GT, GT)
    m.nc.gpsimd.tensor_tensor(m.X[:, mine, :], m.X[:, mine, :], m.X3[:, mine, :], ALU.add)


def post_normalise(q, dve, n):
    dve.wait_ge(q.rooted, n + 1)
    wait(dve, q.turned, n)
    for t in range(GT):
        ins = q.m.nc.vector.tensor_scalar(q.norm[:, t, :], post_stream(q, n, t), q.mv[:, t, 0:1],
                                             q.rstd[:, t:t + 1], ALU.subtract, ALU.mult)
    ins.then_inc(q.normed, 1)


def post_turn(q, pe, n):
    pe.wait_ge(q.normed, n + 1)
    for t in range(GT):
        ins = q.m.nc.tensor.transpose(q.bank_b[:, t * P:(t + 1) * P], q.norm[:, t, :], q.m.ident)
    ins.then_inc(q.turned, 1)


def post_scale(q, act, n):
    act.wait_ge(q.turned, n + 1)
    wait(act, q.nat, n)
    q.m.nc.scalar.activation(q.hT[:], q.bank_b[:], ACT.Identity, bias=q.m.vec[:, V_LN2B:V_LN2B + 1],
                                scale=q.m.vec[:, V_LN2G:V_LN2G + 1]).then_inc(q.hT_done, 1)


def post_natural(q, pe, n, banks):
    pe.wait_ge(q.hT_done, n + 1)
    for t in range(GT):
        w = (t % 2) * (P + E)
        ins = q.m.nc.tensor.matmul(banks[t // 2][:, w:w + P + E], q.hT[:, t * P:(t + 1) * P], q.m.IG[:],
                                   start=True, stop=True, skip_group_check=True)
    ins.then_inc(q.nat, 1)


def post_logits(q, dve, n, b, banks):
    route_logits(q.router, dve, n, b, banks, q.nat)


def post_rows(q, act, n, b, i, banks):
    act.wait_ge(q.router.got, n + 1)
    wait(act, q.router.scattered[b], q.router.sends * i)
    route_rows(q.router, b, banks, q.nat_copied, copies=1)


def post_rows_again(q, act, n, b):
    row = q.router.row[b]
    act.wait_ge(q.nat_copied, n + 1)
    q.m.nc.scalar.activation(row[:, :, 1, 0:P], row[:, :, 0, 0:P], ACT.Copy).then_inc(q.rows_done, 1)


def post_choose(q, dve, n, b):
    route_choose(q.router, dve, q.choices, n, b)


def post_rank(q, pe, n, b, out):
    route_rank(q.router, pe, n, b, out)


def post_index(q, dve, n, b, i, ranks):
    route_index(q.router, dve, q.choices, n, b, i, ranks)


def post_scatter(q, pool, n, b, part=range(GT * TOPK)):
    route_scatter(q.router, pool, n, b, q.rows_done, part)


def due(n):
    return not isinstance(n, int) or n >= 0


def soon(s, behind=2):
    return isinstance(s, int) and s < behind


def attention_loads(m, ctx):
    m.qp, m.kp = ([m.sb(f"{x}{b}", [96, HG, PAIR], F32R, ctx) for b in range(2)] for x in ("qp", "kp"))
    m.pair_in = m.sems("a_pair0", "a_pair1")


def attention(m, d):
    nc = m.nc
    with ExitStack() as ctx:
        sb = lambda n, s, dt=F32: m.sb(n, s, dt, ctx)
        two = lambda n, s, dt=F32: [m.sb(f"{n}{b}", s, dt, ctx) for b in range(2)]
        selr = sb("selr", [P, HG, P], F32R)
        qp, kp, pair_in = m.qp, m.kp, m.pair_in
        qm = two("qm", [96, HG, 4, PAIR], F32R)
        km = two("km", [96, HG, 4, P], F32R)
        vb = two("vb", [P, HEADS, 32])
        mneg = two("mneg", [P, HG, 4])
        xm = two("xmx", [P, 4, P])
        mxT = two("mxT", [P, 4 * P], F32R)
        prob = two("prob", [P, HG, 4 * P])
        rec = two("rec", [P, P])
        oT = two("oT", [P, P])
        ps1, ps2 = m.ps("ps1", [P, 2, 512], ctx), m.ps("ps2", [P, 2, 512], ctx)
        psM, psW = m.ps("psM", [P, 512], ctx), m.ps("psW", [P, 512], ctx)
        psO = m.ps("psAO", [P, 2, 512], ctx)
        (cleared, made, km_pool, km_act, vb_done, scored, maxed, link, parted, turned, mxT_done, shifted,
         exped, mixed, divided, projected, kept) = m.sems(
            "a_cleared", "a_made", "a_km_pool", "a_km_act", "a_vb", "a_scored", "a_maxed", "a_link", "a_parted",
            "a_turned", "a_mxT", "a_shifted", "a_exped", "a_mixed", "a_divided", "a_projected", "a_kept")
        qm_in = m.sems("a_qm_in0", "a_qm_in1")
        zeroed = m.sems("a_zeroed0", "a_zeroed1")
        post = Post(m, ctx, psW, psM)
        tiles = TileTable(m, ctx, "1", post.router.indexed)
        late_banks = [ps1[:, a, 0:2 * (P + E)] for a in range(2)]
        late_rank = ps2[:, 0, 0:(GT + 1) * E]
        mask = lambda j: m.const[0:96, C_MASK + j:C_MASK + j + 1]
        tok = lambda s4: slice((s4 % 2) * P, (s4 % 2 + 1) * P)
        PAIRS = SEQS // 2

        with nc.Block() as block:
            @block.sync
            def _(sp):
                for n, b, i in rounds(sp, PAIRS, 2, head=2):
                    hold(m, sp, shifted, 8 * (n - 1))
                    hold(m, sp, km_pool, 2 * (n - 1))
                    hold(m, sp, km_act, 2 * (n - 1))
                    if not isinstance(n, int):
                        load_pair(m, sp, n, b)
                    if isinstance(n, int):
                        sp.wait_ge(zeroed[b], 1)
                    for j in range(4):
                        for r, a in enumerate((0, 1, 0)):
                            rows = slice(32 * r + 8 * j, 32 * r + 8 * j + 8)
                            source = m.qk_dram[a, :, bass.ds(n * PAIR, PAIR)].rearrange("(g j r) t -> j r g t", g=HG, j=4)[j]
                            sp.dma_start(qm[b][rows, :, j, :].bitcast(F32), source).then_inc(qm_in[b], 16)
                table_sync(tiles, sp)

            @block.gpsimd
            def _(pool):
                nc.gpsimd.memset(post.minus_half[:], -0.5)
                for b in range(2):
                    nc.gpsimd.memset(vb[b][:], 0.0)
                    nc.gpsimd.memset(xm[b][:], 0.0).then_inc(cleared, 1)
                pool.wait_ge(cleared, 2)
                def mask_k(s, u, i):
                    p, b = u % 2, u // 2
                    if p == 0:
                        pool.wait_ge(pair_in[b], 96 * (i + 1))
                    hold(m, pool, scored, 4 * (s - 1))
                    for j in range(KM_POOL):
                        ins = nc.gpsimd.tensor_scalar(km[p][:, :, j, :], kp[b][:, :, tok(u)].bitcast(F32), mask(j), None,
                                                      ALU.mult)
                    ins.then_inc(km_pool, 1)

                def spread_v(s, p):
                    wait(pool, mixed, s - 1)
                    for g in range(HG):
                        v = vb[p][:, 4 * g:4 * g + 4, :]
                        diag = bass.AP(v.tensor, v.offset, [list(v.ap[0]), [40, 4], [1, 8]])
                        ins = nc.gpsimd.tensor_copy(diag, m.V[:, bass.ds(s, 1), 32 * g:32 * g + 32].rearrange(
                            "p a (j e) -> p (a j) e", j=4))
                    ins.then_inc(vb_done, 1)

                parts = {1: range(0, 3), 2: range(3, 8)}
                for s, u, i in rounds(pool, SEQS, GT, head=3 * GT):
                    mask_k(s, u, i)
                    if u in parts and due(i - 3):
                        post_scatter(post, pool, i - 3, 0, parts[u])
                    if u == 1 and due(i - 2):
                        post_root(post, pool, i - 2)
                    if not first(s):
                        spread_v(s - 1, (u - 1) % 2)
                    if is_last(s, 2):
                        nc.gpsimd.memset(qm[1][:].bitcast(F32), 0.0).then_inc(zeroed[1], 1)
                    if u == 3 and due(i - 2):
                        post_join(post, pool, i - 2)
                spread_v(SEQS - 1, 1)
                post_scatter(post, pool, GROUPS - 3, 0, parts[1])
                post_root(post, pool, GROUPS - 2)
                post_scatter(post, pool, GROUPS - 3, 0, parts[2])
                post_join(post, pool, GROUPS - 2)
                post_scatter(post, pool, GROUPS - 2, 1, parts[1])
                post_root(post, pool, GROUPS - 1)
                post_scatter(post, pool, GROUPS - 2, 1, parts[2])
                post_join(post, pool, GROUPS - 1)
                post_scatter(post, pool, GROUPS - 1, 0)
                pool.wait_ge(post.router.scattered[0], post.router.sends * (GROUPS - 1))
                pool.wait_ge(post.router.scattered[1], post.router.sends)

            @block.vector
            def _(dve):
                def maxima(s, u, i):
                    p = u % 2
                    for g in range(HG):
                        dve.wait_ge(scored, 4 * s + g + 1)
                        ins = nc.vector.tensor_reduce(mneg[p][:, g, :], ps1[:, g % 2, :].rearrange("p (j k) -> p j k", j=4),
                                                      AX_X, ALU.max, negate=True)
                        ins.then_inc(maxed, 1)
                    dve.wait_ge(maxed, 4 * s + 4)
                    wait(dve, turned, s - 1)
                    x = xm[p][:]
                    hi, lo = (bass.AP(x.tensor, x.offset + w, [list(x.ap[0]), [32, 4], [130, 4]]) for w in range(2))
                    nc.vector.tensor_copy(hi.bitcast(F32R), mneg[p][:]).then_inc(link, 1)
                    dve.wait_ge(link, s + 1)
                    nc.vector.tensor_tensor(lo, mneg[p][:], hi, ALU.subtract).then_inc(parted, 1)

                def divide(s, u):
                    p = u % 2
                    dve.wait_ge(mixed, s + 1)
                    nc.vector.reciprocal(rec[p][:], psO[:, p, P:2 * P]).then_inc(made, 1)
                    dve.wait_ge(made, s + 1)
                    wait(dve, projected, s - 1)
                    nc.vector.tensor_tensor(oT[p][:], psO[:, p, 0:P], rec[p][:], ALU.mult).then_inc(divided, 1)

                def keep(s, u):
                    dve.wait_ge(projected, s + 1)
                    x3 = m.X3[:, bass.ds(s, 1), :].rearrange("p a c -> p (a c)")
                    nc.vector.tensor_tensor(x3, psW[:, 0:P], x3, ALU.add).then_inc(kept, 1)

                nc.vector.memset(qm[0][:].bitcast(F32), 0.0).then_inc(zeroed[0], 1)
                dve.wait_ge(cleared, 2)
                for g in range(HG):
                    ins = nc.vector.tensor_copy(selr[:, g, :], bc(m.const[:, C_SEL + g:C_SEL + g + 1], P, P))
                maxima(0, 0, 0)
                post_chains(post, dve)
                for s, u, i in rounds(dve, SEQS, GT, head=3 * GT, tail=GT):
                    nxt = (s + 1, (u + 1) % 4, i + (u + 1) // 4)
                    if not is_last(s, SEQS):
                        maxima(*nxt)
                    if u == 2 and due(i - 2):
                        post_logits(post, dve, i - 2, 0, post.natural_banks)
                    if u == 3 and due(i - 2):
                        post_index(post, dve, i - 2, 0, i - 2, post.rank_out)
                    if not soon(s):
                        divide(s - 2, u)
                    if not soon(s, 3):
                        keep(s - 3, u)
                    if u == 0 and due(i - 2):
                        post_normalise(post, dve, i - 2)
                    if u == 2 and due(i - 2):
                        post_choose(post, dve, i - 2, 0)
                    if u == 3 and due(i - 1):
                        post_variances(post, dve, i - 1, kept)
                n, b, i = LAST_GROUPS[0]
                post_normalise(post, dve, n)
                divide(SEQS - 2, 0)
                keep(SEQS - 3, 1)
                post_logits(post, dve, n, b, late_banks)
                post_choose(post, dve, n, b)
                divide(SEQS - 1, 1)
                keep(SEQS - 2, 0)
                post_index(post, dve, n, b, i, late_rank)
                keep(SEQS - 1, 1)
                post_variances(post, dve, n + 1, kept)
                n, b, i = LAST_GROUPS[1]
                post_normalise(post, dve, n)
                post_logits(post, dve, n, b, late_banks)
                post_choose(post, dve, n, b)
                post_index(post, dve, n, b, i, late_rank)
                table_vector(tiles, dve)

            @block.scalar
            def _(act):
                def copy_max(s, u):
                    act.wait_ge(turned, s + 1)
                    wait(act, shifted, 4 * (s - 1))
                    nc.scalar.activation(mxT[u % 2][:], psM[:], ACT.Copy).then_inc(mxT_done, 1)

                def mask_k(s, u, i):
                    p, b = u % 2, u // 2
                    if p == 0:
                        act.wait_ge(pair_in[b], 96 * (i + 1))
                    wait(act, scored, 4 * (s - 1))
                    for j in range(KM_POOL, 4):
                        ins = nc.scalar.activation(km[p][:, :, j, :], kp[b][:, :, tok(u)].bitcast(F32), ACT.Copy,
                                                   scale=mask(j))
                    ins.then_inc(km_act, 1)

                mask_k(0, 0, 0)
                mask_k(1, 1, 0)
                copy_max(0, 0)
                for s, u, i in rounds(act, SEQS, GT, head=3 * GT, tail=GT):
                    p = u % 2
                    wait(act, mixed, s - 1)
                    for g in range(HG):
                        act.wait_ge(shifted, 4 * s + g + 1)
                        nc.scalar.activation(prob[p][:, g, :], ps2[:, g % 2, :], ACT.Exp, scale=ATT_SCALE
                                             ).then_inc(exped, 1)
                    if u == 1 and due(i - 2):
                        post_scale(post, act, i - 2)
                    if u == 2 and due(i - 2):
                        post_rows(post, act, i - 2, 0, i - 2, post.natural_banks)
                    if not (isinstance(s, int) and s >= SEQS - 2):
                        mask_k(s + 2, (u + 2) % 4, i + (u + 2) // 4)
                    if not is_last(s, SEQS):
                        copy_max(s + 1, u + 1)
                    if u == 2 and due(i - 2):
                        post_rows_again(post, act, i - 2, 0)
                for n, b, i in LAST_GROUPS:
                    post_scale(post, act, n)
                    post_rows(post, act, n, b, i, late_banks)
                    post_rows_again(post, act, n, b)
                table_scalar(tiles, act)

            @block.tensor
            def _(pe):
                def score(s, u, i, g):
                    p, b = u % 2, u // 2
                    wait(pe, maxed, 4 * s + g - 1)
                    nc.tensor.matmul(ps1[:, g % 2, :], qp[b][:, g, tok(u)], km[p][:, g].rearrange("p j k -> p (j k)"),
                                     start=True, stop=True).then_inc(scored, 1)

                def shift(s, u, g):
                    p, b = u % 2, u // 2
                    wait(pe, exped, 4 * s + g - 1)
                    nc.tensor.matmul(ps2[:, g % 2, :].rearrange("p (j k) -> p j k", j=4), kp[b][:, g, tok(u)], qm[b][:, g, :, tok(u)],
                                     start=True, stop=False)
                    nc.tensor.matmul(ps2[:, g % 2, :], selr[:, g, :], mxT[p][:], start=False, stop=True
                                     ).then_inc(shifted, 1)

                def turn_max(s, u):
                    pe.wait_ge(parted, s + 1)
                    wait(pe, mxT_done, s)
                    for j in range(4):
                        ins = nc.tensor.transpose(psM[:, j * P:(j + 1) * P], xm[u % 2][:, j, :], m.ident)
                    ins.then_inc(turned, 1)

                def mix(s, u):
                    p = u % 2
                    pe.wait_ge(exped, 4 * s + 4)
                    pe.wait_ge(vb_done, s + 1)
                    wait(pe, divided, s - 1)
                    for j in range(4):
                        for g in range(HG):
                            nc.tensor.matmul(psO[32 * g:32 * g + 32, p, 0:P], vb[p][:, 4 * g + j, :],
                                             prob[p][:, g, j * P:(j + 1) * P], start=(j == 0), stop=(j == 3),
                                             skip_group_check=True)

                def total(s, u):
                    p = u % 2
                    for j in range(4):
                        for g in range(HG):
                            ins = nc.tensor.matmul(psO[32 * g:32 * g + 32, p, P:2 * P],
                                                   m.const[:, C_ONESB + 32 * j:C_ONESB + 32 * j + 32],
                                                   prob[p][:, g, j * P:(j + 1) * P], start=(j == 0), stop=(j == 3),
                                                   skip_group_check=True)
                    ins.then_inc(mixed, 1)

                def project(s, u):
                    pe.wait_ge(divided, s + 1)
                    wait(pe, kept, s)
                    nc.tensor.matmul(psW[:, 0:P], oT[u % 2][:], m.wo[:], start=True, stop=True).then_inc(projected, 1)

                def ready(s, u, i):
                    if u % 2 == 0:
                        pe.wait_ge(pair_in[u // 2], 96 * (i + 1))
                    pe.wait_ge(km_pool, s + 1)
                    pe.wait_ge(km_act, s + 1)

                ready(0, 0, 0)
                for g in range(HG):
                    score(0, 0, 0, g)
                turn_max(0, 0)
                for s, u, i in rounds(pe, SEQS, GT, head=3 * GT, tail=GT):
                    nxt = (s + 1, (u + 1) % 4, i + (u + 1) // 4)
                    more = not is_last(s, SEQS)
                    if more:
                        ready(*nxt)
                    for g in range(HG):
                        if more:
                            score(*nxt, g)
                        if g == 0:
                            if u % 2 == 0:
                                pe.wait_ge(qm_in[u // 2], 16 * 12 * (i + 1))
                            pe.wait_ge(mxT_done, s + 1)
                        shift(s, u, g)
                    if u == 1 and due(i - 2):
                        post_turn(post, pe, i - 2)
                    if u > 1 and due(i - 2):
                        pe.wait_ge(kept, s - 3)
                        if u == 2:
                            post_natural(post, pe, i - 2, post.natural_banks)
                        else:
                            post_rank(post, pe, i - 2, 0, post.rank_out)
                    elif not soon(s, 3):
                        project(s - 3, u + 1)
                    if not first(s):
                        mix(s - 1, u - 1)
                    if u == 2 and due(i - 2):
                        pe.wait_ge(post.nat_copied, i - 1)
                        project(s - 3, u + 1)
                    if u == 3 and due(i - 2):
                        pe.wait_ge(post.router.indexed, i - 1)
                        project(s - 3, u + 1)
                    if u == 1 and due(i - 2):
                        pe.wait_ge(post.hT_done, i - 1)
                    if more:
                        turn_max(s + 1, u + 1)
                    if not first(s):
                        total(s - 1, u - 1)
                project(SEQS - 3, 1)
                mix(SEQS - 1, 1)
                pe.wait_ge(mxT_done, SEQS)
                post_turn(post, pe, GROUPS - 2)
                total(SEQS - 1, 1)
                pe.wait_ge(maxed, HG * SEQS)
                pe.wait_ge(exped, HG * SEQS)
                post_natural(post, pe, GROUPS - 2, late_banks)
                project(SEQS - 2, 0)
                post_rank(post, pe, GROUPS - 2, 1, late_rank)
                project(SEQS - 1, 1)
                pe.wait_ge(post.hT_done, GROUPS - 1)
                post_turn(post, pe, GROUPS - 1)
                pe.wait_ge(post.nat_copied, GROUPS - 1)
                post_natural(post, pe, GROUPS - 1, late_banks)
                post_rank(post, pe, GROUPS - 1, 0, late_rank)



def experts1(m, d):
    nc = m.nc
    WIDE = KT1 * P
    with ExitStack() as ctx:
        sb = lambda n, s, dt=F32: m.sb(n, s, dt, ctx)
        wb = [sb(f"wb{b}", [P, 2 * WIDE + KT1 + P]) for b in range(EB)]
        b2 = [w[:, 2 * WIDE + KT1:] for w in wb]
        xs = [sb(f"xt{b}", [P, 2, ROW]) for b in range(EB)]
        out = [sb(f"fo_{b}", [P, 2, P]) for b in range(OB)]
        h = [sb(f"fh{q}", [P, KT1, SLOTS]) for q in range(2)]
        psT = m.ps("psT1", [P, 2, 512], ctx)
        psA = m.ps("psA1", [P, 4, 512], ctx)
        psO = m.ps("psO1", [P, 2, 512], ctx)
        ld, st = m.ld, m.st
        past = ETILES // EB
        turned, up_a, up_b, relu_a, relu_b, down, evac = m.sems(
            "e1_turned", "e1_up_a", "e1_up_b", "e1_relu_a", "e1_relu_b", "e1_down", "e1_evac")
        parts = Split(m, ctx, "1", WIDE, ld, xs, wb, psT, turned, up_b, st)
        copied = parts.copied
        with nc.Block() as block:
            @block.sync
            def _(sp):
                for n, b, i in rounds(sp, ETILES, EB, head=EB):
                    e = sp.value_load(m.table[0:1, bass.ds(n, 1)], min_val=0, max_val=E - 1)
                    row = sp.value_load(m.table[0:1, bass.ds(n + ETILES, 1)], min_val=0, max_val=E * REGION + (E - 1) * SLOTS)
                    hold(m, sp, down, n - EB + 1)
                    hold(m, sp, copied, n - EB + 1)
                    hold(m, sp, evac, n - EB + 1)
                    sp.dma_start(xs[b][:], m.xbuf[bass.ds(row, SLOTS), :].rearrange("(a p) c -> p a c", p=P)
                                 ).then_inc(ld[b], 16)
                    sp.dma_start(wb[b][:], d["W1b"][bass.ds(e, 1)].rearrange("e p h -> (e p) h")).then_inc(ld[b], 16)

            @block.tensor
            def _(pe):
                def up(n, b):
                    q = b % 2
                    pe.wait_ge(copied, n + 1)
                    for half, free, done in ((0, relu_a, up_a), (1, relu_b, up_b)):
                        wait(pe, free, 2 * (n - 1))
                        for a in range(2):
                            k = 2 * half + a
                            ins = split_product(parts, psA[:, 2 * q + half, a * SLOTS:(a + 1) * SLOTS], q,
                                                slice(k * P, (k + 1) * P))
                        ins.then_inc(done, 1)

                turn_rows(m, pe, 0, 0, past, ld, xs, psT, copied, turned)
                turn_rows(m, pe, 1, 1, past, ld, xs, psT, copied, turned)
                up(0, 0)
                for n, b, i in rounds(pe, ETILES, EB, head=EB, tail=EB):
                    if not nearly(n):
                        turn_rows(m, pe, n + 2, (b + 2) % EB, i + (b + 2) // EB + past, ld, xs, psT, copied, turned)
                    if not is_last(n, ETILES):
                        up(n + 1, (b + 1) % EB)
                    q = b % 2
                    pe.wait_ge(relu_a, 2 * (n + 1))
                    pe.wait_ge(relu_b, 2 * (n + 1))
                    wait(pe, evac, n - 1)
                    for a in range(2):
                        for k in range(KT1):
                            ins = nc.tensor.matmul(psO[:, q, a * P:(a + 1) * P], h[q][:, k, a * P:(a + 1) * P],
                                                   wb[b][:, WIDE + k * P:WIDE + (k + 1) * P],
                                                   start=(k == 0), stop=(k == KT1 - 1), skip_group_check=True)
                    ins.then_inc(down, 1)

            @block.vector
            def _(dve):
                def leave(n, b, i):
                    dve.wait_ge(down, n + 1)
                    wait(dve, st[b % OB], sent_before(b, i))
                    nc.vector.tensor_tensor(out[b % OB][:], psO[:, b % 2, 0:SLOTS].rearrange("p (a c) -> p a c", a=2),
                                            bc(b2[b].unsqueeze(1), P, 2, P), ALU.add).then_inc(evac, 1)

                split_copy(parts, dve, 0, 0, past)
                split_copy(parts, dve, 1, 1, past)
                for n, b, i in rounds(dve, ETILES, EB, head=EB, tail=EB):
                    q = b % 2
                    split_places(parts, dve, b, i + past)
                    dve.wait_ge(up_b, n + 1)
                    wait(dve, down, n - 1)
                    for a in range(2):
                        nc.vector.tensor_scalar(h[q][:, 2 + a, :], psA[:, 2 * q + 1, a * SLOTS:(a + 1) * SLOTS],
                                                wb[b][:, 2 * WIDE + 2 + a:2 * WIDE + 3 + a], 0.0, ALU.add, ALU.max
                                                ).then_inc(relu_b, 1)
                    if not nearly(n):
                        split_copy(parts, dve, n + 2, (b + 2) % EB, i + (b + 2) // EB + past)
                    if not first(n):
                        leave(n - 1, (b - 1) % EB, (i if b else i - 1) + past)
                leave(ETILES - 1, EB - 1, 2 * past - 1)

            @block.gpsimd
            def _(pool):
                for n, b, i in rounds(pool, ETILES, EB, head=EB):
                    send_rows(m, pool, n, b % OB, evac, out, parts.to, st)
                for b in range(OB):
                    pool.wait_ge(st[b], 2 * 32 * (ETILES // OB))

            @block.scalar
            def _(act):
                split_high(parts, act, 0, 0, past)
                split_high(parts, act, 1, 1, past)
                for n, b, i in rounds(act, ETILES, EB, head=EB, tail=EB):
                    q = b % 2
                    act.wait_ge(up_a, n + 1)
                    wait(act, down, n - 1)
                    for a in range(2):
                        nc.scalar.activation(h[q][:, a, :], psA[:, 2 * q, a * SLOTS:(a + 1) * SLOTS], ACT.Relu,
                                             bias=wb[b][:, 2 * WIDE + a:2 * WIDE + a + 1]).then_inc(relu_a, 1)
                    if not nearly(n):
                        split_high(parts, act, n + 2, (b + 2) % EB, i + (b + 2) // EB + past)



def build(nc, d, out):
    with ExitStack() as ctx:
        m = Machine(nc, ctx)
        allocate(m, d)
        with ExitStack() as front:
            loads = layer0_loads(m, front)
            setup(m, d, loads)
            layer0(m, loads)
        experts0(m, d)
        with ExitStack() as middle:
            attention_loads(m, middle)
            pre_attention(m, d)
            attention(m, d)
        experts1(m, d)
        finish(m, d, out)



def laid_out(a):
    x = np.ascontiguousarray(a["x"]).reshape(TOK, P)
    W3 = a["L0_ffn_W3"].reshape(E, 2, HALF, P).transpose(0, 2, 1, 3).reshape(E, HALF, 2 * P)
    W2b = a["L1_ffn_W2"].reshape(E, KT1, P, P).transpose(0, 2, 1, 3).reshape(E, P, KT1 * P)
    b1 = a["L1_ffn_b1"].reshape(E, KT1, P).transpose(0, 2, 1)
    W3 = np.concatenate([W3, np.zeros((E, P - HALF, 2 * P), W3.dtype)], axis=1)
    b2 = np.broadcast_to(a["L1_ffn_b2"][:, None, :], (E, P, P))
    b_qkv = a["L1_ffn_b_qkv"]
    vec = [a["L0_cond_bias"], a["L0_cond_affine_b"], a["L1_ffn_ln1_g"], a["L1_ffn_ln1_b"], a["L1_ffn_ln2_g"],
           a["L1_ffn_ln2_b"], b_qkv[0:P], b_qkv[P:2 * P]]
    out = {
        "x": x, "xT": x.T, "const": constants(),
        "condT": a["cond_512"].T, "affT": a["L0_cond_affine_w"].T, "WT": a["L0_cond_weight"].T,
        "vec": np.stack(vec, axis=1),
        "rows": np.concatenate([b_qkv[2 * P:], a["L1_ffn_b_o"], a["L1_ffn_gate_b"]])[None, :],
        "gb": np.concatenate([a["L1_cond_down_gamma"], a["L1_cond_down_beta"],
                              a["L1_cond_up_gamma"], a["L1_cond_up_beta"]], axis=1),
        "Wg": a["L0_ffn_Wg"], "W123": np.concatenate([a["L0_ffn_W1"], a["L0_ffn_W2"], W3], axis=2),
        "Ws1": a["L0_ffn_Ws1"], "Ws2": a["L0_ffn_Ws2"], "Ws3": a["L0_ffn_Ws3"],
        "dproj": a["L1_cond_down_project"], "uproj": a["L1_cond_up_project"],
        "wqkv": a["L1_ffn_w_qkv"], "wo": a["L1_ffn_w_o"], "gate": a["L1_ffn_gate_w"],
        "W1b": np.concatenate([a["L1_ffn_W1"], W2b, b1, b2], axis=2),
    }
    return {k: np.ascontiguousarray(v) for k, v in out.items()}


def kernel(**inputs):
    import concourse.bacc as bacc
    from concourse.bass_utils import run_bass_kernel_spmd

    nc = bacc.Bacc("TRN2", target_bir_lowering=False, num_devices=1)
    arrays = {f"in_{k}": v for k, v in laid_out({k: np.asarray(v) for k, v in inputs.items()}).items()}
    d = {k[3:]: nc.dram_tensor(k, v.shape, mybir.dt.from_np(v.dtype), kind="ExternalInput").ap()
         for k, v in arrays.items()}
    out = nc.dram_tensor("out", (SEQS, P, P), F32, kind="ExternalOutput").ap()
    build(nc, d, out)
    r = run_bass_kernel_spmd(nc, [arrays], core_ids=[0])
    return r.results[0]["out"]
```
